# Optimizing a Trainium2 kernel written in Bass

```python
import numpy as np
import jax
import jax.numpy as jnp

def _softmax(x, axis=-1):
    return jax.nn.softmax(x, axis=axis)

def _gelu(x):
    return jax.nn.gelu(x, approximate=True)

def _silu(x):
    return jax.nn.silu(x)

def _sigmoid(x):
    return jax.nn.sigmoid(x)

def _layernorm(x, axis=-1, eps=1e-05):
    m = jnp.mean(x, axis=axis, keepdims=True)
    v = jnp.var(x, axis=axis, keepdims=True)
    return (x - m) / jnp.sqrt(v + eps)

def _scatter_add(tgt, idx, src, axis=0):
    return tgt.at[idx].add(src)

def _segment_sum(src, seg, n):
    return jax.ops.segment_sum(src, seg, n)
kernel_name = 'mk_cond_resid_d4_seqx_r8_71c83c'

def setup_inputs(seed: int=0):
    np.random.seed(seed)
    _w = jnp.asarray

    def _rec_inputs():
        import jax
        import jax.numpy as jnp
        _rk = jax.random.key(seed)
        x = -7.109e-05 + 0.9999 * jax.random.normal(jax.random.fold_in(_rk, 1), (128, 32, 256), jnp.float32)
        _lenS = 32 - jax.random.randint(jax.random.fold_in(_rk, 7), (128,), 0, max(1, 32 // 4) + 1, jnp.int32)
        _lenS2 = 32 - jax.random.randint(jax.random.fold_in(_rk, 8), (128,), 0, max(1, 32 // 4) + 1, jnp.int32)
        itok_B_1_198 = jax.random.randint(jax.random.fold_in(_rk, 11), (128,), 1, 199, jnp.int32)
        itok_Bx257_0_4111 = jax.random.randint(jax.random.fold_in(_rk, 12), (128, 257), 0, 514, jnp.int32)
        itok_B_37_3939 = jax.random.randint(jax.random.fold_in(_rk, 13), (128,), 37, 3940, jnp.int32)
        itok_B_0_7 = jax.random.randint(jax.random.fold_in(_rk, 14), (128,), 0, 8, jnp.int32)
        itok_B_0_6 = jax.random.randint(jax.random.fold_in(_rk, 15), (128,), 0, 7, jnp.int32)
        return (x, itok_B_1_198, itok_Bx257_0_4111, itok_B_37_3939, itok_B_0_7, itok_B_0_6)
    x, itok_B_1_198, itok_Bx257_0_4111, itok_B_37_3939, itok_B_0_7, itok_B_0_6 = _rec_inputs()

    def _L0_cond_setup():
        import jax, jax.numpy as jnp
        import numpy as np
        B, C, T = (128, 32, 256)
        S, D = (200, 32)
        key = jax.random.key(seed)
        k1, k2, k3 = jax.random.split(key, 3)
        x = jax.random.normal(k1, (B, C, T), dtype=jnp.float32)
        conditions = jax.random.randint(k2, (B,), 0, S, dtype=jnp.int64)
        weights = jax.random.normal(k3, (S, C, D), dtype=jnp.float32) / jnp.sqrt(jnp.float32(C))
        return {'x': x, 'conditions': conditions, 'weights': weights}
    _L0_cond_all = _L0_cond_setup()
    _L0_cond_in = {k: v for k, v in _L0_cond_all.items() if k in ('weights',)}
    del _L0_cond_all

    def _L1_cond_setup():
        import jax, jax.numpy as jnp
        import numpy as np
        H, G, HD = (8, 4, 32)
        GSZ = H // G
        BLOCK = 16
        WINDOW = 128
        SCALE = 256.0 ** (-0.5)
        EPS = 1e-06
        THETA = 10000.0
        B, T, D = (16, 4, 256)
        NBLK = 257

        def _rms(x, scale):
            var = jnp.mean(x * x, axis=-1, keepdims=True)
            return x * jax.lax.rsqrt(var + EPS) * (1.0 + scale)

        def _rope(x, pos):
            half = HD // 2
            inv = 1.0 / THETA ** (jnp.arange(half, dtype=jnp.float32) / half)
            ang = pos[:, :, None].astype(jnp.float32) * inv
            cos = jnp.cos(ang)[:, None, :, :]
            sin = jnp.sin(ang)[:, None, :, :]
            x1, x2 = (x[..., :half], x[..., half:])
            return jnp.concatenate([x1 * cos - x2 * sin, x2 * cos + x1 * sin], axis=-1)
        key = jax.random.key(seed)
        ks = jax.random.split(key, 10)
        inv_d = 1.0 / np.sqrt(D)
        return {'x': jax.random.normal(ks[0], (B, T, D), jnp.float32), 'Wq': jax.random.normal(ks[1], (H * HD, D), jnp.float32) * inv_d, 'Wk': jax.random.normal(ks[2], (G * HD, D), jnp.float32) * inv_d, 'Wv': jax.random.normal(ks[3], (G * HD, D), jnp.float32) * inv_d, 'Wo': jax.random.normal(ks[4], (D, H * HD), jnp.float32) * inv_d, 'q_norm_scale': jax.random.normal(ks[5], (HD,), jnp.float32) * 0.02, 'k_norm_scale': jax.random.normal(ks[6], (HD,), jnp.float32) * 0.02, 'k_blocks': jax.random.normal(ks[7], (B * NBLK, G, BLOCK, HD), jnp.float32), 'v_blocks': jax.random.normal(ks[8], (B * NBLK, G, BLOCK, HD), jnp.float32), 'block_tables': jnp.arange(B * NBLK, dtype=jnp.int32).reshape(B, NBLK), 'kv_lens': jax.random.randint(ks[9], (B,), 0, 512, dtype=jnp.int32)}
    _L1_cond_all = _L1_cond_setup()
    _L1_cond_in = {k: v for k, v in _L1_cond_all.items() if k in ('Wq', 'Wk', 'Wv', 'Wo', 'q_norm_scale', 'k_norm_scale', 'k_blocks', 'v_blocks')}
    del _L1_cond_all

    def _L2_cond_setup():
        import jax, jax.numpy as jnp
        import numpy as np
        B, C, D, T, N_SUBJECTS = (128, 32, 32, 256, 8)
        key = jax.random.key(seed)
        kx, ks, kw = jax.random.split(key, 3)
        x = jax.random.normal(kx, (B, C, T), dtype=jnp.float32)
        subjects = jax.random.randint(ks, (B,), 0, N_SUBJECTS, dtype=jnp.int64)
        weights = jax.random.normal(kw, (N_SUBJECTS, C, D), dtype=jnp.float32) * (1.0 / C ** 0.5)
        return {'x': x, 'subjects': subjects, 'weights': weights}
    _L2_cond_all = _L2_cond_setup()
    _L2_cond_in = {k: v for k, v in _L2_cond_all.items() if k in ('weights',)}
    del _L2_cond_all

    def _L3_cond_setup():
        import jax, jax.numpy as jnp
        import numpy as np
        B, T, D_IN, D_OUT = (16, 256, 256, 256)
        N_ADAPTERS, RANK = (8, 16)
        key = jax.random.key(seed)
        k_x, k_w, k_a, k_b, k_s, k_idx = jax.random.split(key, 6)
        x = jax.random.normal(k_x, (B, T, D_IN), dtype=jnp.float32)
        W = jax.random.normal(k_w, (D_OUT, D_IN), dtype=jnp.float32) * (1.0 / np.sqrt(D_IN))
        A = jax.random.normal(k_a, (N_ADAPTERS, RANK, D_IN), dtype=jnp.float32) * 0.02
        Bm = jax.random.normal(k_b, (N_ADAPTERS, D_OUT, RANK), dtype=jnp.float32) * 0.02
        scalings = jnp.ones((N_ADAPTERS,), dtype=jnp.float32)
        adapter_idx = jax.random.randint(k_idx, (B,), 0, N_ADAPTERS, dtype=jnp.int32)
        return {'x': x, 'W': W, 'A': A, 'Bm': Bm, 'scalings': scalings, 'adapter_idx': adapter_idx}
    _L3_cond_all = _L3_cond_setup()
    _L3_cond_in = {k: v for k, v in _L3_cond_all.items() if k in ('W', 'A', 'Bm', 'scalings')}
    del _L3_cond_all
    return {'x': x, 'itok_B_1_198': itok_B_1_198, 'itok_Bx257_0_4111': itok_Bx257_0_4111, 'itok_B_37_3939': itok_B_37_3939, 'itok_B_0_7': itok_B_0_7, 'itok_B_0_6': itok_B_0_6, 'L0_cond_weights': _L0_cond_in['weights'], 'L1_cond_Wq': _L1_cond_in['Wq'], 'L1_cond_Wk': _L1_cond_in['Wk'], 'L1_cond_Wv': _L1_cond_in['Wv'], 'L1_cond_Wo': _L1_cond_in['Wo'], 'L1_cond_q_norm_scale': _L1_cond_in['q_norm_scale'], 'L1_cond_k_norm_scale': _L1_cond_in['k_norm_scale'], 'L1_cond_k_blocks': _L1_cond_in['k_blocks'], 'L1_cond_v_blocks': _L1_cond_in['v_blocks'], 'L2_cond_weights': _L2_cond_in['weights'], 'L3_cond_W': _L3_cond_in['W'], 'L3_cond_A': _L3_cond_in['A'], 'L3_cond_Bm': _L3_cond_in['Bm'], 'L3_cond_scalings': _L3_cond_in['scalings']}

def reference(x, itok_B_1_198, itok_Bx257_0_4111, itok_B_37_3939, itok_B_0_7, itok_B_0_6, L0_cond_weights, L1_cond_Wq, L1_cond_Wk, L1_cond_Wv, L1_cond_Wo, L1_cond_q_norm_scale, L1_cond_k_norm_scale, L1_cond_k_blocks, L1_cond_v_blocks, L2_cond_weights, L3_cond_W, L3_cond_A, L3_cond_Bm, L3_cond_scalings):
    import jax
    import jax.numpy as jnp

    def _L0_cond_ref(x, conditions, weights):
        import jax, jax.numpy as jnp
        import numpy as np
        B, C, T = (128, 32, 256)
        S, D = (200, 32)
        w = weights[conditions]
        return jnp.einsum('bct,bcd->bdt', x, w)

    def _L1_cond_ref(x, Wq, Wk, Wv, Wo, q_norm_scale, k_norm_scale, k_blocks, v_blocks, block_tables, kv_lens):
        import jax, jax.numpy as jnp
        import numpy as np
        H, G, HD = (8, 4, 32)
        GSZ = H // G
        BLOCK = 16
        WINDOW = 128
        SCALE = 256.0 ** (-0.5)
        EPS = 1e-06
        THETA = 10000.0
        B, T, D = (16, 4, 256)
        NBLK = 257

        def _rms(x, scale):
            var = jnp.mean(x * x, axis=-1, keepdims=True)
            return x * jax.lax.rsqrt(var + EPS) * (1.0 + scale)

        def _rope(x, pos):
            half = HD // 2
            inv = 1.0 / THETA ** (jnp.arange(half, dtype=jnp.float32) / half)
            ang = pos[:, :, None].astype(jnp.float32) * inv
            cos = jnp.cos(ang)[:, None, :, :]
            sin = jnp.sin(ang)[:, None, :, :]
            x1, x2 = (x[..., :half], x[..., half:])
            return jnp.concatenate([x1 * cos - x2 * sin, x2 * cos + x1 * sin], axis=-1)
        Bx, Tx, _ = x.shape
        q = jnp.einsum('btd,od->bto', x, Wq).reshape(Bx, Tx, H, HD).transpose(0, 2, 1, 3)
        k = jnp.einsum('btd,od->bto', x, Wk).reshape(Bx, Tx, G, HD).transpose(0, 2, 1, 3)
        v = jnp.einsum('btd,od->bto', x, Wv).reshape(Bx, Tx, G, HD).transpose(0, 2, 1, 3)
        q = _rms(q, q_norm_scale)
        k = _rms(k, k_norm_scale)
        pos = kv_lens[:, None] + jnp.arange(Tx, dtype=jnp.int32)
        q = _rope(q, pos)
        k = _rope(k, pos)
        slot = pos // BLOCK
        off = pos % BLOCK
        blk = jnp.take_along_axis(block_tables, slot, axis=1)
        k_blocks = k_blocks.at[blk, :, off, :].set(k.transpose(0, 2, 1, 3))
        v_blocks = v_blocks.at[blk, :, off, :].set(v.transpose(0, 2, 1, 3))
        k_all = k_blocks[block_tables].transpose(0, 2, 1, 3, 4).reshape(Bx, G, -1, HD)
        v_all = v_blocks[block_tables].transpose(0, 2, 1, 3, 4).reshape(Bx, G, -1, HD)
        S = k_all.shape[2]
        qg = q.reshape(Bx, G, GSZ, Tx, HD)
        scores = jnp.einsum('bghtd,bgsd->bghts', qg, k_all) * SCALE
        kpos = jnp.arange(S, dtype=jnp.int32)
        allowed = (kpos[None, None, :] <= pos[:, :, None]) & (kpos[None, None, :] > pos[:, :, None] - WINDOW)
        scores = jnp.where(allowed[:, None, None, :, :], scores, -jnp.inf)
        p = jax.nn.softmax(scores, axis=-1)
        o = jnp.einsum('bghts,bgsd->bghtd', p, v_all).reshape(Bx, H, Tx, HD)
        o = o.transpose(0, 2, 1, 3).reshape(Bx, Tx, H * HD)
        return jnp.einsum('bto,do->btd', o, Wo)

    def _L2_cond_ref(x, subjects, weights):
        import jax, jax.numpy as jnp
        import numpy as np
        B, C, D, T, N_SUBJECTS = (128, 32, 32, 256, 8)
        w = weights[subjects]
        out = jnp.einsum('bct,bcd->bdt', x, w)
        return out

    def _L3_cond_ref(x, W, A, Bm, scalings, adapter_idx):
        import jax, jax.numpy as jnp
        import numpy as np
        B, T, D_IN, D_OUT = (16, 256, 256, 256)
        N_ADAPTERS, RANK = (8, 16)
        H = jnp.einsum('btd,od->bto', x, W)
        A_b = A[adapter_idx]
        B_b = Bm[adapter_idx]
        s_b = scalings[adapter_idx]
        xa = jnp.einsum('btd,brd->btr', x, A_b)
        delta = jnp.einsum('btr,bor->bto', xa, B_b)
        delta = jax.lax.stop_gradient(delta * s_b[:, None, None])
        return H + delta
    x = x + _L0_cond_ref(x, itok_B_1_198, L0_cond_weights)
    x = x + _L1_cond_ref(x, L1_cond_Wq, L1_cond_Wk, L1_cond_Wv, L1_cond_Wo, L1_cond_q_norm_scale, L1_cond_k_norm_scale, L1_cond_k_blocks, L1_cond_v_blocks, itok_Bx257_0_4111, itok_B_37_3939)
    x = x + _L2_cond_ref(x, itok_B_0_7, L2_cond_weights)
    x = x + _L3_cond_ref(x, L3_cond_W, L3_cond_A, L3_cond_Bm, L3_cond_scalings, itok_B_0_6)
    return x

_drawn_inputs = setup_inputs


def setup_inputs(seed=0):
    import zlib

    import numpy as np

    out = dict(_drawn_inputs(seed))
    spreads = {'L3_cond_scalings': (1.0, 0.6)}
    factors = {'L1_cond_q_norm_scale': 8.0,
     'L1_cond_k_norm_scale': 64.0,
     'L1_cond_k_blocks': 3.441,
     'L3_cond_A': 2.986,
     'L3_cond_Bm': 2.944,
     'L1_cond_Wk': 3.034}
    for name, (base, spread) in spreads.items():
        noise = np.random.default_rng([zlib.crc32(name.encode()), seed]).standard_normal(out[name].shape)
        drawn = base * np.exp(spread * noise) if base else spread * noise
        out[name] = jnp.asarray(drawn.astype(out[name].dtype))
    for name, factor in factors.items():
        out[name] = (out[name] * factor).astype(out[name].dtype)
    return out
```

```python
import math
from contextlib import ExitStack

import concourse.bass as bass
from concourse import mybir


def cond_resid_kernel(
    nc, x, cond, table, kvlen, subj, adapt, w0, wq, wk, wv, wo, qscale, kscale, k_blocks, v_blocks, w2, w3, a3, b3, s3, out
):
    f32, bf16, i32 = mybir.dt.float32, mybir.dt.bfloat16, mybir.dt.int32
    ALU = mybir.AluOpType
    ACT = mybir.ActivationFunctionType
    AX = mybir.AxisListType

    B, C, T = x.shape
    NBLK = table.shape[1]
    POOL_BLOCKS, G, BLOCK, HD = k_blocks.shape
    H = wq.shape[0] // HD
    HPG = H // G
    KVD = G * HD
    WINDOW = 128
    W = 11
    WP = 12
    KEYS = W * BLOCK
    GB = 8
    ROWS = GB * W
    NG = B // GB
    TB = 128 // C
    NT = B // TB
    NS = (C + BLOCK - 2) // BLOCK + 1
    NW = NS * B
    HB = BLOCK // 2
    HK = HB * W
    NA, RANK = a3.shape[0], a3.shape[1]
    SCALE = 256.0 ** -0.5
    EPS = 1e-6
    SKIP = 16384.0
    DROP = 1048576.0
    NEG = -1e30
    HALF = HD // 2

    x_t = x.rearrange("(n b) c t -> n (b c) t", b=TB)
    out_t = out.rearrange("(n b) c t -> n (b c) t", b=TB)
    k_old = k_blocks.rearrange("n g o d -> n (g o d)")
    v_old = v_blocks.rearrange("n g o d -> n (g o d)")

    x1_d = nc.dram_tensor("x1_spill", [NT, 128, T], f32, kind="Internal").ap()
    w0_d = nc.dram_tensor("w0_picked", [B, C * C], f32, kind="Internal").ap()
    w2_d = nc.dram_tensor("w2_picked", [B, C * C], f32, kind="Internal").ap()
    new_d = nc.dram_tensor("written_blocks", [NW * BLOCK, 2 * KVD], f32, kind="Internal").ap()
    new_blocks = new_d.rearrange("(n o) c -> n (o c)", o=BLOCK)
    new_rows = new_d.rearrange("(s b o) c -> s b (o c)", b=B, o=BLOCK)

    ctx = ExitStack()
    with ctx:
        def sb(name, shape, dt=f32):
            return ctx.enter_context(nc.sbuf_tensor(name, shape, dt))

        def sem(name):
            return ctx.enter_context(nc.semaphore(name))

        room = sb("turned_blocks", [128, 4 * BLOCK * ROWS])
        turned = room[:, :].rearrange("p (i f o w) -> p i f o w", i=4, o=BLOCK, w=W)
        kT, vT = [turned[:, i] for i in (0, 1)], [turned[:, i] for i in (2, 3)]
        proom = sb("p_room", [128, 4 * HPG * KEYS])
        probs = proom[:, :].rearrange("p (i h k) -> p i h k", i=4, h=HPG)
        pex, pn = [probs[:, i] for i in (0, 1)], [probs[:, i] for i in (2, 3)]
        troom = sb("pT_room", [128, 2 * 2 * HPG * 128])
        pT = [troom[0:HK, 512 * i:512 * i + 512].rearrange("p (c h t) -> p c h t", c=2, h=HPG) for i in range(2)]
        vroom = sb("v_room", [128, 4 * 2 * KVD])
        vs = [vroom[0:HK, 256 * i:256 * i + 256].rearrange("p (c d) -> p c d", c=2) for i in range(4)]
        wnat = room[:, 0:20 * 128].rearrange("p (i d) -> p i d", i=20)
        same = room[:, 20 * 128:20 * 128 + NS * NW].rearrange("p (s w) -> p s w", s=NS)
        later_at = 20 * 128 + NS * NW
        later_or_same = room[:, later_at:later_at + (2 * NS - 1) * 128].rearrange("p (s b) -> p s b", b=128)
        pick_at = later_at + (2 * NS - 1) * 128
        wpick = [room[:, pick_at:pick_at + C * C], proom[:, 0:C * C]]
        kv = room[:, 0:8 * 2 * KVD].rearrange("p (u c) -> p u c", u=8)
        x1s = [vroom[:, T * u:T * u + T] for u in range(4)]

        eroom = sb("end_room", [128, 5 * NT * HALF])
        ang = eroom[:, 0:NT * HALF].rearrange("p (n i) -> p n i", i=HALF)
        turns = eroom[:, NT * HALF:3 * NT * HALF].rearrange("p (j n i) -> p j n i", j=2, i=HALF)
        trig = eroom[:, 3 * NT * HALF:5 * NT * HALF].rearrange("p (j n i) -> p j n i", j=2, i=HALF)
        x2s, x4s = [[eroom[:, T * i:T * i + T] for i in (j, j + 1)] for j in (0, 2)]
        x3T = [eroom[:, T * i:T * i + T].rearrange("p (c t) -> p c t", c=2) for i in (4, 5)]
        oT = [eroom[:, T * i:T * i + T].rearrange("p (h f t) -> p h f t", h=HPG, f=TB) for i in (6, 7)]
        xam = [eroom[:, T * 8 + 128 * i:T * 8 + 128 * i + 128] for i in range(2)]

        zcol = sb("zcol", [128, 1])
        ident = sb("ident", [128, 128])
        ones = sb("ones", [128, 128])
        iota_i = sb("iota_i", [128, NW], i32)
        iota = sb("iota", [128, NW])
        key_i = sb("key_i", [128, BLOCK, W], i32)
        keypos = sb("keypos", [128, KEYS])
        part_i = sb("part_i", [128, 1], i32)
        part = sb("part", [128, 6])
        part_m = sb("part_m", [128, 6], i32)
        in_tile = sb("in_tile", [128, TB])
        of_tile = sb("of_tile", [128, NT])
        in_group = sb("in_group", [128, GB])
        of_group = sb("of_group", [128, NG])
        mask_sel = sb("mask_sel", [128, TB, 128], bf16)
        halfpow = sb("halfpow", [128, H])
        inv = sb("inv", [128, HALF])

        kvlen_i = sb("kvlen_i", [128, 1], i32)
        cond_i = sb("cond_i", [128, 1], i32)
        subj_i = sb("subj_i", [128, 1], i32)
        adapt_i = sb("adapt_i", [128, 1], i32)
        table_i = sb("table_i", [128, NBLK], i32)
        tab = sb("tab", [128, NBLK])
        ci = sb("ci", [128, 8], i32)
        cf = sb("cf", [128, 8])
        slots = sb("slots", [128, NS + WP])
        blk = sb("blk", [128, NS + WP])
        pick = sb("pick", [128, NBLK])
        diag = sb("diag", [128, NS, 128])
        wrow = sb("wrow", [128, NW])
        valid = sb("valid", [128, NS, BLOCK + 1])
        vlow = sb("vlow", [128, NS, BLOCK])
        vtmp = sb("vtmp", [128, NS, BLOCK])
        dest = sb("dest", [128, NS * BLOCK])
        dest2 = sb("dest2", [128, NS * BLOCK])
        number = sb("number", [128, NS])
        owner = sb("owner", [128, NS])
        own = sb("own", [128, NS])
        crow = sb("crow", [128, NW])
        rowid = sb("rowid", [128, NS * BLOCK])
        shift = sb("shift", [128, BLOCK])
        tok = sb("tok", [128, 4, C])
        base_idx = sb("base_idx", [128, 2], i32)
        hits = sb("hits", [128, WP])
        hjunk = sb("hjunk", [128, NW])
        rd = sb("rd", [128, 2, W])
        rtmp = sb("rtmp", [128, 2, W])
        g_idx = sb("g_idx", [128, 4], i32)
        spread = sb("spread", [128, 3, 128])
        gspread = sb("gspread", [128, 2, GB, W])
        tok_idx = sb("tok_idx", [128, NT], i32)
        tok_pos = sb("tok_pos", [128, NT])
        tok_hi = sb("tok_hi", [128, NT])
        tok_lo = sb("tok_lo", [128, NT])
        rd_idx = sb("rd_idx", [128, 2, NG], i32)
        adiag = sb("adiag", [128, 128])
        amask = sb("amask", [128, B])
        scal_col = sb("scal_col", [128, 1])

        gain = sb("gain", [128, 2, HD])
        ngain = sb("ngain", [128, 2, HD])
        ctab = sb("ctab", [128, 2, NT, HD])
        stab = sb("stab", [128, 2, NT, HD])

        wkvT = sb("wkvT", [128, 2, 2 * KVD])
        wqT = sb("wqT", [128, 2, T])
        woT = sb("woT", [128, HPG, T])
        w3T = sb("w3T", [128, 2, T])
        abT = sb("abT", [128, 2, T])
        bd = sb("bd", [128, NT, 128])

        old = [sb(f"old{i}", [128, 2, G * BLOCK * HD]) for i in range(2)]
        new = [sb(f"new{i}", [128, BLOCK, 2, KVD]) for i in range(2)]

        xin = [sb(f"xin{i}", [128, T]) for i in range(4)]
        xT = [sb(f"xT{i}", [128, 2, 128]) for i in range(2)]
        kv_idx = sb("kv_idx", [128, 8], i32)
        rp = sb("rp", [128, 4, T])
        rms = sb("rms", [128, 3, H])
        qs = [sb(f"qs{i}", [128, T]) for i in range(2)]
        qr = [sb(f"qr{i}", [128, T]) for i in range(2)]
        qbd = [sb(f"qbd{i}", [128, GB, HPG, 128]) for i in range(2)]
        pen_hi = sb("pen_hi", [128, KEYS])
        pen = [sb(f"pen{i}", [128, KEYS], bf16) for i in range(2)]
        nmax = sb("nmax", [128, 4, HPG])
        rsum = sb("rsum", [128, 4, HPG])
        rrec = sb("rrec", [128, 4, HPG])

        ps = [ctx.enter_context(nc.psum_tensor(f"bank{i}", [128, 512], f32)) for i in range(8)]
        ps_s, ps_p, ps_v, ps_o, ps_m = ps[0:2], ps[2:4], ps[4], ps[5], ps[6:8]

        s_len, s_tab, s_cond, s_subj, s_adapt = (sem(n) for n in ("len_in", "table_in", "cond_in", "subj_in", "adapt_in"))
        s_gain, s_scal = sem("gain_in"), sem("scal_in")
        s_wk, s_wq, s_wo, s_w3, s_ab = (sem(n) for n in ("wkv_in", "wq_in", "wo_in", "w3_in", "ab_in"))
        s_pick = [sem("w0_picked_in"), sem("w2_picked_in")]
        s_pickw = [sem("w0_picked_out"), sem("w2_picked_out")]
        s_bd = [sem("bd0_in"), sem("bd2_in")]
        s_xin = [sem(f"x_in{i}") for i in range(4)]
        s_spill = [sem(f"x1_out{i}") for i in range(4)]
        s_x1 = [sem(f"x1_in{i}") for i in range(4)]
        s_bg = [sem(f"base_in{i}") for i in range(2)]
        s_bs = [sem(f"base_out{i}") for i in range(2)]
        s_scat = [sem(f"tokens_out{i}") for i in range(8)]
        s_gold = [sem(f"old_in{i}") for i in range(2)]
        s_gnew = [sem(f"new_in{i}") for i in range(2)]
        s_out = [sem(f"out_done{i}") for i in range(2)]
        s_cchain = sem("constant_made")
        s_dset = sem("setup_op")
        s_wrow, s_later, s_relay, s_reads = (sem(n) for n in ("wrow_ps", "later_ps", "relay_ps", "reads_ps"))
        s_wt, s_wtc, s_trig, s_perm, s_w3i = (sem(n) for n in ("weights_turned", "weights_copied", "trig_ready", "base_permuted", "w3_plus_i"))
        s_zero, s_zfill, s_crow = sem("old_zeroed"), sem("second_blocks_zeroed"), sem("crow_ps")
        s_order = [sem(f"old_reordered{i}") for i in range(2)]
        s_gix = [sem("old_index_staged"), sem("new_index_staged")]
        s_look, s_passed = sem("slot_looked_up"), sem("pool_passed")
        s_l0, s_xtc, s_tr1, s_kvp, s_kvc, s_x1c = (
            sem(n) for n in ("l0_done", "x1T_copied", "x1_turned", "kv_projected", "kv_copied", "x1_copied"))
        s_kr, s_ms, s_rstd, s_rope = (sem(n) for n in ("k_roped", "ms_ready", "rstd_ready", "rope_op"))
        s_tix = sem("token_index_staged")
        s_qk, s_max, s_exp, s_rec, s_pn, s_pt, s_ptc, s_vt, s_vc, s_pv = (
            sem(n) for n in ("qk_done", "max_done", "exp_done", "rec_done", "p_normal", "p_turned", "pT_copied",
                             "v_turned", "v_copied", "pv_done"))
        s_oc, s_pen1, s_pen, s_qrd = (sem(n) for n in ("oT_copied", "pen_half", "pen_ready", "q_roped"))
        s_full = [sem("misc_full0"), sem("misc_full1")]
        s_empty = [sem("misc_empty0"), sem("misc_empty1")]

        block = ctx.enter_context(nc.Block())
        mark = {}
        cmark_iota, cmark_bd, cmark_masks = 5, 7, 10
        cmark_all = cmark_masks + 4 + HALF
        cmark_qbd = cmark_all + 2

        PREP = {0: [("x1", 0), ("k0", None)], 1: [("q", 0), ("k1", None)], 2: [("k2", None)],
                3: [("qT", 0), ("k3", None)], 4: [("x1", 1), ("v0", None)], 5: [("q", 1), ("v1", None)],
                6: [("v2", None), ("v3", None)], 7: [("qT", 1)]}
        FIRST_PREP = {0: [("x1", 0)], 1: [("q", 0)], 2: [("x1", 1)], 3: [("q", 1), ("qT", 0)], 4: [("qT", 1), ("k0", None)],
                      5: [("k1", None), ("k2", None)], 6: [("k3", None), ("v0", None)],
                      7: [("v1", None), ("v2", None), ("v3", None)]}
        FIN = {2: ("x2", 6), 3: ("x3", 7), 0: ("xa", 8), 1: ("x4", 9)}
        LAST = 4 * (NT - 1) + 9

        def fin_step(k):
            kind, lag = FIN[k % 4]
            n = (k - lag) // 4
            return [(kind, n)] if 0 <= n < NT else []

        def prep_steps(k):
            grp = k // 8 + 1
            if not 0 <= grp < NG:
                return []
            steps = PREP[k % 8] if grp else FIRST_PREP[k % 8]
            return [(kind, grp if u is None else 2 * grp + u) for kind, u in steps]

        place = {}
        served = [0, 0]
        for k in range(-8, LAST + 1):
            turn = k % 8 + sum(len(PREP[j]) for j in range(k % 8)) if k >= 0 else sum(served)
            for i, found in enumerate([fin_step(k)] + [[s] for s in prep_steps(k)]):
                for step in found:
                    place[step] = ((turn + i) % 2, served[(turn + i) % 2])
                    served[(turn + i) % 2] += 1
        PER_LOOP = 22
        LOOPS = B // 16 - 2

        def misc(step, it):
            bank, before = place[step]
            return bank, before + PER_LOOP * it

        def await_bank(eng, step, it):
            bank, before = misc(step, it)
            if not isinstance(before, int) or before > 0:
                eng.wait_ge(s_empty[bank], before)

        def await_step(eng, step, it):
            bank, before = misc(step, it)
            eng.wait_ge(s_full[bank], before + 1)

        def await_copied(eng, step, it):
            bank, before = misc(step, it)
            eng.wait_ge(s_empty[bank], before + 1)

        def reordered_piece(i, which, piece):
            at = slice(4 * piece, 4 * piece + 4)
            return (new[i][0:ROWS, at, which, :].rearrange("p o (g d) -> p g o d", g=G),
                    old[i][0:ROWS, which, :].rearrange("p (g o d) -> p g o d", g=G, o=BLOCK)[:, :, at, :])

        def run_slots(eng, slot):
            for k in range(-8, 8):
                slot(0, k)
            with eng.Fori(0, LOOPS) as it:
                for k in range(8, 24):
                    slot(it, k)
            for k in range(8 + 16 * LOOPS, LAST + 1):
                slot(0, k)

        @block.vector
        def _(dve):
            v = nc.vector
            done = [0]

            def put(ins):
                done[0] += 1
                ins.then_inc(s_dset, 1)

            def settled():
                dve.wait_ge(s_dset, done[0])

            dve.wait_ge(s_len, 16)
            dve.wait_ge(s_cchain, cmark_iota)
            put(v.tensor_copy(iota[:, :], iota_i[:, :]))
            put(v.tensor_scalar(ci[:, 0:1], kvlen_i[:, :], 4, None, ALU.arith_shift_right))
            put(v.tensor_scalar(ci[:, 1:2], kvlen_i[:, :], BLOCK - 1, None, ALU.bitwise_and))
            put(v.tensor_scalar(ci[:, 2:3], kvlen_i[:, :], float(1 - WINDOW), 0.0, ALU.add, ALU.max))
            put(v.tensor_copy(cf[:, 4:5], kvlen_i[:, :]))
            put(v.tensor_scalar(part_m[:, 1:2], part_i[:, :], TB - 1, None, ALU.bitwise_and))
            put(v.tensor_scalar(part_m[:, 2:3], part_i[:, :], 2, None, ALU.arith_shift_right))
            put(v.tensor_scalar(part_m[:, 3:4], part_i[:, :], GB - 1, None, ALU.bitwise_and))
            put(v.tensor_scalar(part_m[:, 4:5], part_i[:, :], 3, None, ALU.arith_shift_right))
            put(v.tensor_scalar(part_m[:, 5:6], part_i[:, :], 4, None, ALU.arith_shift_right))
            settled()
            put(v.tensor_scalar(ci[:, 3:4], ci[:, 2:3], 4, None, ALU.arith_shift_right))
            put(v.tensor_copy(cf[:, 0:2], ci[:, 0:2]))
            put(v.tensor_copy(part[:, 0:1], part_i[:, :]))
            put(v.tensor_copy(part[:, 1:6], part_m[:, 1:6]))
            settled()
            put(v.tensor_scalar(cf[:, 3:4], ci[:, 3:4], float(NBLK - W), None, ALU.min))
            put(v.tensor_scalar(in_tile[:, :], iota[:, 0:TB], part[:, 1:2], None, ALU.is_equal))
            put(v.tensor_scalar(of_tile[:, :], iota[:, 0:NT], part[:, 2:3], None, ALU.is_equal))
            put(v.tensor_scalar(in_group[:, :], iota[:, 0:GB], part[:, 3:4], None, ALU.is_equal))
            put(v.tensor_scalar(of_group[:, :], iota[:, 0:NG], part[:, 4:5], None, ALU.is_equal))
            settled()
            put(v.scalar_tensor_tensor(cf[:, 5:6], cf[:, 3:4], -float(BLOCK), cf[:, 4:5], ALU.mult, ALU.add))
            put(v.tensor_scalar(slots[:, 0:NS], iota[:, 0:NS], cf[:, 0:1], None, ALU.add))
            put(v.tensor_scalar(slots[:, NS:], iota[:, 0:WP], cf[:, 3:4], None, ALU.add))
            dve.wait_ge(s_tab, 16)
            put(v.tensor_copy(tab[:, :], table_i[:, :]))
            settled()
            for j in range(NS):
                put(v.scalar_tensor_tensor(pick[:, :], iota[:, 0:NBLK], slots[:, j:j + 1], tab[:, :], ALU.is_equal, ALU.mult,
                                           accum_out=blk[:, j:j + 1]))
                settled()
            put(v.tensor_scalar(cf[:, 6:7], cf[:, 1:2], 0.0, None, ALU.is_gt))
            settled()
            put(v.scalar_tensor_tensor(cf[:, 7:8], blk[:, NS - 1:NS], 1.0, cf[:, 6:7], ALU.add, ALU.mult))
            settled()
            put(v.tensor_scalar(blk[:, NS - 1:NS], cf[:, 7:8], -1.0, None, ALU.add))
            settled()
            for s in range(NS):
                put(v.tensor_scalar(diag[:, s, :], ident[:, :], blk[:, s:s + 1], None, ALU.mult))
            mark["diag"] = done[0]
            for i, s in enumerate((0, NS - 1)):
                put(v.tensor_scalar(base_idx[:, i:i + 1], blk[:, s:s + 1], 0.0, None, ALU.max))
            mark["base"] = done[0]
            for s in range(NS):
                put(v.tensor_scalar(vtmp[:, s, :], iota[:, BLOCK * s:BLOCK * s + BLOCK], cf[:, 1:2], None, ALU.subtract))
                put(v.tensor_scalar(number[:, s:s + 1], part[:, 0:1], float(B * s + 1), None, ALU.add))
            settled()
            for s in range(NS):
                put(v.tensor_scalar(valid[:, s, 0:BLOCK], vtmp[:, s, :], 0.0, None, ALU.is_ge))
                put(v.tensor_scalar(valid[:, s, BLOCK:BLOCK + 1], blk[:, s:s + 1], 0.0, None, ALU.is_ge))
            put(v.tensor_scalar(vlow[:, :, :], vtmp[:, :, :], float(C), None, ALU.is_lt))
            put(v.tensor_scalar(shift[:, :], iota[:, 0:BLOCK], cf[:, 1:2], None, ALU.is_equal))
            settled()
            for s in range(NS):
                put(v.tensor_tensor(valid[:, s, 0:BLOCK], valid[:, s, 0:BLOCK], vlow[:, s, :], ALU.mult))
            dve.wait_ge(s_wrow, 1)
            put(v.tensor_copy(wrow[:, :], ps[6][:, 0:NW]))
            dve.wait_ge(s_cchain, cmark_masks)
            settled()
            for s in range(NS):
                masks = later_or_same[:, NS - 1 - s:2 * NS - 1 - s, :].rearrange("p s b -> p (s b)")
                put(v.scalar_tensor_tensor(same[:, s, :], wrow[:, :], blk[:, s:s + 1], masks, ALU.is_equal, ALU.mult))
            mark["same"] = done[0]
            for i in range(2):
                dve.wait_ge(s_pick[i], 16)
                put(v.tensor_scalar(wpick[i][:, ::C + 1], wpick[i][:, ::C + 1], 1.0, None, ALU.add))
                mark[f"w{i}"] = done[0]
            put(v.tensor_scalar(tok[:, 2, :], iota[:, 0:C], cf[:, 4:5], None, ALU.add))
            put(v.tensor_scalar(tok[:, 3, :], iota[:, 0:C], cf[:, 5:6], None, ALU.add))
            dve.wait_ge(s_later, 1)
            later = ps[7][:, 0:NS * (BLOCK + 1)].rearrange("p (s c) -> p s c", s=NS)
            for s in range(NS):
                put(v.tensor_scalar(owner[:, s:s + 1], later[:, s, BLOCK:BLOCK + 1], 0.0, number[:, s:s + 1], ALU.is_equal, ALU.mult))
            settled()
            for s in range(NS):
                put(v.tensor_scalar(owner[:, s:s + 1], owner[:, s:s + 1], valid[:, s, BLOCK:BLOCK + 1], None, ALU.mult))
            settled()
            for s in range(NS):
                put(v.tensor_scalar(diag[:, s, :], ident[:, :], owner[:, s:s + 1], None, ALU.mult))
            mark["owner"] = done[0]
            for s in range(NS):
                put(v.tensor_scalar(dest[:, BLOCK * s:BLOCK * s + BLOCK], later[:, s, 0:BLOCK], 0.0, DROP, ALU.is_gt, ALU.mult))
            dve.wait_ge(s_crow, 1)
            put(v.tensor_copy(crow[:, :], ps[6][:, 0:NW]))
            settled()
            for s in range(NS):
                put(v.scalar_tensor_tensor(hjunk[:, :], wrow[:, :], blk[:, s:s + 1], crow[:, :], ALU.is_equal, ALU.mult,
                                           accum_out=own[:, s:s + 1]))
                settled()
            put(v.tensor_scalar(own[:, :], own[:, :], -1.0, float(BLOCK), ALU.add, ALU.mult))
            settled()
            for s in range(NS):
                put(v.tensor_scalar(rowid[:, BLOCK * s:BLOCK * s + BLOCK], iota[:, 0:BLOCK], own[:, s:s + 1], None, ALU.add))
            settled()
            put(v.tensor_tensor(dest2[:, :], dest[:, :], rowid[:, :], ALU.add))
            settled()
            put(v.tensor_scalar(tok[:, 0, :], dest2[:, 0:C], shift[:, 0:1], None, ALU.mult))
            for j in range(1, BLOCK):
                settled()
                put(v.scalar_tensor_tensor(tok[:, j % 2, :], dest2[:, j:j + C], shift[:, j:j + 1], tok[:, 1 - j % 2, :], ALU.mult, ALU.add))
            settled()
            for i, src in enumerate(((BLOCK - 1) % 2, 2, 3)):
                for f in range(TB):
                    put(v.tensor_scalar(spread[:, i, C * f:C * f + C], tok[:, src, :], in_tile[:, f:f + 1], None, ALU.mult))
            mark["spread"] = done[0]
            dve.wait_ge(s_relay, 1)
            put(v.tensor_copy(tok_idx[:, :], ps[6][:, 0:NT]))
            mark["tokens"] = done[0]
            put(v.tensor_copy(tok_pos[:, :], ps[6][:, NT:2 * NT]))
            put(v.tensor_copy(tok_hi[:, :], ps[6][:, 2 * NT:3 * NT]))
            put(v.tensor_scalar(tok_lo[:, :], ps[6][:, 2 * NT:3 * NT], -float(WINDOW), None, ALU.add))
            mark["relayed"] = done[0]
            BIG = 12582912.0
            TWO_PI = 2.0 * math.pi
            C1 = 6.28125
            C2 = math.floor((TWO_PI - C1) * 2 ** 21) / 2 ** 21
            C3 = TWO_PI - C1 - C2
            PI = 3.1415925
            flat = "p n i -> p (n i)"
            dve.wait_ge(s_cchain, cmark_all)
            settled()
            for i in range(HALF):
                put(v.tensor_scalar(ang[:, :, i], tok_pos[:, :], inv[:, i:i + 1], None, ALU.mult))
            settled()
            put(v.tensor_scalar(turns[:, 0, :, :], ang[:, :, :], 1.0 / TWO_PI, 0.25, ALU.mult, ALU.add))
            put(v.tensor_scalar(turns[:, 1, :, :], ang[:, :, :], 1.0 / TWO_PI, None, ALU.mult))
            settled()
            put(v.tensor_scalar(turns[:, :, :, :], turns[:, :, :, :], BIG, None, ALU.add))
            settled()
            put(v.tensor_scalar(turns[:, :, :, :], turns[:, :, :, :], -BIG, None, ALU.add))
            for part_of_turn in (C1, C2, C3):
                settled()
                for j in range(2):
                    before = ang[:, :, :] if part_of_turn == C1 else trig[:, j, :, :]
                    put(v.scalar_tensor_tensor(trig[:, j, :, :].rearrange(flat), turns[:, j, :, :].rearrange(flat), -part_of_turn,
                                               before.rearrange(flat), ALU.mult, ALU.add))
            settled()
            put(v.tensor_scalar(trig[:, 0, :, :], trig[:, 0, :, :], math.pi / 2, None, ALU.add))
            settled()
            put(v.tensor_scalar(trig[:, :, :, :], trig[:, :, :, :], PI, -PI, ALU.min, ALU.max))
            mark["angles"] = done[0]
            for i in range(2):
                dve.wait_ge(s_bg[i], 32)
                v.tensor_copy(new[i][:, :, 0, :].rearrange("p o (g d) -> p g o d", g=G),
                              old[i][:, 0, :].rearrange("p (g o d) -> p g o d", g=G, o=BLOCK)).then_inc(s_perm, 1)
            dve.wait_ge(s_gain, 32)
            put(v.tensor_scalar(gain[:, :, :], gain[:, :, :], 1.0, None, ALU.add))
            settled()
            put(v.tensor_scalar(ngain[:, :, :], gain[:, :, :], -1.0, None, ALU.mult))
            dve.wait_ge(s_trig, 1)
            settled()
            for which in (1, 0):
                for dst, of, by, lo in ((ctab[:, which, :, 0:HALF], 0, gain, 0), (ctab[:, which, :, HALF:], 0, gain, HALF),
                                        (stab[:, which, :, 0:HALF], 1, ngain, HALF), (stab[:, which, :, HALF:], 1, gain, 0)):
                    put(v.tensor_tensor(dst, trig[:, of, :, :], by[:, which, lo:lo + HALF].unsqueeze(1).broadcast_to([128, NT, HALF]),
                                        ALU.mult))
            settled()

            ROPE = 6

            def rotate(src, cos_t, sin_t, index):
                outer, inner = src.shape[1:3]

                def shaped(ap):
                    return ap.rearrange("p (a h d) -> p a h d", a=outer, d=HD)

                def cut(ap, lo, hi):
                    return ap[:, :, :, lo:hi]

                def over_heads(ap, lo, hi):
                    one = ap[:, :, lo:hi].unsqueeze(2) if ap.shape[1] == outer else ap[:, :, lo:hi].unsqueeze(1)
                    return one.broadcast_to([128, outer, inner, hi - lo])

                first = ROPE * index
                v.tensor_tensor(shaped(rp[:, 0, :]), src, src, ALU.mult).then_inc(s_rope, 1)
                dve.wait_ge(s_rope, first + 1)
                v.tensor_reduce(rms[:, 0, :], rp[:, 0, :].rearrange("p (h d) -> p h d", d=HD), AX.X, ALU.add).then_inc(s_rope, 1)
                dve.wait_ge(s_rope, first + 2)
                v.tensor_scalar(rms[:, 1, :], rms[:, 0, :], 1.0 / HD, EPS, ALU.mult, ALU.add).then_inc(s_ms, 1)
                v.tensor_tensor(shaped(rp[:, 1, :]), src, over_heads(cos_t, 0, HD), ALU.mult).then_inc(s_rope, 1)
                v.tensor_tensor(cut(shaped(rp[:, 2, :]), 0, HALF), cut(src, HALF, HD), over_heads(sin_t, 0, HALF), ALU.mult).then_inc(s_rope, 1)
                v.tensor_tensor(cut(shaped(rp[:, 2, :]), HALF, HD), cut(src, 0, HALF), over_heads(sin_t, HALF, HD), ALU.mult).then_inc(s_rope, 1)
                dve.wait_ge(s_rope, first + 5)
                v.tensor_tensor(rp[:, 3, :], rp[:, 1, :], rp[:, 2, :], ALU.add).then_inc(s_rope, 1)

            def scale_by_rstd(dst, dst_sem, index):
                outer, inner = dst.shape[1:3]
                dve.wait_ge(s_rope, ROPE * index + ROPE)
                dve.wait_ge(s_rstd, index + 1)
                per_head = rms[:, 2, :].rearrange("p (a h) -> p a h", a=outer).unsqueeze(3).broadcast_to([128, outer, inner, HD])
                v.tensor_tensor(dst, rp[:, 3, :].rearrange("p (a h d) -> p a h d", a=outer, d=HD), per_head, ALU.mult).then_inc(dst_sem, 1)

            def look_up(j):
                v.scalar_tensor_tensor(pick[:, :], iota[:, 0:NBLK], slots[:, bass.ds(NS + j, 1)], tab[:, :], ALU.is_equal, ALU.mult,
                                       accum_out=blk[:, bass.ds(NS + j, 1)]).then_inc(s_look, 1)
                dve.wait_ge(s_look, 2 * j + 1)
                v.scalar_tensor_tensor(hjunk[:, :], wrow[:, :], blk[:, bass.ds(NS + j, 1)], crow[:, :], ALU.is_equal, ALU.mult,
                                       accum_out=hits[:, bass.ds(j, 1)]).then_inc(s_look, 1)
                dve.wait_ge(s_look, 2 * j + 2)

            def four_pairs(it, looking):
                for p in range(4):
                    tile0, index, u = 8 * it + 2 * p, 4 * it + p, 2 * p
                    dve.wait_ge(s_kvc, tile0 + 2)
                    keys = kv[:, u:u + 2, 0:KVD].rearrange("p a (h d) -> p a h d", d=HD)
                    rotate(keys, ctab[:, 1, bass.ds(tile0, 2), :], stab[:, 1, bass.ds(tile0, 2), :], index)
                    if looking:
                        for j in ((0, 1), (2,), (3, 4), (5,))[p]:
                            look_up(6 * it + j)
                    scale_by_rstd(keys, s_kr, index)

            with dve.Fori(0, 2) as it:
                four_pairs(it, True)

            put(v.tensor_scalar(rtmp[:, 0, :], hits[:, 0:W], 0.0, SKIP, ALU.is_gt, ALU.mult))
            put(v.tensor_scalar(rtmp[:, 1, :], hits[:, 0:W], 0.0, SKIP, ALU.is_equal, ALU.mult))
            settled()
            put(v.tensor_tensor(rd[:, 0, :], rtmp[:, 0, :], blk[:, NS:NS + W], ALU.add))
            put(v.scalar_tensor_tensor(rd[:, 1, :], hits[:, 0:W], -1.0, rtmp[:, 1, :], ALU.add, ALU.add))
            settled()
            for j in range(2):
                for f in range(GB):
                    put(v.tensor_scalar(gspread[:, j, f, :], rd[:, j, :], in_group[:, f:f + 1], None, ALU.mult))
            dve.wait_ge(s_adapt, 16)
            put(v.tensor_copy(cf[:, 2:3], adapt_i[:, :]))
            settled()
            put(v.tensor_scalar(adiag[:, :], ident[:, :], cf[:, 2:3], None, ALU.mult))
            mark["reads"] = done[0]
            four_pairs(2, False)
            put(v.tensor_copy(keypos[:, :], key_i[:, :, :].rearrange("p o w -> p (o w)")))
            dve.wait_ge(s_scal, 16)
            dve.wait_ge(s_reads, 1)
            put(v.tensor_copy(rd_idx[0:ROWS, :, :].rearrange("p j n -> p (j n)"), ps[7][0:ROWS, 0:2 * NG]))
            mark["second"] = done[0]
            put(v.tensor_scalar(amask[:, :], ps[7][:, 128:128 + B], part[:, 5:6], scal_col[:, :], ALU.is_equal, ALU.mult))
            mark["amask"] = done[0]
            settled()
            four_pairs(3, False)

            for i in range(2):
                dve.wait_ge(s_gold[i], 32)
                for piece in range(4):
                    v.tensor_copy(*reordered_piece(i, 0, piece)).then_inc(s_order[i], 1)

            def make_pen(n, n0):
                v.tensor_scalar(pen_hi[:, :], keypos[:, :], tok_hi[:, bass.ds(n, 1)], None, ALU.is_gt).then_inc(s_pen1, 1)
                dve.wait_ge(s_pen1, n + 1)
                v.scalar_tensor_tensor(pen[n0 % 2][:, :], keypos[:, :], tok_lo[:, bass.ds(n, 1)], pen_hi[:, :],
                                       ALU.is_le, ALU.add).then_inc(s_pen, 1)

            def slot(it, k):
                b = 16 * it + k
                if k == -8:
                    make_pen(0, 0)
                if 0 <= k < B:
                    dve.wait_ge(s_qk, b + 1)
                    v.tensor_reduce(nmax[:, k % 4, :], ps_s[k % 2][:, 0:HPG * KEYS].rearrange("p (h k) -> p h k", h=HPG),
                                    AX.X, ALU.max, negate=True).then_inc(s_max, 1)
                for kind, n in fin_step(k):
                    bank, _ = misc((kind, n), it)
                    if kind == "x2":
                        await_step(dve, (kind, n), it)
                        v.tensor_tensor(x2s[n % 2][:, :], ps_m[bank][:, 0:T], xin[n % 4][:, :], ALU.add).then_inc(s_empty[bank], 1)
                    if kind == "xa":
                        await_step(dve, (kind, n), it)
                        v.tensor_tensor(xam[n % 2][:, :].rearrange("p (f t) -> p f t", f=TB),
                                        ps_m[bank][:, 0:128].rearrange("p (f t) -> p f t", f=TB),
                                        amask[:, bass.ds(16 * it + 4 * n, TB)].unsqueeze(2).broadcast_to([128, TB, C]),
                                        ALU.mult).then_inc(s_empty[bank], 1)
                if 0 <= k < B:
                    dve.wait_ge(s_vt, b + 1)
                    v.tensor_copy(vs[k % 4][:, :, :].rearrange("p c d -> p (c d)"), ps_v[0:HK, 0:2 * KVD]).then_inc(s_vc, 1)
                    dve.wait_ge(s_exp, b + 1)
                    v.reciprocal(rrec[:, k % 4, :], rsum[:, k % 4, :]).then_inc(s_rec, 1)
                    dve.wait_ge(s_rec, b + 1)
                    if k >= 2:
                        dve.wait_ge(s_pt, b - 1)
                    for h in range(HPG):
                        last = v.tensor_scalar(pn[k % 2][:, h, :], pex[k % 2][:, h, :], rrec[:, k % 4, h:h + 1], None, ALU.mult)
                    last.then_inc(s_pn, 1)
                for kind, n in prep_steps(k - 1):
                    if kind == "q":
                        scale_by_rstd(qr[n % 2][:, :].rearrange("p (h g d) -> p g h d", g=G, d=HD), s_qrd, NT // 2 + 4 * it + n)
                if 0 <= k < B - 4 and k % 4 == 1:
                    make_pen(4 * it + k // 4 + 1, k // 4 + 1)
                for kind, n in prep_steps(k):
                    bank, _ = misc((kind, n), it)
                    if kind in ("k0", "k1", "k2", "k3"):
                        await_step(dve, (kind, n), it)
                        o = 4 * int(kind[1])
                        v.tensor_copy(kT[n % 2][:, :, o:o + 4, :].rearrange("p f o w -> p o f w"),
                                      ps_m[bank][:, 0:4 * ROWS].rearrange("p (o f w) -> p o f w", o=4, w=W)).then_inc(s_empty[bank], 1)
                if 0 <= k and k // 8 + 2 < NG and k % 8 < 4:
                    i = k // 8 % 2
                    if k % 8 == 0:
                        dve.wait_ge(s_gold[i], 32 * (it + k // 16 + 1) + 32)
                        await_copied(dve, ("v2", k // 8), it)
                        await_copied(dve, ("v3", k // 8), it)
                    v.tensor_copy(*reordered_piece(i, 0, k % 8)).then_inc(s_order[i], 1)
                for kind, n in prep_steps(k):
                    if kind == "q":
                        await_copied(dve, (kind, n), it)
                        at = 4 * it + n
                        rotate(qs[n % 2][:, :].rearrange("p (g h d) -> p g h d", g=G, d=HD),
                               ctab[:, 0, bass.ds(at, 1), :], stab[:, 0, bass.ds(at, 1), :], NT // 2 + at)

            run_slots(dve, slot)

        @block.gpsimd
        def _(pool):
            made = [0]

            def make(ins):
                made[0] += 1
                ins.then_inc(s_cchain, 1)

            def settled():
                pool.wait_ge(s_cchain, made[0])

            make(pool.memset(zcol[:, :], 0.0))
            make(pool.memset(ident[:, :], 0.0))
            make(pool.iota(iota_i[:, :], pattern=[[1, NW]], base=0, channel_multiplier=0))
            make(pool.iota(part_i[:, :], pattern=[[0, 1]], base=0, channel_multiplier=1))
            settled()
            make(pool.affine_select(out=ident[:, :], in_=ident[:, :], compare_op=ALU.not_equal, fill=1.0, base=0,
                                    pattern=[[-1, 128]], channel_multiplier=1))
            assert made[0] == cmark_iota
            for i, (s_idx, idx, w) in enumerate(((s_cond, cond_i, w0), (s_subj, subj_i, w2))):
                pool.wait_ge(s_idx, 16)
                pool.indirect_dma_start(out=wpick[i][:, :], out_offset=None, in_=w.rearrange("s c d -> s (c d)"),
                                        in_offset=bass.IndirectOffsetOnAxis(ap=idx[:, 0:1], axis=0),
                                        bounds_check=w.shape[0] - 1, oob_is_err=False).then_inc(s_pick[i], 16)
                if i == 0:
                    make(pool.memset(ones[:, :], 1.0))
                    make(pool.memset(bd[:, :, :], 0.0))
                    make(pool.memset(later_or_same[:, :, :], 1.0))
                    assert made[0] == cmark_bd + 1
            settled()
            make(pool.affine_select(out=later_or_same[:, 0:NS - 1, :], in_=later_or_same[:, 0:NS - 1, :], compare_op=ALU.is_ge,
                                    fill=0.0, base=0, pattern=[[0, NS - 1], [-1, 128]], channel_multiplier=1))
            make(pool.affine_select(out=later_or_same[:, NS - 1:, :], in_=later_or_same[:, NS - 1:, :], compare_op=ALU.is_gt,
                                    fill=0.0, base=0, pattern=[[0, NS], [-1, 128]], channel_multiplier=1))
            assert made[0] == cmark_masks
            make(pool.memset(mask_sel[:, :, :], 0.0))
            make(pool.memset(halfpow[:, :], -0.5))
            for i in range(HALF):
                make(pool.memset(inv[:, i:i + 1], 1.0 / 10000.0 ** (i / HALF)))
            make(pool.iota(key_i[:, :, :], pattern=[[1, BLOCK], [BLOCK, W]], base=0, channel_multiplier=0))
            settled()
            sel_v = mask_sel[:, :, :].rearrange("p f (g t) -> p f g t", g=G)
            make(pool.affine_select(out=sel_v, in_=sel_v, compare_op=ALU.not_equal, fill=NEG, base=0,
                                    pattern=[[-C, TB], [0, G], [-1, C]], channel_multiplier=1))
            assert made[0] == cmark_all

            pool.wait_ge(s_dset, mark["base"])
            pool.wait_ge(s_zero, 2)
            for i in range(2):
                for j, src in enumerate((k_old, v_old)):
                    pool.indirect_dma_start(out=old[i][:, j, :], out_offset=None, in_=src,
                                            in_offset=bass.IndirectOffsetOnAxis(ap=base_idx[:, i:i + 1], axis=0),
                                            bounds_check=POOL_BLOCKS - 1, oob_is_err=False).then_inc(s_bg[i], 16)
            pool.wait_ge(s_w3, 32)
            for r in range(2):
                at = wnat[:, 12 + 3 * r, :]
                pool.tensor_tensor(out=at, in0=at, in1=ident[:, :], op=ALU.add).then_inc(s_w3i, 1)
            for i in range(2):
                make(pool.memset(qbd[i][:, :, :, :], 0.0))
            assert made[0] == cmark_qbd
            def past_waits():
                pool.sem_inc(s_passed, 1)

            def rstd(index):
                pool.wait_ge(s_ms, index + 1)
                pool.tensor_tensor(out=rms[:, 2, :], in0=rms[:, 1, :], in1=halfpow[:, :], op=ALU.pow).then_inc(s_rstd, 1)

            def pair(it, p):
                tile0, u0, index = 8 * it + 2 * p, 2 * p, 4 * it + p
                for u in (u0, u0 + 1):
                    if not isinstance(it, int) or it > 0:
                        pool.wait_ge(s_scat[u], 16 * it)
                    past_waits()
                    pool.tensor_copy(kv_idx[:, u:u + 1], tok_idx[:, bass.ds(tile0 + (u - u0), 1)]).then_inc(s_tix, 1)
                rstd(index)
                pool.wait_ge(s_kr, index + 1)
                if isinstance(it, int) and index == 0:
                    pool.wait_ge(s_zfill, 32)
                    for i in range(2):
                        pool.wait_ge(s_bs[i], 16)
                pool.wait_ge(s_tix, tile0 + 2)
                past_waits()
                for u in (u0, u0 + 1):
                    pool.indirect_dma_start(out=new_d, out_offset=bass.IndirectOffsetOnAxis(ap=kv_idx[:, u:u + 1], axis=0),
                                            in_=kv[:, u, :], in_offset=None,
                                            bounds_check=NW * BLOCK - 1, oob_is_err=False).then_inc(s_scat[u], 16)

            def stage_index(i, j, g2):
                past_waits()
                pool.tensor_copy(g_idx[0:ROWS, 2 * i + j:2 * i + j + 1], rd_idx[0:ROWS, j, bass.ds(g2, 1)]).then_inc(s_gix[j], 1)

            def gather_old(i, g2):
                stage_index(i, 0, g2)
                pool.wait_ge(s_gix[0], g2 + 1)
                past_waits()
                for j, src in enumerate((k_old, v_old)):
                    pool.indirect_dma_start(out=old[i][0:ROWS, j, :], out_offset=None, in_=src,
                                            in_offset=bass.IndirectOffsetOnAxis(ap=g_idx[0:ROWS, 2 * i:2 * i + 1], axis=0),
                                            bounds_check=POOL_BLOCKS - 1, oob_is_err=False).then_inc(s_gold[i], 16)

            def gather_new(i, g2, reordered):
                stage_index(i, 1, g2)
                pool.wait_ge(s_gix[1], g2 + 1)
                pool.wait_ge(s_order[i], reordered)
                past_waits()
                pool.indirect_dma_start(out=new[i][0:ROWS, :, :, :].rearrange("p o k c -> p (o k c)"), out_offset=None, in_=new_blocks,
                                        in_offset=bass.IndirectOffsetOnAxis(ap=g_idx[0:ROWS, 2 * i + 1:2 * i + 2], axis=0),
                                        bounds_check=NW - 1, oob_is_err=False).then_inc(s_gnew[i], 16)

            def reorder_values(i, piece):
                pool.tensor_copy(*reordered_piece(i, 1, piece)).then_inc(s_order[i], 1)

            pool.wait_ge(s_dset, mark["tokens"])
            for p in range(4):
                pair(0, p)
            with pool.Fori(1, NT // 8 - 1) as it:
                for p in range(4):
                    pair(it, p)
            pair(NT // 8 - 1, 0)
            pool.wait_ge(s_dset, mark["second"])
            for i in range(2):
                gather_old(i, i)
            for p in range(1, 4):
                pair(NT // 8 - 1, p)
            for u in range(8):
                pool.wait_ge(s_scat[u], 16 * (NT // 8))
            for i in range(2):
                gather_new(i, i, 8)
            gather_old(0, 2)

            def slot(it, k):
                b = 16 * it + k
                for kind, n in prep_steps(k):
                    if kind == "q":
                        rstd(NT // 2 + 4 * it + n)
                if 0 <= k and k // 8 + 2 < NG:
                    i, j = (k // 8) % 2, k % 8
                    fills = it + k // 16 + 1
                    if j == 0:
                        pool.wait_ge(s_gold[i], 32 * fills + 32)
                        await_copied(pool, ("v2", k // 8), it)
                        await_copied(pool, ("v3", k // 8), it)
                    if j < 4:
                        past_waits()
                        reorder_values(i, j)
                    if j == 4:
                        pool.wait_ge(s_gnew[i], 16 * fills)
                        gather_new(i, 2 * it + k // 8 + 2, 8 * fills + 8)
                    if j == 5 and k // 8 + 3 < NG:
                        gather_old(1 - i, 2 * it + k // 8 + 3)

            run_slots(pool, slot)

        @block.sync
        def _(sp):
            column = "(b u) -> b u"
            sp.dma_start(kvlen_i[:, :], kvlen.rearrange(column, u=1)).then_inc(s_len, 16)
            sp.dma_start(cond_i[:, :], cond.rearrange(column, u=1)).then_inc(s_cond, 16)
            sp.dma_start(table_i[:, :], table).then_inc(s_tab, 16)
            sp.dma_start(subj_i[:, :], subj.rearrange(column, u=1)).then_inc(s_subj, 16)
            for u in range(4):
                sp.dma_start(xin[u][:, :], x_t[u, :, :]).then_inc(s_xin[u], 16)
            sp.wait_ge(s_cchain, cmark_bd)
            for i, wd in enumerate((w0_d, w2_d)):
                sp.wait_ge(s_dset, mark[f"w{i}"])
                sp.dma_start(wd, wpick[i][:, :]).then_inc(s_pickw[i], 16)
                if i == 0:
                    sp.wait_ge(s_pickw[0], 16)
                    for f in range(TB):
                        sp.dma_start(bd[C * f:C * f + C, :, C * f:C * f + C],
                                     w0_d.rearrange("(n f) (c d) -> f c n d", f=TB, d=C)[f]).then_inc(s_bd[0], 16)

            sp.wait_ge(s_cchain, cmark_qbd)
            for j in range(2):
                sp.dma_start(new_rows[1][:, 2048 * j:2048 * j + 2048], qbd[j][:, :, :, :].rearrange("p f h t -> p (f h t)")).then_inc(s_zfill, 16)
            sp.wait_ge(s_perm, 4)
            for i, s in enumerate((0, NS - 1)):
                sp.dma_start(new_rows[s], new[i][:, :, :, :].rearrange("p o k c -> p (o k c)")).then_inc(s_bs[i], 16)

            def load_and_spill(n, u, load):
                if load:
                    sp.wait_ge(s_l0, n + 1)
                    sp.dma_start(xin[u][:, :], x_t[n + 4, :, :]).then_inc(s_xin[u], 16)
                sp.wait_ge(s_x1c, n + 1)
                sp.dma_start(x1_d[n, :, :], x1s[u][:, :]).then_inc(s_spill[u], 16)

            with sp.Fori(0, NT // 4 - 1) as it:
                for u in range(4):
                    load_and_spill(4 * it + u, u, True)
            for u in range(4):
                load_and_spill(NT - 4 + u, u, False)
            sp.wait_ge(s_pickw[1], 16)
            for u in range(4):
                sp.wait_ge(s_spill[u], 16 * (NT // 4))
            for u in range(4):
                sp.dma_start(xin[u][:, :], x1_d[u, :, :]).then_inc(s_x1[u], 16)
            for f in range(TB):
                sp.dma_start(bd[C * f:C * f + C, :, C * f:C * f + C],
                             w2_d.rearrange("(n f) (c d) -> f c n d", f=TB, d=C)[f]).then_inc(s_bd[1], 16)

            def slot(it, k):
                for kind, n in fin_step(k):
                    if kind == "x2" and n + 4 < NT:
                        await_copied(sp, (kind, n), it)
                        sp.dma_start(xin[n % 4][:, :], x1_d[4 * it + n + 4, :, :]).then_inc(s_x1[n % 4], 16)
                    if kind == "x4":
                        await_copied(sp, (kind, n), it)
                        sp.dma_start(out_t[4 * it + n, :, :], x4s[n % 2][:, :]).then_inc(s_out[n % 2], 16)

            run_slots(sp, slot)
            for u in range(2):
                sp.wait_ge(s_out[u], 16 * (NT // 2))

        @block.scalar
        def _(act):
            a = nc.scalar
            halves = "o (c d) -> o c d"
            act.wait_ge(s_cchain, 1)
            for i in range(2):
                a.activation(old[i][:, :, :].rearrange("p k c -> p (k c)"), zcol[:, :].broadcast_to([128, 2 * G * BLOCK * HD]), ACT.Copy).then_inc(s_zero, 1)
            act.dma_start(wnat[:, 0:2, :], wk.rearrange(halves, c=2)).then_inc(s_wk, 16)
            act.dma_start(wnat[:, 2:4, :], wv.rearrange(halves, c=2)).then_inc(s_wk, 16)
            act.dma_start(adapt_i[:, :], adapt.rearrange("(b u) -> b u", u=1)).then_inc(s_adapt, 16)
            act.dma_start(gain[:, 0, :], qscale.partition_broadcast(128)).then_inc(s_gain, 16)
            act.dma_start(gain[:, 1, :], kscale.partition_broadcast(128)).then_inc(s_gain, 16)
            act.dma_start(scal_col[:, :], s3.rearrange("(a u) -> a u", u=1).broadcast_to([NA, RANK])).then_inc(s_scal, 16)
            for at, w, s_w in ((4, wq, s_wq), (8, wo, s_wo), (12, w3, s_w3)):
                for r in range(2):
                    rows = w[128 * r:128 * r + 128, :]
                    if w is wo:
                        for h in range(HPG):
                            act.dma_start(wnat[:, at + 2 * r + h, :].rearrange("p (g d) -> p g d", g=G),
                                          rows.rearrange("o (g h d) -> o g h d", g=G, h=HPG)[:, :, h, :]).then_inc(s_w, 16)
                    else:
                        act.dma_start(wnat[:, at + 2 * r:at + 2 * r + 2, :], rows.rearrange(halves, c=2)).then_inc(s_w, 16)
            act.dma_start(wnat[:, 16:18, :], a3.rearrange("a r (c d) -> (a r) c d", c=2)).then_inc(s_ab, 16)
            for c in range(2):
                act.dma_start(wnat[:, 18 + c, :].rearrange("p (a r) -> p a r", a=NA),
                              b3[:, 128 * c:128 * c + 128, :].rearrange("a o r -> o a r")).then_inc(s_ab, 16)
            for i, dst in enumerate((wkvT, wqT, woT, w3T, abT)):
                if i == 3:
                    act.wait_ge(s_dset, mark["angles"])
                    a.activation(trig[:, :, :, :], trig[:, :, :, :], ACT.Sin).then_inc(s_trig, 1)
                act.wait_ge(s_wt, i + 1)
                a.activation(dst[:, :, :].rearrange("p c o -> p (c o)"), ps[i][:, :], ACT.Copy).then_inc(s_wtc, 1)
            for i in range(2):
                act.wait_ge(s_bg[i], 32)
                a.activation(new[i][:, :, 1, :].rearrange("p o (g d) -> p g o d", g=G),
                             old[i][:, 1, :].rearrange("p (g o d) -> p g o d", g=G, o=BLOCK), ACT.Copy).then_inc(s_perm, 1)

            def copy_x1T(n, u):
                act.wait_ge(s_l0, n + 1)
                if not isinstance(n, int) or n >= 2:
                    act.wait_ge(s_kvp, n - 1)
                a.activation(xT[u % 2][:, :, :].rearrange("p c t -> p (c t)"), ps[u % 2][:, 0:T], ACT.Copy).then_inc(s_xtc, 1)

            def copy_kv_x1(n, u, turn):
                if turn is not None:
                    act.wait_ge(s_scat[u], 16 * turn)
                act.wait_ge(s_kvp, n + 1)
                a.activation(kv[:, u, :], ps[4 + u % 2][:, 0:2 * KVD], ACT.Copy).then_inc(s_kvc, 1)
                if turn is not None or u >= 4:
                    act.wait_ge(s_spill[u % 4], 16 * (2 * (0 if turn is None else turn) + u // 4))
                a.activation(x1s[u % 4][:, :], ps[2 + u % 2][:, 0:T], ACT.Copy).then_inc(s_x1c, 1)

            def eight(n0, turn, last):
                for u in range(8):
                    if not (last and u == 7):
                        copy_x1T(n0 + u + 1, u + 1)
                    copy_kv_x1(n0 + u, u, turn)

            copy_x1T(0, 0)
            eight(0, None, False)
            with act.Fori(1, NT // 8 - 1) as it:
                eight(8 * it, it, False)
            eight(NT - 8, NT // 8 - 1, True)
            for i in range(2):
                act.wait_ge(s_gold[i], 32)
                for piece in range(4):
                    a.activation(*reordered_piece(i, 1, piece), ACT.Copy).then_inc(s_order[i], 1)

            def slot(it, k):
                b = 16 * it + k
                for kind, n in fin_step(k):
                    bank, _ = misc((kind, n), it)
                    if kind == "x3":
                        await_step(act, (kind, n), it)
                        a.activation(x3T[n % 2][:, :, :].rearrange("p c t -> p (c t)"), ps_m[bank][:, 0:T], ACT.Copy).then_inc(s_empty[bank], 1)
                    if kind == "x4":
                        if n >= 2:
                            act.wait_ge(s_out[n % 2], 16 * (2 * it + n // 2))
                        await_step(act, (kind, n), it)
                        a.activation(x4s[n % 2][:, :], ps_m[bank][:, 0:T], ACT.Copy).then_inc(s_empty[bank], 1)
                if 0 <= k < B:
                    act.wait_ge(s_max, b + 1)
                    if k >= 2:
                        act.wait_ge(s_pn, b - 1)
                    for h in range(HPG):
                        last = a.activation(pex[k % 2][:, h, :], ps_s[k % 2][:, h * KEYS:(h + 1) * KEYS], ACT.Exp,
                                            bias=nmax[:, k % 4, h:h + 1], accum_out=rsum[:, k % 4, h:h + 1])
                    last.then_inc(s_exp, 1)
                if 0 <= k - 1 < B:
                    if k >= 3:
                        act.wait_ge(s_pv, b - 2)
                    act.wait_ge(s_pt, b)
                    a.activation(pT[(k - 1) % 2][:, :, :, :].rearrange("p c h t -> p (c h t)"), ps_p[(k - 1) % 2][0:HK, :],
                                 ACT.Copy).then_inc(s_ptc, 1)
                for kind, n in prep_steps(k):
                    bank, _ = misc((kind, n), it)
                    m = ps_m[bank]
                    if kind == "x1":
                        await_step(act, (kind, n), it)
                        a.activation(xT[n % 2][:, :, :].rearrange("p c t -> p (c t)"), m[:, 0:T], ACT.Copy).then_inc(s_empty[bank], 1)
                    if kind == "q":
                        await_step(act, (kind, n), it)
                        a.activation(qs[n % 2][:, :], m[:, 0:T], ACT.Copy).then_inc(s_empty[bank], 1)
                    if kind == "qT":
                        await_step(act, (kind, n), it)
                        for g in range(G):
                            rows = slice(HD * g, HD * g + HD)
                            last = a.activation(
                                qbd[n // 2 % 2][rows, TB * (n % 2):TB * (n % 2) + TB, :, C * g:C * g + C],
                                m[rows, 0:HPG * 128].rearrange("p (h f t) -> p f h t", h=HPG, f=TB), ACT.Copy, scale=SCALE)
                        last.then_inc(s_empty[bank], 1)
                    if kind in ("v0", "v1", "v2", "v3"):
                        await_step(act, (kind, n), it)
                        o = 4 * int(kind[1])
                        a.activation(vT[n % 2][:, :, o:o + 4, :].rearrange("p f o w -> p o f w"),
                                     m[:, 0:4 * ROWS].rearrange("p (o f w) -> p o f w", o=4, w=W), ACT.Copy).then_inc(s_empty[bank], 1)
                if k % 4 == 1 and 0 <= (k - 5) // 4 < NT:
                    n = (k - 5) // 4
                    act.wait_ge(s_pv, 16 * it + 4 * n + 4)
                    a.activation(oT[n % 2][:, :, :, :].rearrange("p h f t -> p f h t"),
                                 ps_o[:, 0:TB * HPG * C].rearrange("p (f h t) -> p f h t", f=TB, h=HPG), ACT.Copy).then_inc(s_oc, 1)

            run_slots(act, slot)

        @block.tensor
        def _(pe):
            mm, turn_over = nc.tensor.matmul, nc.tensor.transpose

            def turn_weights(i):
                o = ps[i][:, :].rearrange("p (c o) -> p c o", c=2)
                for c in range(2):
                    for r in range(2):
                        dst = o[:, c, 128 * r:128 * r + 128]
                        if i == 0:
                            src = wnat[:, 2 * r + c, :]
                        elif i == 4:
                            src = wnat[:, 16 + 2 * c + r, :]
                        else:
                            src = wnat[:, 4 * i + 2 * r + c, :]
                        last = turn_over(dst, src, ident[:, :])
                last.then_inc(s_wt, 1)

            pe.wait_ge(s_cchain, cmark_iota)
            pe.wait_ge(s_wk, 32)
            turn_weights(0)
            pe.wait_ge(s_wq, 32)
            turn_weights(1)
            pe.wait_ge(s_wo, 64)
            turn_weights(2)
            pe.wait_ge(s_cchain, cmark_bd)
            pe.wait_ge(s_dset, mark["diag"])
            mm(ps[6][:, 0:NW], ones[:, :], diag[:, :, :].rearrange("p s b -> p (s b)"), start=True, stop=True).then_inc(s_wrow, 1)
            pe.wait_ge(s_dset, mark["same"])
            for s in range(NS):
                for t in range(NS):
                    last = mm(ps[7][:, s * (BLOCK + 1):(s + 1) * (BLOCK + 1)], same[:, t, 128 * s:128 * s + 128], valid[:, t, :],
                              start=(t == 0), stop=(t == NS - 1))
            last.then_inc(s_later, 1)
            pe.wait_ge(s_dset, mark["owner"])
            mm(ps[6][:, 0:NW], ones[:, :], diag[:, :, :].rearrange("p s b -> p (s b)"), start=True, stop=True).then_inc(s_crow, 1)
            pe.wait_ge(s_dset, mark["spread"])
            for i in range(3):
                last = mm(ps[6][:, NT * i:NT * i + NT], spread[:, i, :], of_tile[:, :], start=True, stop=True)
            last.then_inc(s_relay, 1)
            pe.wait_ge(s_w3i, 2)
            turn_weights(3)
            pe.wait_ge(s_ab, 48)
            turn_weights(4)

            pe.wait_ge(s_bd[0], 16 * TB)
            pe.wait_ge(s_wtc, 5)

            def first_stage(n, u, turn):
                pe.wait_ge(s_xin[u % 4], 16 * (2 * turn + u // 4) + 16)
                if not isinstance(n, int) or n >= 2:
                    pe.wait_ge(s_xtc, n - 1)
                for c in range(2):
                    last = mm(ps[u % 2][:, 128 * c:128 * c + 128], xin[u % 4][:, 128 * c:128 * c + 128],
                              bd[:, bass.ds(n, 1), :].rearrange("p a b -> p (a b)"), start=True, stop=True)
                last.then_inc(s_l0, 1)

            def project(n, u):
                pe.wait_ge(s_xtc, n + 1)
                if not isinstance(n, int) or n >= 2:
                    pe.wait_ge(s_kvc, n - 1)
                    pe.wait_ge(s_x1c, n - 1)
                for c in range(2):
                    last = turn_over(ps[2 + u % 2][:, 128 * c:128 * c + 128], xT[u % 2][:, c, :], ident[:, :])
                last.then_inc(s_tr1, 1)
                for c in range(2):
                    last = mm(ps[4 + u % 2][:, 0:2 * KVD], xT[u % 2][:, c, :], wkvT[:, c, :], start=(c == 0), stop=(c == 1))
                last.then_inc(s_kvp, 1)

            def eight(n0, turn, last):
                for u in range(8):
                    if not (last and u == 7):
                        first_stage(n0 + u + 1, (u + 1) % 8, turn + (u + 1) // 8)
                    project(n0 + u, u)

            first_stage(0, 0, 0)
            eight(0, 0, False)
            with pe.Fori(1, NT // 8 - 1) as it:
                eight(8 * it, it, False)
            pe.wait_ge(s_dset, mark["reads"])
            for j in range(2):
                mm(ps[7][0:ROWS, NG * j:NG * j + NG], gspread[:, j, :, :].rearrange("p f w -> p (f w)"), of_group[:, :],
                   start=True, stop=True)
            mm(ps[7][:, 128:128 + B], ones[:, :], adiag[:, :], start=True, stop=True).then_inc(s_reads, 1)
            eight(NT - 8, NT // 8 - 1, True)

            pe.wait_ge(s_xtc, NT)
            pe.wait_ge(s_kvc, NT)
            pe.wait_ge(s_x1c, NT)
            pe.wait_ge(s_dset, mark["amask"])
            pe.wait_ge(s_cchain, cmark_qbd)

            def misc_step(it, kind, n):
                bank, _ = misc((kind, n), it)
                m = ps_m[bank]
                if kind == "x1":
                    pe.wait_ge(s_x1[n % 4], 16 * (it + n // 4) + 16)
                    await_bank(pe, (kind, n), it)
                    for c in range(2):
                        last = turn_over(m[:, 128 * c:128 * c + 128], xin[n % 4][:, 128 * c:128 * c + 128], ident[:, :])
                if kind == "q":
                    await_copied(pe, ("x1", n), it)
                    await_bank(pe, (kind, n), it)
                    for c in range(2):
                        last = mm(m[:, 0:T], xT[n % 2][:, c, :], wqT[:, c, :], start=(c == 0), stop=(c == 1))
                if kind == "qT":
                    pe.wait_ge(s_qrd, 4 * it + n + 1)
                    await_bank(pe, (kind, n), it)
                    for h in range(HPG):
                        last = turn_over(m[:, 128 * h:128 * h + 128],
                                         qr[n % 2][:, 128 * h:128 * h + 128], ident[:, :])
                if kind[0] in "kv":
                    i, which, o0 = n % 2, int(kind[0] == "v"), 4 * int(kind[1])
                    if kind == "k0":
                        pe.wait_ge(s_gnew[i], 16 * (it + n // 2) + 16)
                    await_bank(pe, (kind, n), it)
                    for o in range(4):
                        last = turn_over(m[:, ROWS * o:ROWS * o + ROWS], new[i][0:ROWS, o0 + o, which, :], ident[0:ROWS, 0:ROWS])
                if kind == "x2":
                    pe.wait_ge(s_oc, 4 * it + n + 1)
                    await_bank(pe, (kind, n), it)
                    for h in range(HPG):
                        last = mm(m[:, 0:T], oT[n % 2][:, h, :, :].rearrange("p f t -> p (f t)"), woT[:, h, :],
                                  start=(h == 0), stop=(h == HPG - 1))
                if kind == "x3":
                    if n == 0:
                        pe.wait_ge(s_bd[1], 16 * TB)
                    await_copied(pe, ("x2", n), it)
                    await_bank(pe, (kind, n), it)
                    for c in range(2):
                        last = mm(m[:, 128 * c:128 * c + 128], x2s[n % 2][:, 128 * c:128 * c + 128],
                                  bd[:, bass.ds(4 * it + n, 1), :].rearrange("p a b -> p (a b)"), start=True, stop=True)
                if kind == "xa":
                    await_copied(pe, ("x3", n), it)
                    await_bank(pe, (kind, n), it)
                    for c in range(2):
                        last = mm(m[:, 0:128], abT[:, 0, 128 * c:128 * c + 128], x3T[n % 2][:, c, :], start=(c == 0), stop=(c == 1))
                if kind == "x4":
                    await_copied(pe, ("xa", n), it)
                    await_bank(pe, (kind, n), it)
                    for c in range(2):
                        mm(m[:, 0:T], x3T[n % 2][:, c, :], w3T[:, c, :], start=(c == 0), stop=False)
                    last = mm(m[:, 0:T], xam[n % 2][:, :], abT[:, 1, :], start=False, stop=True)
                last.then_inc(s_full[bank], 1)

            def slot(it, k):
                b = 16 * it + k
                if 0 <= k < B:
                    grp, f, n = k // 8, k % 8, k // 4
                    if k % 4 == 0:
                        await_copied(pe, ("qT", n), it)
                        pe.wait_ge(s_pen, 4 * it + n + 1)
                    if f == 0:
                        await_copied(pe, ("k2", grp), it)
                        await_copied(pe, ("k3", grp), it)
                    if k >= 2:
                        pe.wait_ge(s_exp, b - 1)
                    for h in range(HPG):
                        dst = ps_s[k % 2][:, h * KEYS:(h + 1) * KEYS]
                        mm(dst, qbd[grp % 2][:, f, h, :], kT[grp % 2][:, f, :, :].rearrange("p o w -> p (o w)"), start=True, stop=False)
                        last = mm(dst, mask_sel[:, k % 4, :], pen[n % 2][:, :], start=False, stop=True)
                    last.then_inc(s_qk, 1)
                for kind, n in fin_step(k):
                    misc_step(it, kind, n)
                if 0 <= k < B:
                    if f == 0:
                        await_copied(pe, ("v2", grp), it)
                        await_copied(pe, ("v3", grp), it)
                    if k >= 1:
                        pe.wait_ge(s_vc, b)
                    for c in range(2):
                        last = turn_over(ps_v[0:HK, KVD * c:KVD * c + KVD],
                                         vT[grp % 2][:, f, HB * c:HB * c + HB, :].rearrange("p o w -> p (o w)"), ident[:, :])
                    last.then_inc(s_vt, 1)
                if 0 <= k - 1 < B:
                    pe.wait_ge(s_pn, b)
                    if k >= 3:
                        pe.wait_ge(s_ptc, b - 2)
                    for c in range(2):
                        for h in range(HPG):
                            last = turn_over(ps_p[(k - 1) % 2][0:HK, (HPG * c + h) * 128:(HPG * c + h + 1) * 128],
                                             pn[(k - 1) % 2][:, h, HK * c:HK * c + HK], ident[:, :])
                    last.then_inc(s_pt, 1)
                for kind, n in prep_steps(k):
                    misc_step(it, kind, n)
                if 0 <= k - 2 < B:
                    kb = k - 2
                    pe.wait_ge(s_ptc, b - 1)
                    pe.wait_ge(s_vc, b - 1)
                    if kb % 4 == 0 and kb >= 4:
                        pe.wait_ge(s_oc, 4 * it + kb // 4)
                    col = HPG * C * (kb % 4)
                    for c in range(2):
                        for g in range(G):
                            last = mm(ps_o[HD * g:HD * g + HD, col:col + HPG * C], vs[kb % 4][:, c, HD * g:HD * g + HD],
                                      pT[kb % 2][:, c, :, C * g:C * g + C], start=(c == 0), stop=(c == 1))
                    last.then_inc(s_pv, 1)

            run_slots(pe, slot)


_INS = ["x", "itok_B_1_198", "itok_Bx257_0_4111", "itok_B_37_3939", "itok_B_0_7", "itok_B_0_6", "L0_cond_weights", "L1_cond_Wq",
        "L1_cond_Wk", "L1_cond_Wv", "L1_cond_Wo", "L1_cond_q_norm_scale", "L1_cond_k_norm_scale", "L1_cond_k_blocks",
        "L1_cond_v_blocks", "L2_cond_weights", "L3_cond_W", "L3_cond_A", "L3_cond_Bm", "L3_cond_scalings"]
_OUTS = [((128, 32, 256), "float32")]


def kernel(**inputs):
    import numpy as _np
    import concourse.bacc as _bacc
    from concourse import mybir as _mybir
    from concourse.bass_utils import run_bass_kernel_spmd as _run

    nc = _bacc.Bacc("TRN2", target_bir_lowering=False, num_devices=1)
    arrays, args = {}, []
    for name in _INS:
        a = _np.ascontiguousarray(inputs[name])
        arrays[f"in_{name}_dram"] = a
        args.append(nc.dram_tensor(f"in_{name}_dram", a.shape, _mybir.dt.from_np(a.dtype), kind="ExternalInput").ap())
    for i, (shape, dtype) in enumerate(_OUTS):
        dt = _mybir.dt.from_np(_np.dtype(dtype))
        args.append(nc.dram_tensor(f"out_{i}_dram", shape, dt, kind="ExternalOutput").ap())
    cond_resid_kernel(nc, *args)
    r = _run(nc, [arrays], core_ids=[0])
    return r.results[0]["out_0_dram"]
```

```python
import math
from contextlib import ExitStack

import concourse.bass as bass
from concourse import mybir


def cond_resid_kernel(
    nc, x, cond, table, kvlen, subj, adapt, w0, wq, wk, wv, wo, qscale, kscale, k_blocks, v_blocks, w2, w3, a3, b3, s3, out
):
    f32, bf16, i32 = mybir.dt.float32, mybir.dt.bfloat16, mybir.dt.int32
    ALU = mybir.AluOpType
    ACT = mybir.ActivationFunctionType
    AX = mybir.AxisListType

    B, C, T = x.shape
    NBLK = table.shape[1]
    POOL_BLOCKS, G, BLOCK, HD = k_blocks.shape
    H = wq.shape[0] // HD
    HPG = H // G
    KVD = G * HD
    WINDOW = 128
    W = 11
    WP = 12
    KEYS = W * BLOCK
    GB = 8
    ROWS = GB * W
    NG = B // GB
    TB = 128 // C
    NT = B // TB
    NS = (C + BLOCK - 2) // BLOCK + 1
    NW = NS * B
    HB = BLOCK // 2
    HK = HB * W
    NA, RANK = a3.shape[0], a3.shape[1]
    SCALE = 256.0 ** -0.5
    EPS = 1e-6
    SKIP = 16384.0
    DROP = 1048576.0
    NEG = -1e30
    HALF = HD // 2

    x_t = x.rearrange("(n b) c t -> n (b c) t", b=TB)
    out_t = out.rearrange("(n b) c t -> n (b c) t", b=TB)
    k_old = k_blocks.rearrange("n g o d -> n (g o d)")
    v_old = v_blocks.rearrange("n g o d -> n (g o d)")

    q_d = nc.dram_tensor("q_spill", [NT, 128, T], f32, kind="Internal").ap()
    v_d = nc.dram_tensor("values_by_group", [NG, ROWS * BLOCK, KVD], f32, kind="Internal").ap()
    x1_d = nc.dram_tensor("x1_spill", [NT, 128, T], f32, kind="Internal").ap()
    w0_d = nc.dram_tensor("w0_picked", [B, C * C], f32, kind="Internal").ap()
    w2_d = nc.dram_tensor("w2_picked", [B, C * C], f32, kind="Internal").ap()
    new_d = nc.dram_tensor("written_blocks", [NW * BLOCK, 2 * KVD], f32, kind="Internal").ap()
    new_blocks = new_d.rearrange("(n o) c -> n (o c)", o=BLOCK)
    new_rows = new_d.rearrange("(s b o) c -> s b (o c)", b=B, o=BLOCK)

    ctx = ExitStack()
    with ctx:
        def sb(name, shape, dt=f32):
            return ctx.enter_context(nc.sbuf_tensor(name, shape, dt))

        def sem(name):
            return ctx.enter_context(nc.semaphore(name))

        room = sb("blocks_room", [128, 4 * BLOCK * ROWS])
        turned = room[:, 0:2 * BLOCK * ROWS].rearrange("p (i f w o) -> p i f w o", i=2, o=BLOCK, w=W)
        kT = [turned[:, i] for i in (0, 1)]
        vg_at = 2 * BLOCK * ROWS
        qs = [room[:, vg_at + GB * 2 * KVD + T * i:vg_at + GB * 2 * KVD + T * i + T] for i in range(2)]
        proom = sb("p_room", [128, 4 * HPG * KEYS])
        probs = proom[:, :].rearrange("p (i h k) -> p i h k", i=4, h=HPG)
        pex, pn = [probs[:, i] for i in (0, 1)], [probs[:, i] for i in (2, 3)]
        troom = sb("pT_room", [128, 2 * 2 * HPG * 128])
        pT = [troom[0:HK, 512 * i:512 * i + 512].rearrange("p (c h t) -> p c h t", c=2, h=HPG) for i in range(2)]
        vroom = sb("v_room", [128, GB * 2 * KVD])
        vg = [half[0:HK, :].rearrange("p (f c d) -> p f c d", f=GB, c=2)
              for half in (room[:, vg_at:vg_at + GB * 2 * KVD], vroom)]
        wnat = room[:, 0:20 * 128].rearrange("p (i d) -> p i d", i=20)
        same = room[:, 20 * 128:20 * 128 + NS * NW].rearrange("p (s w) -> p s w", s=NS)
        later_at = 20 * 128 + NS * NW
        later_or_same = room[:, later_at:later_at + (2 * NS - 1) * 128].rearrange("p (s b) -> p s b", b=128)
        pick_at = later_at + (2 * NS - 1) * 128
        wpick = [room[:, pick_at:pick_at + C * C], proom[:, 0:C * C]]
        kv = room[:, 0:8 * 2 * KVD].rearrange("p (u c) -> p u c", u=8)
        x1s = [vroom[:, T * u:T * u + T] for u in range(4)]
        q1s = [vroom[:, T * u:T * u + T] for u in range(4, 8)]
        xT = [troom[:, T * i:T * i + T].rearrange("p (c t) -> p c t", c=2) for i in range(2)]

        eroom = sb("end_room", [128, 5 * NT * HALF])
        ang = eroom[:, 0:NT * HALF].rearrange("p (n i) -> p n i", i=HALF)
        turns = eroom[:, NT * HALF:3 * NT * HALF].rearrange("p (j n i) -> p j n i", j=2, i=HALF)
        trig = eroom[:, 3 * NT * HALF:5 * NT * HALF].rearrange("p (j n i) -> p j n i", j=2, i=HALF)
        x2s, x4s = [[eroom[:, T * i:T * i + T] for i in (j, j + 1)] for j in (0, 2)]
        x3T = [eroom[:, T * i:T * i + T].rearrange("p (c t) -> p c t", c=2) for i in (4, 5)]
        oT = [eroom[:, T * i:T * i + T].rearrange("p (h f t) -> p h f t", h=HPG, f=TB) for i in (6, 7)]
        xam = [eroom[:, T * 8 + 128 * i:T * 8 + 128 * i + 128] for i in range(2)]

        zcol = sb("zcol", [128, 1])
        ident = sb("ident", [128, 128])
        ones = sb("ones", [128, 128])
        iota_i = sb("iota_i", [128, NW], i32)
        iota = sb("iota", [128, NW])
        key_i = sb("key_i", [128, KEYS], i32)
        keypos = sb("keypos", [128, KEYS])
        part_i = sb("part_i", [128, 1], i32)
        part = sb("part", [128, 6])
        part_m = sb("part_m", [128, 6], i32)
        in_tile = sb("in_tile", [128, TB])
        of_tile = sb("of_tile", [128, NT])
        in_group = sb("in_group", [128, GB])
        of_group = sb("of_group", [128, NG])
        mask_sel = sb("mask_sel", [128, TB, 128], bf16)
        halfpow = sb("halfpow", [128, H])
        inv = sb("inv", [128, HALF])

        kvlen_i = sb("kvlen_i", [128, 1], i32)
        cond_i = sb("cond_i", [128, 1], i32)
        subj_i = sb("subj_i", [128, 1], i32)
        adapt_i = sb("adapt_i", [128, 1], i32)
        table_i = sb("table_i", [128, NBLK], i32)
        tab = sb("tab", [128, NBLK])
        ci = sb("ci", [128, 8], i32)
        cf = sb("cf", [128, 8])
        slots = sb("slots", [128, NS + WP])
        blk = sb("blk", [128, NS + WP])
        pick = sb("pick", [128, NBLK])
        diag = sb("diag", [128, NS, 128])
        wrow = sb("wrow", [128, NW])
        valid = sb("valid", [128, NS, BLOCK + 1])
        vlow = sb("vlow", [128, NS, BLOCK])
        vtmp = sb("vtmp", [128, NS, BLOCK])
        dest = sb("dest", [128, NS * BLOCK])
        dest2 = sb("dest2", [128, NS * BLOCK])
        number = sb("number", [128, NS])
        owner = sb("owner", [128, NS])
        own = sb("own", [128, NS])
        crow = sb("crow", [128, NW])
        rowid = sb("rowid", [128, NS * BLOCK])
        shift = sb("shift", [128, BLOCK])
        tok = sb("tok", [128, 4, C])
        base_idx = sb("base_idx", [128, 2], i32)
        hits = sb("hits", [128, WP])
        hjunk = sb("hjunk", [128, NW])
        rd = sb("rd", [128, 2, W])
        rtmp = sb("rtmp", [128, 2, W])
        g_idx = sb("g_idx", [128, 4], i32)
        spread = sb("spread", [128, 3, 128])
        gspread = sb("gspread", [128, 2, GB, W])
        tok_idx = sb("tok_idx", [128, NT], i32)
        tok_pos = sb("tok_pos", [128, NT])
        tok_hi = sb("tok_hi", [128, NT])
        tok_lo = sb("tok_lo", [128, NT])
        rd_idx = sb("rd_idx", [128, 2, NG], i32)
        adiag = sb("adiag", [128, 128])
        amask = sb("amask", [128, B])
        scal_col = sb("scal_col", [128, 1])

        gain = sb("gain", [128, 2, HD])
        ngain = sb("ngain", [128, 2, HD])
        ctab = sb("ctab", [128, 2, NT, HD])
        stab = sb("stab", [128, 2, NT, HD])

        wkvT = sb("wkvT", [128, 2, 2 * KVD])
        wqT = sb("wqT", [128, 2, T])
        woT = sb("woT", [128, HPG, T])
        w3T = sb("w3T", [128, 2, T])
        abT = sb("abT", [128, 2, T])
        bd = sb("bd", [128, NT, 128])

        old = [sb(f"old{i}", [128, 2, G * BLOCK * HD]) for i in range(2)]
        new = [sb(f"new{i}", [128, BLOCK, 2, KVD]) for i in range(2)]

        xin = [sb(f"xin{i}", [128, T]) for i in range(4)]
        kv_idx = sb("kv_idx", [128, 8], i32)
        rp = sb("rp", [128, 5, T])
        rms = sb("rms", [128, 2, 3, H])
        qr = [sb(f"qr{i}", [128, T]) for i in range(2)]
        qbd = [sb(f"qbd{i}", [128, GB, HPG, 128]) for i in range(2)]
        pen_hi = sb("pen_hi", [128, KEYS])
        pen = [sb(f"pen{i}", [128, KEYS], bf16) for i in range(2)]
        nmax = sb("nmax", [128, 4, HPG])
        rsum = sb("rsum", [128, 4, HPG])
        rrec = sb("rrec", [128, 4, HPG])

        ps = [ctx.enter_context(nc.psum_tensor(f"bank{i}", [128, 512], f32)) for i in range(8)]
        ps_s, ps_p, ps_o, ps_m = ps[0:2], [ps[2], ps[4]], ps[5], [ps[6], ps[7], ps[3]]

        s_len, s_tab, s_cond, s_subj, s_adapt = (sem(n) for n in ("len_in", "table_in", "cond_in", "subj_in", "adapt_in"))
        s_gain, s_scal = sem("gain_in"), sem("scal_in")
        s_wk, s_wq, s_wo, s_w3, s_ab = (sem(n) for n in ("wkv_in", "wq_in", "wo_in", "w3_in", "ab_in"))
        s_pick = [sem("w0_picked_in"), sem("w2_picked_in")]
        s_pickw = [sem("w0_picked_out"), sem("w2_picked_out")]
        s_bd = [sem("bd0_in"), sem("bd2_in")]
        s_xin = [sem(f"x_in{i}") for i in range(4)]
        s_q = [sem(f"q_in{i}") for i in range(2)]
        s_vst = [sem(f"values_out{i}") for i in range(2)]
        s_vin = [sem(f"values_in{i}") for i in range(2)]
        s_spill = [sem(f"x1_out{i}") for i in range(4)]
        s_x1 = [sem(f"x1_in{i}") for i in range(4)]
        s_bg = [sem(f"base_in{i}") for i in range(2)]
        s_bs = [sem(f"base_out{i}") for i in range(2)]
        s_scat = [sem(f"tokens_out{i}") for i in range(8)]
        s_gold = [sem(f"old_in{i}") for i in range(2)]
        s_gnew = [sem(f"new_in{i}") for i in range(2)]
        s_out = [sem(f"out_done{i}") for i in range(2)]
        s_cchain = sem("constant_made")
        s_dset = sem("setup_op")
        s_wrow, s_later, s_relay, s_reads = (sem(n) for n in ("wrow_ps", "later_ps", "relay_ps", "reads_ps"))
        s_wt, s_wtc, s_trig, s_perm, s_w3i = (sem(n) for n in ("weights_turned", "weights_copied", "trig_ready", "base_permuted", "w3_plus_i"))
        s_zero, s_zfill, s_crow = sem("old_zeroed"), sem("second_blocks_zeroed"), sem("crow_ps")
        s_order = [sem(f"old_reordered{i}") for i in range(2)]
        s_gix = [sem("old_index_staged"), sem("new_index_staged")]
        s_look, s_passed, s_sp_passed = sem("slot_looked_up"), sem("pool_passed"), sem("sync_passed")
        s_l0, s_xtc, s_tr1, s_kvp, s_kvc, s_qc, s_x1c = (
            sem(n) for n in ("l0_done", "x1T_copied", "x1_turned", "kvq_projected", "kv_copied", "q_copied", "x1_copied"))
        s_kr, s_ms, s_rstd, s_rope = (sem(n) for n in ("k_roped", "ms_ready", "rstd_ready", "rope_op"))
        s_tix = sem("token_index_staged")
        s_qk, s_max, s_exp, s_rec, s_pn, s_pt, s_ptc, s_pv = (
            sem(n) for n in ("qk_done", "max_done", "exp_done", "rec_done", "p_normal", "p_turned", "pT_copied", "pv_done"))
        s_oc, s_pen1, s_pen, s_qrd = (sem(n) for n in ("oT_copied", "pen_half", "pen_ready", "q_roped"))
        s_full = [sem("prep_full0"), sem("prep_full1"), sem("end_full")]
        s_empty = [sem("prep_empty0"), sem("prep_empty1"), sem("end_empty")]

        block = ctx.enter_context(nc.Block())
        mark = {}
        cmark_iota, cmark_bd, cmark_masks = 5, 7, 10
        cmark_all = cmark_masks + 4 + HALF
        cmark_qbd = cmark_all + 2

        PREP = {0: [("k0", None)], 1: [("k1", None)], 2: [("k2", None)], 3: [("qT", 0)], 4: [("k3", None)], 7: [("qT", 1)]}
        FIRST_PREP = {3: [("qT", 0)], 4: [("qT", 1)], 5: [("k0", None)], 6: [("k1", None)],
                      7: [("k2", None), ("k3", None)]}
        ROTATE, FIRST_ROTATE = {0: 0, 4: 1}, {0: 0, 1: 1}
        FIN = {3: ("x2", 7), 0: ("x3", 8), 1: ("xa", 9), 2: ("x4", 10)}
        LAST = 4 * (NT - 1) + 10

        def fin_step(k):
            kind, lag = FIN[k % 4]
            n = (k - lag) // 4
            return [(kind, n)] if 0 <= n < NT else []

        def prep_steps(k):
            grp, table = k // 8 + 1, PREP if k >= 0 else FIRST_PREP
            if not 0 <= grp < NG:
                return []
            return [(kind, grp if u is None else 2 * grp + u) for kind, u in table.get(k % 8, [])]

        def rotated_tiles(k):
            grp, table = k // 8 + 1, ROTATE if k >= 0 else FIRST_ROTATE
            return [2 * grp + table[k % 8]] if 0 <= grp < NG and k % 8 in table else []

        place = {}
        served = [0, 0, 0]
        for k in range(-8, LAST + 1):
            for step in prep_steps(k):
                bank = (served[0] + served[1]) % 2
                place[step] = (bank, served[bank])
                served[bank] += 1
            for step in fin_step(k):
                place[step] = (2, served[2])
                served[2] += 1
        PER_LOOP = [6, 6, 16]
        LOOPS = B // 16 - 2

        EARLY = 3
        ROPE = 6

        def misc(step, it):
            bank, before = place[step]
            return bank, before + PER_LOOP[bank] * it

        def await_bank(eng, step, it):
            bank, before = misc(step, it)
            if not isinstance(before, int) or before > 0:
                eng.wait_ge(s_empty[bank], before)

        def await_step(eng, step, it):
            bank, before = misc(step, it)
            eng.wait_ge(s_full[bank], before + 1)

        def await_copied(eng, step, it):
            bank, before = misc(step, it)
            eng.wait_ge(s_empty[bank], before + 1)

        def await_keys(eng, grp, it):
            last = {place[(f"k{i}", grp)][0]: (f"k{i}", grp) for i in range(4)}
            for step in last.values():
                await_copied(eng, step, it)

        def reordered_piece(i, which, piece):
            at = slice(4 * piece, 4 * piece + 4)
            return (new[i][0:ROWS, at, which, :].rearrange("p o (g d) -> p g o d", g=G),
                    old[i][0:ROWS, which, :].rearrange("p (g o d) -> p g o d", g=G, o=BLOCK)[:, :, at, :])

        def run_slots(eng, slot):
            for k in range(-8, 8):
                slot(0, k)
            with eng.Fori(0, LOOPS) as it:
                for k in range(8, 24):
                    slot(it, k)
            for k in range(8 + 16 * LOOPS, LAST + 1):
                slot(0, k)

        @block.vector
        def _(dve):
            v = nc.vector
            done = [0]

            def put(ins):
                done[0] += 1
                ins.then_inc(s_dset, 1)

            def settled():
                dve.wait_ge(s_dset, done[0])

            dve.wait_ge(s_len, 16)
            dve.wait_ge(s_cchain, cmark_iota)
            put(v.tensor_copy(iota[:, :], iota_i[:, :]))
            put(v.tensor_scalar(ci[:, 0:1], kvlen_i[:, :], 4, None, ALU.arith_shift_right))
            put(v.tensor_scalar(ci[:, 1:2], kvlen_i[:, :], BLOCK - 1, None, ALU.bitwise_and))
            put(v.tensor_scalar(ci[:, 2:3], kvlen_i[:, :], float(1 - WINDOW), 0.0, ALU.add, ALU.max))
            put(v.tensor_copy(cf[:, 4:5], kvlen_i[:, :]))
            put(v.tensor_scalar(part_m[:, 1:2], part_i[:, :], TB - 1, None, ALU.bitwise_and))
            put(v.tensor_scalar(part_m[:, 2:3], part_i[:, :], 2, None, ALU.arith_shift_right))
            put(v.tensor_scalar(part_m[:, 3:4], part_i[:, :], GB - 1, None, ALU.bitwise_and))
            put(v.tensor_scalar(part_m[:, 4:5], part_i[:, :], 3, None, ALU.arith_shift_right))
            put(v.tensor_scalar(part_m[:, 5:6], part_i[:, :], 4, None, ALU.arith_shift_right))
            settled()
            put(v.tensor_scalar(ci[:, 3:4], ci[:, 2:3], 4, None, ALU.arith_shift_right))
            put(v.tensor_copy(cf[:, 0:2], ci[:, 0:2]))
            put(v.tensor_copy(part[:, 0:1], part_i[:, :]))
            put(v.tensor_copy(part[:, 1:6], part_m[:, 1:6]))
            settled()
            put(v.tensor_scalar(cf[:, 3:4], ci[:, 3:4], float(NBLK - W), None, ALU.min))
            put(v.tensor_scalar(in_tile[:, :], iota[:, 0:TB], part[:, 1:2], None, ALU.is_equal))
            put(v.tensor_scalar(of_tile[:, :], iota[:, 0:NT], part[:, 2:3], None, ALU.is_equal))
            put(v.tensor_scalar(in_group[:, :], iota[:, 0:GB], part[:, 3:4], None, ALU.is_equal))
            put(v.tensor_scalar(of_group[:, :], iota[:, 0:NG], part[:, 4:5], None, ALU.is_equal))
            settled()
            put(v.scalar_tensor_tensor(cf[:, 5:6], cf[:, 3:4], -float(BLOCK), cf[:, 4:5], ALU.mult, ALU.add))
            put(v.tensor_scalar(slots[:, 0:NS], iota[:, 0:NS], cf[:, 0:1], None, ALU.add))
            put(v.tensor_scalar(slots[:, NS:], iota[:, 0:WP], cf[:, 3:4], None, ALU.add))
            dve.wait_ge(s_tab, 16)
            put(v.tensor_copy(tab[:, :], table_i[:, :]))
            settled()
            for j in range(NS):
                put(v.scalar_tensor_tensor(pick[:, :], iota[:, 0:NBLK], slots[:, j:j + 1], tab[:, :], ALU.is_equal, ALU.mult,
                                           accum_out=blk[:, j:j + 1]))
                settled()
            put(v.tensor_scalar(cf[:, 6:7], cf[:, 1:2], 0.0, None, ALU.is_gt))
            settled()
            put(v.scalar_tensor_tensor(cf[:, 7:8], blk[:, NS - 1:NS], 1.0, cf[:, 6:7], ALU.add, ALU.mult))
            settled()
            put(v.tensor_scalar(blk[:, NS - 1:NS], cf[:, 7:8], -1.0, None, ALU.add))
            settled()
            for s in range(NS):
                put(v.tensor_scalar(diag[:, s, :], ident[:, :], blk[:, s:s + 1], None, ALU.mult))
            mark["diag"] = done[0]
            for i, s in enumerate((0, NS - 1)):
                put(v.tensor_scalar(base_idx[:, i:i + 1], blk[:, s:s + 1], 0.0, None, ALU.max))
            mark["base"] = done[0]
            for s in range(NS):
                put(v.tensor_scalar(vtmp[:, s, :], iota[:, BLOCK * s:BLOCK * s + BLOCK], cf[:, 1:2], None, ALU.subtract))
                put(v.tensor_scalar(number[:, s:s + 1], part[:, 0:1], float(B * s + 1), None, ALU.add))
            settled()
            for s in range(NS):
                put(v.tensor_scalar(valid[:, s, 0:BLOCK], vtmp[:, s, :], 0.0, None, ALU.is_ge))
                put(v.tensor_scalar(valid[:, s, BLOCK:BLOCK + 1], blk[:, s:s + 1], 0.0, None, ALU.is_ge))
            put(v.tensor_scalar(vlow[:, :, :], vtmp[:, :, :], float(C), None, ALU.is_lt))
            put(v.tensor_scalar(shift[:, :], iota[:, 0:BLOCK], cf[:, 1:2], None, ALU.is_equal))
            settled()
            for s in range(NS):
                put(v.tensor_tensor(valid[:, s, 0:BLOCK], valid[:, s, 0:BLOCK], vlow[:, s, :], ALU.mult))
            dve.wait_ge(s_wrow, 1)
            put(v.tensor_copy(wrow[:, :], ps[6][:, 0:NW]))
            dve.wait_ge(s_cchain, cmark_masks)
            settled()
            for s in range(NS):
                masks = later_or_same[:, NS - 1 - s:2 * NS - 1 - s, :].rearrange("p s b -> p (s b)")
                put(v.scalar_tensor_tensor(same[:, s, :], wrow[:, :], blk[:, s:s + 1], masks, ALU.is_equal, ALU.mult))
            mark["same"] = done[0]
            for i in range(2):
                dve.wait_ge(s_pick[i], 16)
                put(v.tensor_scalar(wpick[i][:, ::C + 1], wpick[i][:, ::C + 1], 1.0, None, ALU.add))
                mark[f"w{i}"] = done[0]
            put(v.tensor_scalar(tok[:, 2, :], iota[:, 0:C], cf[:, 4:5], None, ALU.add))
            put(v.tensor_scalar(tok[:, 3, :], iota[:, 0:C], cf[:, 5:6], None, ALU.add))
            dve.wait_ge(s_later, 1)
            later = ps[7][:, 0:NS * (BLOCK + 1)].rearrange("p (s c) -> p s c", s=NS)
            for s in range(NS):
                put(v.tensor_scalar(owner[:, s:s + 1], later[:, s, BLOCK:BLOCK + 1], 0.0, number[:, s:s + 1], ALU.is_equal, ALU.mult))
            settled()
            for s in range(NS):
                put(v.tensor_scalar(owner[:, s:s + 1], owner[:, s:s + 1], valid[:, s, BLOCK:BLOCK + 1], None, ALU.mult))
            settled()
            for s in range(NS):
                put(v.tensor_scalar(diag[:, s, :], ident[:, :], owner[:, s:s + 1], None, ALU.mult))
            mark["owner"] = done[0]
            for s in range(NS):
                put(v.tensor_scalar(dest[:, BLOCK * s:BLOCK * s + BLOCK], later[:, s, 0:BLOCK], 0.0, DROP, ALU.is_gt, ALU.mult))
            dve.wait_ge(s_crow, 1)
            put(v.tensor_copy(crow[:, :], ps[6][:, 0:NW]))
            settled()
            for s in range(NS):
                put(v.scalar_tensor_tensor(hjunk[:, :], wrow[:, :], blk[:, s:s + 1], crow[:, :], ALU.is_equal, ALU.mult,
                                           accum_out=own[:, s:s + 1]))
                settled()
            put(v.tensor_scalar(own[:, :], own[:, :], -1.0, float(BLOCK), ALU.add, ALU.mult))
            settled()
            for s in range(NS):
                put(v.tensor_scalar(rowid[:, BLOCK * s:BLOCK * s + BLOCK], iota[:, 0:BLOCK], own[:, s:s + 1], None, ALU.add))
            settled()
            put(v.tensor_tensor(dest2[:, :], dest[:, :], rowid[:, :], ALU.add))
            settled()
            put(v.tensor_scalar(tok[:, 0, :], dest2[:, 0:C], shift[:, 0:1], None, ALU.mult))
            for j in range(1, BLOCK):
                settled()
                put(v.scalar_tensor_tensor(tok[:, j % 2, :], dest2[:, j:j + C], shift[:, j:j + 1], tok[:, 1 - j % 2, :], ALU.mult, ALU.add))
            settled()
            for i, src in enumerate(((BLOCK - 1) % 2, 2, 3)):
                for f in range(TB):
                    put(v.tensor_scalar(spread[:, i, C * f:C * f + C], tok[:, src, :], in_tile[:, f:f + 1], None, ALU.mult))
            mark["spread"] = done[0]
            dve.wait_ge(s_relay, 1)
            put(v.tensor_copy(tok_idx[:, :], ps[6][:, 0:NT]))
            mark["tokens"] = done[0]
            put(v.tensor_copy(tok_pos[:, :], ps[6][:, NT:2 * NT]))
            put(v.tensor_copy(tok_hi[:, :], ps[6][:, 2 * NT:3 * NT]))
            put(v.tensor_scalar(tok_lo[:, :], ps[6][:, 2 * NT:3 * NT], -float(WINDOW), None, ALU.add))
            mark["relayed"] = done[0]
            BIG = 12582912.0
            TWO_PI = 2.0 * math.pi
            C1 = 6.28125
            C2 = math.floor((TWO_PI - C1) * 2 ** 21) / 2 ** 21
            C3 = TWO_PI - C1 - C2
            PI = 3.1415925
            flat = "p n i -> p (n i)"
            dve.wait_ge(s_cchain, cmark_all)
            settled()
            for i in range(HALF):
                put(v.tensor_scalar(ang[:, :, i], tok_pos[:, :], inv[:, i:i + 1], None, ALU.mult))
            settled()
            put(v.tensor_scalar(turns[:, 0, :, :], ang[:, :, :], 1.0 / TWO_PI, 0.25, ALU.mult, ALU.add))
            put(v.tensor_scalar(turns[:, 1, :, :], ang[:, :, :], 1.0 / TWO_PI, None, ALU.mult))
            settled()
            put(v.tensor_scalar(turns[:, :, :, :], turns[:, :, :, :], BIG, None, ALU.add))
            settled()
            put(v.tensor_scalar(turns[:, :, :, :], turns[:, :, :, :], -BIG, None, ALU.add))
            for part_of_turn in (C1, C2, C3):
                settled()
                for j in range(2):
                    before = ang[:, :, :] if part_of_turn == C1 else trig[:, j, :, :]
                    put(v.scalar_tensor_tensor(trig[:, j, :, :].rearrange(flat), turns[:, j, :, :].rearrange(flat), -part_of_turn,
                                               before.rearrange(flat), ALU.mult, ALU.add))
            settled()
            put(v.tensor_scalar(trig[:, 0, :, :], trig[:, 0, :, :], math.pi / 2, None, ALU.add))
            settled()
            put(v.tensor_scalar(trig[:, :, :, :], trig[:, :, :, :], PI, -PI, ALU.min, ALU.max))
            mark["angles"] = done[0]
            for i in range(2):
                dve.wait_ge(s_bg[i], 32)
                v.tensor_copy(new[i][:, :, 0, :].rearrange("p o (g d) -> p g o d", g=G),
                              old[i][:, 0, :].rearrange("p (g o d) -> p g o d", g=G, o=BLOCK)).then_inc(s_perm, 1)
            dve.wait_ge(s_gain, 32)
            put(v.tensor_scalar(gain[:, :, :], gain[:, :, :], 1.0, None, ALU.add))
            settled()
            put(v.tensor_scalar(ngain[:, :, :], gain[:, :, :], -1.0, None, ALU.mult))
            dve.wait_ge(s_trig, 1)
            settled()
            for which in (1, 0):
                for dst, of, by, lo in ((ctab[:, which, :, 0:HALF], 0, gain, 0), (ctab[:, which, :, HALF:], 0, gain, HALF),
                                        (stab[:, which, :, 0:HALF], 1, ngain, HALF), (stab[:, which, :, HALF:], 1, gain, 0)):
                    put(v.tensor_tensor(dst, trig[:, of, :, :], by[:, which, lo:lo + HALF].unsqueeze(1).broadcast_to([128, NT, HALF]),
                                        ALU.mult))
            settled()

            def rotate(src, cos_t, sin_t, index, i, parts=(0, 1)):
                outer, inner = src.shape[1:3]

                def shaped(ap):
                    return ap.rearrange("p (a h d) -> p a h d", a=outer, d=HD)

                def cut(ap, lo, hi):
                    return ap[:, :, :, lo:hi]

                def over_heads(ap, lo, hi):
                    one = ap[:, :, lo:hi].unsqueeze(2) if ap.shape[1] == outer else ap[:, :, lo:hi].unsqueeze(1)
                    return one.broadcast_to([128, outer, inner, hi - lo])

                first = ROPE * index
                if 0 in parts:
                    v.tensor_tensor(shaped(rp[:, 0, :]), src, src, ALU.mult).then_inc(s_rope, 1)
                    dve.wait_ge(s_rope, first + 1)
                    v.tensor_reduce(rms[:, i, 0, :], rp[:, 0, :].rearrange("p (h d) -> p h d", d=HD), AX.X, ALU.add).then_inc(s_rope, 1)
                    dve.wait_ge(s_rope, first + 2)
                    v.tensor_scalar(rms[:, i, 1, :], rms[:, i, 0, :], 1.0 / HD, EPS, ALU.mult, ALU.add).then_inc(s_ms, 1)
                    v.tensor_tensor(shaped(rp[:, 1, :]), src, over_heads(cos_t, 0, HD), ALU.mult).then_inc(s_rope, 1)
                if 1 in parts:
                    v.tensor_tensor(cut(shaped(rp[:, 2, :]), 0, HALF), cut(src, HALF, HD), over_heads(sin_t, 0, HALF), ALU.mult).then_inc(s_rope, 1)
                    v.tensor_tensor(cut(shaped(rp[:, 2, :]), HALF, HD), cut(src, 0, HALF), over_heads(sin_t, HALF, HD), ALU.mult).then_inc(s_rope, 1)
                    dve.wait_ge(s_rope, first + 5)
                    v.tensor_tensor(rp[:, 3 + i, :], rp[:, 1, :], rp[:, 2, :], ALU.add).then_inc(s_rope, 1)

            def scale_by_rstd(dst, dst_sem, index, i):
                outer, inner = dst.shape[1:3]
                dve.wait_ge(s_rope, ROPE * index + ROPE)
                dve.wait_ge(s_rstd, index + 1)
                per_head = rms[:, i, 2, :].rearrange("p (a h) -> p a h", a=outer).unsqueeze(3).broadcast_to([128, outer, inner, HD])
                v.tensor_tensor(dst, rp[:, 3 + i, :].rearrange("p (a h d) -> p a h d", a=outer, d=HD), per_head, ALU.mult).then_inc(dst_sem, 1)

            def look_up(j):
                v.scalar_tensor_tensor(pick[:, :], iota[:, 0:NBLK], slots[:, bass.ds(NS + j, 1)], tab[:, :], ALU.is_equal, ALU.mult,
                                       accum_out=blk[:, bass.ds(NS + j, 1)]).then_inc(s_look, 1)
                dve.wait_ge(s_look, 2 * j + 1)
                v.scalar_tensor_tensor(hjunk[:, :], wrow[:, :], blk[:, bass.ds(NS + j, 1)], crow[:, :], ALU.is_equal, ALU.mult,
                                       accum_out=hits[:, bass.ds(j, 1)]).then_inc(s_look, 1)
                dve.wait_ge(s_look, 2 * j + 2)

            def keys_of(p):
                return kv[:, 2 * (p % 4):2 * (p % 4) + 2, 0:KVD].rearrange("p a (h d) -> p a h d", d=HD)

            def rotate_keys(it, p):
                tile0 = 8 * it + 2 * p
                dve.wait_ge(s_kvc, tile0 + 2)
                rotate(keys_of(p), ctab[:, 1, bass.ds(tile0, 2), :], stab[:, 1, bass.ds(tile0, 2), :], 4 * it + p, p % 2)

            def four_pairs(it, looking, last=False):
                for p in range(4):
                    if not (last and p == 3):
                        rotate_keys(it, p + 1)
                    if looking:
                        for j in ((0, 1), (2,), (3, 4), (5,))[p]:
                            look_up(6 * it + j)
                    scale_by_rstd(keys_of(p), s_kr, 4 * it + p, p % 2)

            rotate_keys(0, 0)
            with dve.Fori(0, 2) as it:
                four_pairs(it, True)

            put(v.tensor_scalar(rtmp[:, 0, :], hits[:, 0:W], 0.0, SKIP, ALU.is_gt, ALU.mult))
            put(v.tensor_scalar(rtmp[:, 1, :], hits[:, 0:W], 0.0, SKIP, ALU.is_equal, ALU.mult))
            settled()
            put(v.tensor_tensor(rd[:, 0, :], rtmp[:, 0, :], blk[:, NS:NS + W], ALU.add))
            put(v.scalar_tensor_tensor(rd[:, 1, :], hits[:, 0:W], -1.0, rtmp[:, 1, :], ALU.add, ALU.add))
            settled()
            for j in range(2):
                for f in range(GB):
                    put(v.tensor_scalar(gspread[:, j, f, :], rd[:, j, :], in_group[:, f:f + 1], None, ALU.mult))
            dve.wait_ge(s_adapt, 16)
            put(v.tensor_copy(cf[:, 2:3], adapt_i[:, :]))
            settled()
            put(v.tensor_scalar(adiag[:, :], ident[:, :], cf[:, 2:3], None, ALU.mult))
            mark["reads"] = done[0]
            four_pairs(2, False)
            put(v.tensor_copy(keypos[:, :], key_i[:, :]))
            dve.wait_ge(s_scal, 16)
            dve.wait_ge(s_reads, 1)
            put(v.tensor_copy(rd_idx[0:ROWS, :, :].rearrange("p j n -> p (j n)"), ps[7][0:ROWS, 0:2 * NG]))
            mark["second"] = done[0]
            put(v.tensor_scalar(amask[:, :], ps[7][:, 128:128 + B], part[:, 5:6], scal_col[:, :], ALU.is_equal, ALU.mult))
            mark["amask"] = done[0]
            settled()
            four_pairs(3, False, last=True)

            def make_pen(n, n0):
                v.tensor_scalar(pen_hi[:, :], keypos[:, :], tok_hi[:, bass.ds(n, 1)], None, ALU.is_gt).then_inc(s_pen1, 1)
                dve.wait_ge(s_pen1, n + 1)
                v.scalar_tensor_tensor(pen[n0 % 2][:, :], keypos[:, :], tok_lo[:, bass.ds(n, 1)], pen_hi[:, :],
                                       ALU.is_le, ALU.add).then_inc(s_pen, 1)

            def rotate_queries(it, n, parts):
                at = 4 * it + n
                rotate(qs[n % 2][:, :].rearrange("p (g h d) -> p g h d", g=G, d=HD),
                       ctab[:, 0, bass.ds(at, 1), :], stab[:, 0, bass.ds(at, 1), :], NT // 2 + at, n % 2, parts)

            def slot(it, k):
                b = 16 * it + k
                if k == -8:
                    make_pen(0, 0)
                if 0 <= k < B:
                    dve.wait_ge(s_qk, b + 1)
                    v.tensor_reduce(nmax[:, k % 4, :], ps_s[k % 2][:, 0:HPG * KEYS].rearrange("p (h k) -> p h k", h=HPG),
                                    AX.X, ALU.max, negate=True).then_inc(s_max, 1)
                for kind, n in prep_steps(k) if k < 0 else prep_steps(k - 1) if k > 0 else []:
                    bank, _ = misc((kind, n), it)
                    if kind in ("k0", "k1", "k2", "k3"):
                        await_step(dve, (kind, n), it)
                        o = 4 * int(kind[1])
                        v.tensor_copy(kT[n % 2][:, :, :, o:o + 4].rearrange("p f w o -> p o f w"),
                                      ps_m[bank][:, 0:4 * ROWS].rearrange("p (o f w) -> p o f w", o=4, w=W)).then_inc(s_empty[bank], 1)
                for n in rotated_tiles(k - 2):
                    scale_by_rstd(qr[n % 2][:, :].rearrange("p (h g d) -> p g h d", g=G, d=HD), s_qrd, NT // 2 + 4 * it + n, n % 2)
                for n in rotated_tiles(k - 1):
                    rotate_queries(it, n, (1,))
                for n in rotated_tiles(k):
                    dve.wait_ge(s_q[n % 2], 16 * (2 * it + n // 2) + 16)
                    rotate_queries(it, n, (0,))
                    if k < 0:
                        dve.wait_ge(s_gold[n], 32)
                        for piece in range(4):
                            v.tensor_copy(*reordered_piece(n, 0, piece)).then_inc(s_order[n], 1)
                if 0 <= k < B - 4 and k % 4 == 2:
                    make_pen(4 * it + k // 4 + 1, k // 4 + 1)
                kk = k + EARLY
                if 0 <= k and kk // 8 + 2 < NG:
                    i = kk // 8 % 2
                    for piece in {6: (0,), 7: (1,), 0: (2, 3) if k > 0 else (0, 1, 2, 3)}.get(k % 8, ()):
                        if piece == 0:
                            dve.wait_ge(s_gold[i], 32 * (it + kk // 16 + 1) + 32)
                            await_keys(dve, kk // 8, it)
                            dve.wait_ge(s_vst[i], 16 * (it + kk // 16 + 1))
                        v.tensor_copy(*reordered_piece(i, 0, piece)).then_inc(s_order[i], 1)
                for kind, n in fin_step(k):
                    bank, _ = misc((kind, n), it)
                    if kind == "x2":
                        dve.wait_ge(s_x1[n % 4], 16 * (it + n // 4) + 16)
                        await_step(dve, (kind, n), it)
                        v.tensor_tensor(x2s[n % 2][:, :], ps_m[bank][:, 0:T], xin[n % 4][:, :], ALU.add).then_inc(s_empty[bank], 1)
                    if kind == "xa":
                        await_step(dve, (kind, n), it)
                        v.tensor_tensor(xam[n % 2][:, :].rearrange("p (f t) -> p f t", f=TB),
                                        ps_m[bank][:, 0:128].rearrange("p (f t) -> p f t", f=TB),
                                        amask[:, bass.ds(16 * it + 4 * n, TB)].unsqueeze(2).broadcast_to([128, TB, C]),
                                        ALU.mult).then_inc(s_empty[bank], 1)
                if 0 <= k < B:
                    dve.wait_ge(s_exp, b + 1)
                    v.reciprocal(rrec[:, k % 4, :], rsum[:, k % 4, :]).then_inc(s_rec, 1)
                    dve.wait_ge(s_rec, b + 1)
                    if k >= 2:
                        dve.wait_ge(s_pt, b - 1)
                    for h in range(HPG):
                        last = v.tensor_scalar(pn[k % 2][:, h, :], pex[k % 2][:, h, :], rrec[:, k % 4, h:h + 1], None, ALU.mult)
                    last.then_inc(s_pn, 1)

            run_slots(dve, slot)

        @block.gpsimd
        def _(pool):
            made = [0]

            def make(ins):
                made[0] += 1
                ins.then_inc(s_cchain, 1)

            def settled():
                pool.wait_ge(s_cchain, made[0])

            make(pool.memset(zcol[:, :], 0.0))
            make(pool.memset(ident[:, :], 0.0))
            make(pool.iota(iota_i[:, :], pattern=[[1, NW]], base=0, channel_multiplier=0))
            make(pool.iota(part_i[:, :], pattern=[[0, 1]], base=0, channel_multiplier=1))
            settled()
            make(pool.affine_select(out=ident[:, :], in_=ident[:, :], compare_op=ALU.not_equal, fill=1.0, base=0,
                                    pattern=[[-1, 128]], channel_multiplier=1))
            assert made[0] == cmark_iota
            for i, (s_idx, idx, w) in enumerate(((s_cond, cond_i, w0), (s_subj, subj_i, w2))):
                pool.wait_ge(s_idx, 16)
                pool.indirect_dma_start(out=wpick[i][:, :], out_offset=None, in_=w.rearrange("s c d -> s (c d)"),
                                        in_offset=bass.IndirectOffsetOnAxis(ap=idx[:, 0:1], axis=0),
                                        bounds_check=w.shape[0] - 1, oob_is_err=False).then_inc(s_pick[i], 16)
                if i == 0:
                    make(pool.memset(ones[:, :], 1.0))
                    make(pool.memset(bd[:, :, :], 0.0))
                    make(pool.memset(later_or_same[:, :, :], 1.0))
                    assert made[0] == cmark_bd + 1
            settled()
            make(pool.affine_select(out=later_or_same[:, 0:NS - 1, :], in_=later_or_same[:, 0:NS - 1, :], compare_op=ALU.is_ge,
                                    fill=0.0, base=0, pattern=[[0, NS - 1], [-1, 128]], channel_multiplier=1))
            make(pool.affine_select(out=later_or_same[:, NS - 1:, :], in_=later_or_same[:, NS - 1:, :], compare_op=ALU.is_gt,
                                    fill=0.0, base=0, pattern=[[0, NS], [-1, 128]], channel_multiplier=1))
            assert made[0] == cmark_masks
            make(pool.memset(mask_sel[:, :, :], 0.0))
            make(pool.memset(halfpow[:, :], -0.5))
            for i in range(HALF):
                make(pool.memset(inv[:, i:i + 1], 1.0 / 10000.0 ** (i / HALF)))
            make(pool.iota(key_i[:, :], pattern=[[1, KEYS]], base=0, channel_multiplier=0))
            settled()
            sel_v = mask_sel[:, :, :].rearrange("p f (g t) -> p f g t", g=G)
            make(pool.affine_select(out=sel_v, in_=sel_v, compare_op=ALU.not_equal, fill=NEG, base=0,
                                    pattern=[[-C, TB], [0, G], [-1, C]], channel_multiplier=1))
            assert made[0] == cmark_all

            pool.wait_ge(s_dset, mark["base"])
            pool.wait_ge(s_zero, 2)
            for i in range(2):
                for j, src in enumerate((k_old, v_old)):
                    pool.indirect_dma_start(out=old[i][:, j, :], out_offset=None, in_=src,
                                            in_offset=bass.IndirectOffsetOnAxis(ap=base_idx[:, i:i + 1], axis=0),
                                            bounds_check=POOL_BLOCKS - 1, oob_is_err=False).then_inc(s_bg[i], 16)
            pool.wait_ge(s_w3, 32)
            for r in range(2):
                at = wnat[:, 12 + 3 * r, :]
                pool.tensor_tensor(out=at, in0=at, in1=ident[:, :], op=ALU.add).then_inc(s_w3i, 1)
            for i in range(2):
                make(pool.memset(qbd[i][:, :, :, :], 0.0))
            assert made[0] == cmark_qbd
            def past_waits():
                pool.sem_inc(s_passed, 1)

            def rstd(index, i):
                pool.wait_ge(s_ms, index + 1)
                pool.tensor_tensor(out=rms[:, i, 2, :], in0=rms[:, i, 1, :], in1=halfpow[:, :], op=ALU.pow).then_inc(s_rstd, 1)

            def pair(it, p, last=False):
                tile0, u0, index = 8 * it + 2 * p, 2 * p, 4 * it + p
                for u in (u0, u0 + 1):
                    if not isinstance(it, int) or it > 0:
                        pool.wait_ge(s_scat[u], 16 * it)
                    past_waits()
                    pool.tensor_copy(kv_idx[:, u:u + 1], tok_idx[:, bass.ds(tile0 + (u - u0), 1)]).then_inc(s_tix, 1)
                if not last:
                    rstd(index + 1, (p + 1) % 2)
                pool.wait_ge(s_kr, index + 1)
                if isinstance(it, int) and index == 0:
                    pool.wait_ge(s_zfill, 32)
                    for i in range(2):
                        pool.wait_ge(s_bs[i], 16)
                pool.wait_ge(s_tix, tile0 + 2)
                past_waits()
                for u in (u0, u0 + 1):
                    pool.indirect_dma_start(out=new_d, out_offset=bass.IndirectOffsetOnAxis(ap=kv_idx[:, u:u + 1], axis=0),
                                            in_=kv[:, u, :], in_offset=None,
                                            bounds_check=NW * BLOCK - 1, oob_is_err=False).then_inc(s_scat[u], 16)

            def stage_index(i, j, g2):
                past_waits()
                pool.tensor_copy(g_idx[0:ROWS, 2 * i + j:2 * i + j + 1], rd_idx[0:ROWS, j, bass.ds(g2, 1)]).then_inc(s_gix[j], 1)

            def gather_old(i, g2):
                stage_index(i, 0, g2)
                pool.wait_ge(s_gix[0], g2 + 1)
                past_waits()
                for j, src in enumerate((k_old, v_old)):
                    pool.indirect_dma_start(out=old[i][0:ROWS, j, :], out_offset=None, in_=src,
                                            in_offset=bass.IndirectOffsetOnAxis(ap=g_idx[0:ROWS, 2 * i:2 * i + 1], axis=0),
                                            bounds_check=POOL_BLOCKS - 1, oob_is_err=False).then_inc(s_gold[i], 16)

            def gather_new(i, g2, reordered):
                stage_index(i, 1, g2)
                pool.wait_ge(s_gix[1], g2 + 1)
                pool.wait_ge(s_order[i], reordered)
                past_waits()
                pool.indirect_dma_start(out=new[i][0:ROWS, :, :, :].rearrange("p o k c -> p (o k c)"), out_offset=None, in_=new_blocks,
                                        in_offset=bass.IndirectOffsetOnAxis(ap=g_idx[0:ROWS, 2 * i + 1:2 * i + 2], axis=0),
                                        bounds_check=NW - 1, oob_is_err=False).then_inc(s_gnew[i], 16)

            def reorder_values(i, piece):
                pool.tensor_copy(*reordered_piece(i, 1, piece)).then_inc(s_order[i], 1)

            pool.wait_ge(s_dset, mark["tokens"])
            rstd(0, 0)
            for p in range(4):
                pair(0, p)
            with pool.Fori(1, NT // 8 - 1) as it:
                for p in range(4):
                    pair(it, p)
            pair(NT // 8 - 1, 0)
            pool.wait_ge(s_dset, mark["second"])
            for i in range(2):
                gather_old(i, i)
            for p in range(1, 4):
                pair(NT // 8 - 1, p, last=(p == 3))
            for n in range(2):
                rstd(NT // 2 + n, n)
            for u in range(8):
                pool.wait_ge(s_scat[u], 16 * (NT // 8))
            for i in range(2):
                gather_new(i, i, 8)
            gather_old(0, 2)

            def slot(it, k):
                b = 16 * it + k
                if k >= 0:
                    for n in rotated_tiles(k):
                        rstd(NT // 2 + 4 * it + n, n % 2)
                kk = k + EARLY
                if 0 <= kk and kk // 8 + 2 < NG:
                    i, j = (kk // 8) % 2, kk % 8
                    fills = it + kk // 16 + 1
                    if j == 0:
                        pool.wait_ge(s_gold[i], 32 * fills + 32)
                        await_keys(pool, kk // 8, it)
                        pool.wait_ge(s_vst[i], 16 * fills)
                    if j < 4:
                        past_waits()
                        reorder_values(i, j)
                    if j == 4:
                        pool.wait_ge(s_gnew[i], 16 * fills)
                        gather_new(i, 2 * it + kk // 8 + 2, 8 * fills + 8)
                    if j == 5 and kk // 8 + 3 < NG:
                        gather_old(1 - i, 2 * it + kk // 8 + 3)

            run_slots(pool, slot)

        @block.sync
        def _(sp):
            column = "(b u) -> b u"
            sp.dma_start(kvlen_i[:, :], kvlen.rearrange(column, u=1)).then_inc(s_len, 16)
            sp.dma_start(cond_i[:, :], cond.rearrange(column, u=1)).then_inc(s_cond, 16)
            sp.dma_start(table_i[:, :], table).then_inc(s_tab, 16)
            sp.dma_start(subj_i[:, :], subj.rearrange(column, u=1)).then_inc(s_subj, 16)
            for u in range(4):
                sp.dma_start(xin[u][:, :], x_t[u, :, :]).then_inc(s_xin[u], 16)
            sp.wait_ge(s_cchain, cmark_bd)
            for i, wd in enumerate((w0_d, w2_d)):
                sp.wait_ge(s_dset, mark[f"w{i}"])
                sp.dma_start(wd, wpick[i][:, :]).then_inc(s_pickw[i], 16)
                if i == 0:
                    sp.wait_ge(s_pickw[0], 16)
                    for f in range(TB):
                        sp.dma_start(bd[C * f:C * f + C, :, C * f:C * f + C],
                                     w0_d.rearrange("(n f) (c d) -> f c n d", f=TB, d=C)[f]).then_inc(s_bd[0], 16)

            sp.wait_ge(s_cchain, cmark_qbd)
            for j in range(2):
                sp.dma_start(new_rows[1][:, 2048 * j:2048 * j + 2048], qbd[j][:, :, :, :].rearrange("p f h t -> p (f h t)")).then_inc(s_zfill, 16)
            sp.wait_ge(s_perm, 4)
            for i, s in enumerate((0, NS - 1)):
                sp.dma_start(new_rows[s], new[i][:, :, :, :].rearrange("p o k c -> p (o k c)")).then_inc(s_bs[i], 16)

            def past_waits():
                sp.sem_inc(s_sp_passed, 1)

            def load_and_spill(n, u, load):
                if load:
                    sp.wait_ge(s_l0, n + 1)
                    sp.dma_start(xin[u][:, :], x_t[n + 4, :, :]).then_inc(s_xin[u], 16)
                sp.wait_ge(s_x1c, n + 1)
                sp.dma_start(x1_d[n, :, :], x1s[u][:, :]).then_inc(s_spill[u], 16)
                sp.wait_ge(s_qc, n + 1)
                past_waits()
                sp.dma_start(q_d[n, :, :], q1s[u][:, :]).then_inc(s_spill[u], 16)

            with sp.Fori(0, NT // 4 - 1) as it:
                for u in range(4):
                    load_and_spill(4 * it + u, u, True)
            for u in range(4):
                load_and_spill(NT - 4 + u, u, False)
            for u in range(2):
                sp.sem_inc(s_out[u], 16)
            sp.wait_ge(s_pickw[1], 16)
            for u in range(4):
                sp.wait_ge(s_spill[u], 32 * (NT // 4))
            for i in range(2):
                sp.dma_start(qs[i][:, :], q_d[i, :, :]).then_inc(s_q[i], 16)
            for u in range(4):
                sp.dma_start(xin[u][:, :], x1_d[u, :, :]).then_inc(s_x1[u], 16)
            for f in range(TB):
                sp.dma_start(bd[C * f:C * f + C, :, C * f:C * f + C],
                             w2_d.rearrange("(n f) (c d) -> f c n d", f=TB, d=C)[f]).then_inc(s_bd[1], 16)

            def slot(it, k):
                grp = k // 8 + 1
                for n in rotated_tiles(k - 2):
                    if n + 2 < NT:
                        sp.wait_ge(s_rope, ROPE * (NT // 2 + 4 * it + n) + ROPE)
                        past_waits()
                        sp.dma_start(qs[n % 2][:, :], q_d[4 * it + n + 2, :, :]).then_inc(s_q[n % 2], 16)
                if grp < NG:
                    i, fills = grp % 2, it + grp // 2
                    if k % 8 == 0:
                        sp.wait_ge(s_gnew[i], 16 * fills + 16)
                        past_waits()
                        sp.dma_start(v_d[2 * it + grp, :, :].rearrange("(r o) c -> r o c", o=BLOCK), new[i][0:ROWS, :, 1, :]).then_inc(s_vst[i], 16)
                    if k % 8 == 3:
                        sp.wait_ge(s_vst[i], 16 * fills + 16)
                        if grp >= 2:
                            past_waits()
                            sp.wait_ge(s_pv, 16 * it + GB * (grp - 1))
                        past_waits()
                        sp.dma_start(vg[i][:, :, :, :].rearrange("p f c d -> p (f c) d"),
                                     v_d[2 * it + grp, :, :].rearrange("(a p) d -> p a d", p=HK)).then_inc(s_vin[i], 16)
                for kind, n in fin_step(k):
                    if kind == "x2" and n + 4 < NT:
                        await_copied(sp, (kind, n), it)
                        sp.dma_start(xin[n % 4][:, :], x1_d[4 * it + n + 4, :, :]).then_inc(s_x1[n % 4], 16)
                    if kind == "x4":
                        await_copied(sp, (kind, n), it)
                        sp.dma_start(out_t[4 * it + n, :, :], x4s[n % 2][:, :]).then_inc(s_out[n % 2], 16)

            run_slots(sp, slot)
            for u in range(2):
                sp.wait_ge(s_out[u], 16 * (NT // 2) + 16)

        @block.scalar
        def _(act):
            a = nc.scalar
            halves = "o (c d) -> o c d"
            act.wait_ge(s_cchain, 1)
            for i in range(2):
                a.activation(old[i][:, :, :].rearrange("p k c -> p (k c)"), zcol[:, :].broadcast_to([128, 2 * G * BLOCK * HD]), ACT.Copy).then_inc(s_zero, 1)
            act.dma_start(wnat[:, 0:2, :], wk.rearrange(halves, c=2)).then_inc(s_wk, 16)
            act.dma_start(wnat[:, 2:4, :], wv.rearrange(halves, c=2)).then_inc(s_wk, 16)
            act.dma_start(adapt_i[:, :], adapt.rearrange("(b u) -> b u", u=1)).then_inc(s_adapt, 16)
            act.dma_start(gain[:, 0, :], qscale.partition_broadcast(128)).then_inc(s_gain, 16)
            act.dma_start(gain[:, 1, :], kscale.partition_broadcast(128)).then_inc(s_gain, 16)
            act.dma_start(scal_col[:, :], s3.rearrange("(a u) -> a u", u=1).broadcast_to([NA, RANK])).then_inc(s_scal, 16)
            for at, w, s_w in ((4, wq, s_wq), (8, wo, s_wo), (12, w3, s_w3)):
                for r in range(2):
                    rows = w[128 * r:128 * r + 128, :]
                    if w is wo:
                        for h in range(HPG):
                            act.dma_start(wnat[:, at + 2 * r + h, :].rearrange("p (g d) -> p g d", g=G),
                                          rows.rearrange("o (g h d) -> o g h d", g=G, h=HPG)[:, :, h, :]).then_inc(s_w, 16)
                    else:
                        act.dma_start(wnat[:, at + 2 * r:at + 2 * r + 2, :], rows.rearrange(halves, c=2)).then_inc(s_w, 16)
            act.dma_start(wnat[:, 16:18, :], a3.rearrange("a r (c d) -> (a r) c d", c=2)).then_inc(s_ab, 16)
            for c in range(2):
                act.dma_start(wnat[:, 18 + c, :].rearrange("p (a r) -> p a r", a=NA),
                              b3[:, 128 * c:128 * c + 128, :].rearrange("a o r -> o a r")).then_inc(s_ab, 16)
            for i, dst in enumerate((wkvT, wqT, woT, w3T, abT)):
                if i == 3:
                    act.wait_ge(s_dset, mark["angles"])
                    a.activation(trig[:, :, :, :], trig[:, :, :, :], ACT.Sin).then_inc(s_trig, 1)
                act.wait_ge(s_wt, i + 1)
                a.activation(dst[:, :, :].rearrange("p c o -> p (c o)"), ps[i][:, :], ACT.Copy).then_inc(s_wtc, 1)
            for i in range(2):
                act.wait_ge(s_bg[i], 32)
                a.activation(new[i][:, :, 1, :].rearrange("p o (g d) -> p g o d", g=G),
                             old[i][:, 1, :].rearrange("p (g o d) -> p g o d", g=G, o=BLOCK), ACT.Copy).then_inc(s_perm, 1)

            def copy_x1T(n, u):
                act.wait_ge(s_l0, n + 1)
                if not isinstance(n, int) or n >= 2:
                    act.wait_ge(s_kvp, n - 1)
                a.activation(xT[u % 2][:, :, :].rearrange("p c t -> p (c t)"), ps[u % 2][:, 0:T], ACT.Copy).then_inc(s_xtc, 1)

            def copy_kv_x1(n, u, turn):
                if turn is not None:
                    act.wait_ge(s_scat[u], 16 * turn)
                act.wait_ge(s_kvp, n + 1)
                a.activation(kv[:, u, :], ps[4 + u % 2][:, 0:2 * KVD], ACT.Copy).then_inc(s_kvc, 1)
                if turn is not None or u >= 4:
                    act.wait_ge(s_spill[u % 4], 32 * (2 * (0 if turn is None else turn) + u // 4))
                a.activation(x1s[u % 4][:, :], ps[2 + u % 2][:, 0:T], ACT.Copy).then_inc(s_x1c, 1)
                a.activation(q1s[u % 4][:, :], ps[4 + u % 2][:, 2 * KVD:2 * KVD + T], ACT.Copy).then_inc(s_qc, 1)

            def eight(n0, turn, last):
                for u in range(8):
                    if not (last and u == 7):
                        copy_x1T(n0 + u + 1, u + 1)
                    copy_kv_x1(n0 + u, u, turn)

            copy_x1T(0, 0)
            eight(0, None, False)
            with act.Fori(1, NT // 8 - 1) as it:
                eight(8 * it, it, False)
            eight(NT - 8, NT // 8 - 1, True)
            def slot(it, k):
                b = 16 * it + k
                if k % 4 == 2 and 0 <= (k - 6) // 4 < NT:
                    n = (k - 6) // 4
                    act.wait_ge(s_pv, 16 * it + 4 * n + 4)
                    a.activation(oT[n % 2][:, :, :, :].rearrange("p h f t -> p f h t"),
                                 ps_o[:, 0:TB * HPG * C].rearrange("p (f h t) -> p f h t", f=TB, h=HPG), ACT.Copy).then_inc(s_oc, 1)
                for kind, n in fin_step(k):
                    bank, _ = misc((kind, n), it)
                    if kind == "x3":
                        await_step(act, (kind, n), it)
                        a.activation(x3T[n % 2][:, :, :].rearrange("p c t -> p (c t)"), ps_m[bank][:, 0:T], ACT.Copy).then_inc(s_empty[bank], 1)
                    if kind == "x4":
                        if k >= 8:
                            act.wait_ge(s_out[n % 2], 16 * (2 * it + n // 2) + 16)
                        await_step(act, (kind, n), it)
                        a.activation(x4s[n % 2][:, :], ps_m[bank][:, 0:T], ACT.Copy).then_inc(s_empty[bank], 1)
                if 0 <= k < B:
                    act.wait_ge(s_max, b + 1)
                    if k >= 2:
                        act.wait_ge(s_pn, b - 1)
                    for h in range(HPG):
                        last = a.activation(pex[k % 2][:, h, :], ps_s[k % 2][:, h * KEYS:(h + 1) * KEYS], ACT.Exp,
                                            bias=nmax[:, k % 4, h:h + 1], accum_out=rsum[:, k % 4, h:h + 1])
                    last.then_inc(s_exp, 1)
                if 0 <= k - 1 < B:
                    if k >= 3:
                        act.wait_ge(s_pv, b - 2)
                    act.wait_ge(s_pt, b)
                    a.activation(pT[(k - 1) % 2][:, :, :, :].rearrange("p c h t -> p (c h t)"), ps_p[(k - 1) % 2][0:HK, :],
                                 ACT.Copy).then_inc(s_ptc, 1)
                for kind, n in prep_steps(k):
                    bank, _ = misc((kind, n), it)
                    m = ps_m[bank]
                    if kind == "qT":
                        await_step(act, (kind, n), it)
                        for g in range(G):
                            rows = slice(HD * g, HD * g + HD)
                            last = a.activation(
                                qbd[n // 2 % 2][rows, TB * (n % 2):TB * (n % 2) + TB, :, C * g:C * g + C],
                                m[rows, 0:HPG * 128].rearrange("p (h f t) -> p f h t", h=HPG, f=TB), ACT.Copy, scale=SCALE)
                        last.then_inc(s_empty[bank], 1)
                for n in rotated_tiles(k) if k < 0 else []:
                    act.wait_ge(s_gold[n], 32)
                    for piece in range(4):
                        a.activation(*reordered_piece(n, 1, piece), ACT.Copy).then_inc(s_order[n], 1)
            run_slots(act, slot)

        @block.tensor
        def _(pe):
            mm, turn_over = nc.tensor.matmul, nc.tensor.transpose

            def turn_weights(i):
                o = ps[i][:, :].rearrange("p (c o) -> p c o", c=2)
                for c in range(2):
                    for r in range(2):
                        dst = o[:, c, 128 * r:128 * r + 128]
                        if i == 0:
                            src = wnat[:, 2 * r + c, :]
                        elif i == 4:
                            src = wnat[:, 16 + 2 * c + r, :]
                        else:
                            src = wnat[:, 4 * i + 2 * r + c, :]
                        last = turn_over(dst, src, ident[:, :])
                last.then_inc(s_wt, 1)

            pe.wait_ge(s_cchain, cmark_iota)
            pe.wait_ge(s_wk, 32)
            turn_weights(0)
            pe.wait_ge(s_wq, 32)
            turn_weights(1)
            pe.wait_ge(s_wo, 64)
            turn_weights(2)
            pe.wait_ge(s_cchain, cmark_bd)
            pe.wait_ge(s_dset, mark["diag"])
            mm(ps[6][:, 0:NW], ones[:, :], diag[:, :, :].rearrange("p s b -> p (s b)"), start=True, stop=True).then_inc(s_wrow, 1)
            pe.wait_ge(s_dset, mark["same"])
            for s in range(NS):
                for t in range(NS):
                    last = mm(ps[7][:, s * (BLOCK + 1):(s + 1) * (BLOCK + 1)], same[:, t, 128 * s:128 * s + 128], valid[:, t, :],
                              start=(t == 0), stop=(t == NS - 1))
            last.then_inc(s_later, 1)
            pe.wait_ge(s_dset, mark["owner"])
            mm(ps[6][:, 0:NW], ones[:, :], diag[:, :, :].rearrange("p s b -> p (s b)"), start=True, stop=True).then_inc(s_crow, 1)
            pe.wait_ge(s_dset, mark["spread"])
            for i in range(3):
                last = mm(ps[6][:, NT * i:NT * i + NT], spread[:, i, :], of_tile[:, :], start=True, stop=True)
            last.then_inc(s_relay, 1)
            pe.wait_ge(s_w3i, 2)
            turn_weights(3)
            pe.wait_ge(s_ab, 48)
            turn_weights(4)

            pe.wait_ge(s_bd[0], 16 * TB)
            pe.wait_ge(s_wtc, 5)

            def first_stage(n, u, turn):
                pe.wait_ge(s_xin[u % 4], 16 * (2 * turn + u // 4) + 16)
                if not isinstance(n, int) or n >= 2:
                    pe.wait_ge(s_xtc, n - 1)
                for c in range(2):
                    last = mm(ps[u % 2][:, 128 * c:128 * c + 128], xin[u % 4][:, 128 * c:128 * c + 128],
                              bd[:, bass.ds(n, 1), :].rearrange("p a b -> p (a b)"), start=True, stop=True)
                last.then_inc(s_l0, 1)

            def project(n, u):
                pe.wait_ge(s_xtc, n + 1)
                if not isinstance(n, int) or n >= 2:
                    pe.wait_ge(s_kvc, n - 1)
                    pe.wait_ge(s_x1c, n - 1)
                    pe.wait_ge(s_qc, n - 1)
                for c in range(2):
                    last = turn_over(ps[2 + u % 2][:, 128 * c:128 * c + 128], xT[u % 2][:, c, :], ident[:, :])
                last.then_inc(s_tr1, 1)
                for c in range(2):
                    mm(ps[4 + u % 2][:, 0:2 * KVD], xT[u % 2][:, c, :], wkvT[:, c, :], start=(c == 0), stop=(c == 1))
                for c in range(2):
                    last = mm(ps[4 + u % 2][:, 2 * KVD:2 * KVD + T], xT[u % 2][:, c, :], wqT[:, c, :], start=(c == 0), stop=(c == 1))
                last.then_inc(s_kvp, 1)

            def eight(n0, turn, last):
                for u in range(8):
                    if not (last and u == 7):
                        first_stage(n0 + u + 1, (u + 1) % 8, turn + (u + 1) // 8)
                    project(n0 + u, u)

            first_stage(0, 0, 0)
            eight(0, 0, False)
            with pe.Fori(1, NT // 8 - 1) as it:
                eight(8 * it, it, False)
            pe.wait_ge(s_dset, mark["reads"])
            for j in range(2):
                mm(ps[7][0:ROWS, NG * j:NG * j + NG], gspread[:, j, :, :].rearrange("p f w -> p (f w)"), of_group[:, :],
                   start=True, stop=True)
            mm(ps[7][:, 128:128 + B], ones[:, :], adiag[:, :], start=True, stop=True).then_inc(s_reads, 1)
            eight(NT - 8, NT // 8 - 1, True)

            pe.wait_ge(s_xtc, NT)
            pe.wait_ge(s_kvc, NT)
            pe.wait_ge(s_x1c, NT)
            pe.wait_ge(s_qc, NT)
            pe.wait_ge(s_dset, mark["amask"])
            pe.wait_ge(s_cchain, cmark_qbd)

            def misc_step(it, kind, n):
                bank, _ = misc((kind, n), it)
                m = ps_m[bank]
                if kind == "qT":
                    pe.wait_ge(s_qrd, 4 * it + n + 1)
                    await_bank(pe, (kind, n), it)
                    for h in range(HPG):
                        last = turn_over(m[:, 128 * h:128 * h + 128],
                                         qr[n % 2][:, 128 * h:128 * h + 128], ident[:, :])
                if kind[0] == "k":
                    i, o0 = n % 2, 4 * int(kind[1])
                    if kind == "k0":
                        pe.wait_ge(s_gnew[i], 16 * (it + n // 2) + 16)
                    await_bank(pe, (kind, n), it)
                    for o in range(4):
                        last = turn_over(m[:, ROWS * o:ROWS * o + ROWS], new[i][0:ROWS, o0 + o, 0, :], ident[0:ROWS, 0:ROWS])
                if kind == "x2":
                    pe.wait_ge(s_oc, 4 * it + n + 1)
                    await_bank(pe, (kind, n), it)
                    for h in range(HPG):
                        last = mm(m[:, 0:T], oT[n % 2][:, h, :, :].rearrange("p f t -> p (f t)"), woT[:, h, :],
                                  start=(h == 0), stop=(h == HPG - 1))
                if kind == "x3":
                    if n == 0:
                        pe.wait_ge(s_bd[1], 16 * TB)
                    await_copied(pe, ("x2", n), it)
                    await_bank(pe, (kind, n), it)
                    for c in range(2):
                        last = mm(m[:, 128 * c:128 * c + 128], x2s[n % 2][:, 128 * c:128 * c + 128],
                                  bd[:, bass.ds(4 * it + n, 1), :].rearrange("p a b -> p (a b)"), start=True, stop=True)
                if kind == "xa":
                    await_copied(pe, ("x3", n), it)
                    await_bank(pe, (kind, n), it)
                    for c in range(2):
                        last = mm(m[:, 0:128], abT[:, 0, 128 * c:128 * c + 128], x3T[n % 2][:, c, :], start=(c == 0), stop=(c == 1))
                if kind == "x4":
                    await_copied(pe, ("xa", n), it)
                    await_bank(pe, (kind, n), it)
                    for c in range(2):
                        mm(m[:, 0:T], x3T[n % 2][:, c, :], w3T[:, c, :], start=(c == 0), stop=False)
                    last = mm(m[:, 0:T], xam[n % 2][:, :], abT[:, 1, :], start=False, stop=True)
                last.then_inc(s_full[bank], 1)

            def slot(it, k):
                b = 16 * it + k
                if 0 <= k < B:
                    grp, f, n = k // 8, k % 8, k // 4
                    if k % 4 == 0:
                        await_copied(pe, ("qT", n), it)
                        pe.wait_ge(s_pen, 4 * it + n + 1)
                    if f == 0:
                        await_keys(pe, grp, it)
                    if k >= 2:
                        pe.wait_ge(s_exp, b - 1)
                    for h in range(HPG):
                        dst = ps_s[k % 2][:, h * KEYS:(h + 1) * KEYS]
                        mm(dst, qbd[grp % 2][:, f, h, :], kT[grp % 2][:, f, :, :].rearrange("p w o -> p (w o)"), start=True, stop=False)
                        last = mm(dst, mask_sel[:, k % 4, :], pen[n % 2][:, :], start=False, stop=True)
                    last.then_inc(s_qk, 1)
                for kind, n in fin_step(k):
                    misc_step(it, kind, n)
                if 0 <= k - 1 < B:
                    pe.wait_ge(s_pn, b)
                    if k >= 3:
                        pe.wait_ge(s_ptc, b - 2)
                    for c in range(2):
                        for h in range(HPG):
                            last = turn_over(ps_p[(k - 1) % 2][0:HK, (HPG * c + h) * 128:(HPG * c + h + 1) * 128],
                                             pn[(k - 1) % 2][:, h, HK * c:HK * c + HK], ident[:, :])
                    last.then_inc(s_pt, 1)
                for kind, n in prep_steps(k):
                    misc_step(it, kind, n)
                if 0 <= k - 2 < B:
                    kb = k - 2
                    pe.wait_ge(s_ptc, b - 1)
                    if kb % GB == 0:
                        pe.wait_ge(s_vin[kb // GB % 2], 16 * (it + kb // 16) + 16)
                    if kb % 4 == 0 and kb >= 4:
                        pe.wait_ge(s_oc, 4 * it + kb // 4)
                    col = HPG * C * (kb % 4)
                    for c in range(2):
                        for g in range(G):
                            last = mm(ps_o[HD * g:HD * g + HD, col:col + HPG * C], vg[kb // GB % 2][:, kb % GB, c, HD * g:HD * g + HD],
                                      pT[kb % 2][:, c, :, C * g:C * g + C], start=(c == 0), stop=(c == 1))
                    last.then_inc(s_pv, 1)

            run_slots(pe, slot)


_INS = ["x", "itok_B_1_198", "itok_Bx257_0_4111", "itok_B_37_3939", "itok_B_0_7", "itok_B_0_6", "L0_cond_weights", "L1_cond_Wq",
        "L1_cond_Wk", "L1_cond_Wv", "L1_cond_Wo", "L1_cond_q_norm_scale", "L1_cond_k_norm_scale", "L1_cond_k_blocks",
        "L1_cond_v_blocks", "L2_cond_weights", "L3_cond_W", "L3_cond_A", "L3_cond_Bm", "L3_cond_scalings"]
_OUTS = [((128, 32, 256), "float32")]


def kernel(**inputs):
    import numpy as _np
    import concourse.bacc as _bacc
    from concourse import mybir as _mybir
    from concourse.bass_utils import run_bass_kernel_spmd as _run

    nc = _bacc.Bacc("TRN2", target_bir_lowering=False, num_devices=1)
    arrays, args = {}, []
    for name in _INS:
        a = _np.ascontiguousarray(inputs[name])
        arrays[f"in_{name}_dram"] = a
        args.append(nc.dram_tensor(f"in_{name}_dram", a.shape, _mybir.dt.from_np(a.dtype), kind="ExternalInput").ap())
    for i, (shape, dtype) in enumerate(_OUTS):
        dt = _mybir.dt.from_np(_np.dtype(dtype))
        args.append(nc.dram_tensor(f"out_{i}_dram", shape, dt, kind="ExternalOutput").ap())
    cond_resid_kernel(nc, *args)
    r = _run(nc, [arrays], core_ids=[0])
    return r.results[0]["out_0_dram"]
```

```python
import math
from contextlib import ExitStack

import concourse.bass as bass
from concourse import mybir


def cond_resid_kernel(
    nc, x, cond, table, kvlen, subj, adapt, w0, wq, wk, wv, wo, qscale, kscale, k_blocks, v_blocks, w2, w3, a3, b3, s3, out
):
    f32, bf16, i32 = mybir.dt.float32, mybir.dt.bfloat16, mybir.dt.int32
    ALU = mybir.AluOpType
    ACT = mybir.ActivationFunctionType
    AX = mybir.AxisListType

    B, C, T = x.shape
    NBLK = table.shape[1]
    POOL_BLOCKS, G, BLOCK, HD = k_blocks.shape
    H = wq.shape[0] // HD
    HPG = H // G
    KVD = G * HD
    WINDOW = 128
    W = 11
    WP = 12
    KEYS = W * BLOCK
    GB = 8
    ROWS = GB * W
    NG = B // GB
    TB = 128 // C
    NT = B // TB
    NS = (C + BLOCK - 2) // BLOCK + 1
    NW = NS * B
    HB = BLOCK // 2
    HK = HB * W
    NA, RANK = a3.shape[0], a3.shape[1]
    SCALE = 256.0 ** -0.5
    EPS = 1e-6
    SKIP = 16384.0
    DROP = 1048576.0
    NEG = -1e30
    HALF = HD // 2

    x_t = x.rearrange("(n b) c t -> n (b c) t", b=TB)
    out_t = out.rearrange("(n b) c t -> n (b c) t", b=TB)
    k_old = k_blocks.rearrange("n g o d -> n (g o d)")
    v_old = v_blocks.rearrange("n g o d -> n (g o d)")

    q_d = nc.dram_tensor("q_spill", [NT, 128, T], f32, kind="Internal").ap()
    v_d = nc.dram_tensor("values_by_group", [NG, ROWS * BLOCK, KVD], f32, kind="Internal").ap()
    x1_d = nc.dram_tensor("x1_spill", [NT, 128, T], f32, kind="Internal").ap()
    w0_d = nc.dram_tensor("w0_picked", [B, C * C], f32, kind="Internal").ap()
    w2_d = nc.dram_tensor("w2_picked", [B, C * C], f32, kind="Internal").ap()
    new_d = nc.dram_tensor("written_blocks", [NW * BLOCK, 2 * KVD], f32, kind="Internal").ap()
    new_blocks = new_d.rearrange("(n o) c -> n (o c)", o=BLOCK)
    new_rows = new_d.rearrange("(s b o) c -> s b (o c)", b=B, o=BLOCK)

    ctx = ExitStack()
    with ctx:
        def sb(name, shape, dt=f32):
            return ctx.enter_context(nc.sbuf_tensor(name, shape, dt))

        def sem(name):
            return ctx.enter_context(nc.semaphore(name))

        room = sb("blocks_room", [128, 4 * BLOCK * ROWS])
        turned = room[:, 0:2 * BLOCK * ROWS].rearrange("p (i f w o) -> p i f w o", i=2, o=BLOCK, w=W)
        kT = [turned[:, i] for i in (0, 1)]
        vg_at = 2 * BLOCK * ROWS
        qs = [room[:, vg_at + GB * 2 * KVD + T * i:vg_at + GB * 2 * KVD + T * i + T] for i in range(2)]
        proom = sb("p_room", [128, 4 * HPG * KEYS])
        probs = proom[:, :].rearrange("p (i h k) -> p i h k", i=4, h=HPG)
        pex, pn = [probs[:, i] for i in (0, 1)], [probs[:, i] for i in (2, 3)]
        troom = sb("pT_room", [128, 2 * 2 * HPG * 128])
        pT = [troom[0:HK, 512 * i:512 * i + 512].rearrange("p (c h t) -> p c h t", c=2, h=HPG) for i in range(2)]
        vroom = sb("v_room", [128, GB * 2 * KVD])
        vg = [half[0:HK, :].rearrange("p (f c d) -> p f c d", f=GB, c=2)
              for half in (room[:, vg_at:vg_at + GB * 2 * KVD], vroom)]
        wnat = room[:, 0:20 * 128].rearrange("p (i d) -> p i d", i=20)
        same = room[:, 20 * 128:20 * 128 + NS * NW].rearrange("p (s w) -> p s w", s=NS)
        later_at = 20 * 128 + NS * NW
        later_or_same = room[:, later_at:later_at + (2 * NS - 1) * 128].rearrange("p (s b) -> p s b", b=128)
        pick_at = later_at + (2 * NS - 1) * 128
        wpick = [room[:, pick_at:pick_at + C * C], proom[:, 0:C * C]]
        kv = room[:, vg_at:vg_at + 8 * 2 * KVD].rearrange("p (u c) -> p u c", u=8)
        x1s = [vroom[:, T * u:T * u + T] for u in range(4)]
        q1s = [vroom[:, T * u:T * u + T] for u in range(4, 8)]
        xT = [troom[:, T * i:T * i + T].rearrange("p (c t) -> p c t", c=2) for i in range(2)]

        eroom = sb("end_room", [128, 5 * NT * HALF])
        ang = eroom[:, 0:NT * HALF].rearrange("p (n i) -> p n i", i=HALF)
        turns = eroom[:, NT * HALF:2 * NT * HALF].rearrange("p (n i) -> p n i", i=HALF)
        trig = eroom[:, 3 * NT * HALF:5 * NT * HALF].rearrange("p (j n i) -> p j n i", j=2, i=HALF)
        x2s, x4s = [[eroom[:, T * i:T * i + T] for i in (j, j + 1)] for j in (0, 2)]
        x3T = [eroom[:, T * i:T * i + T].rearrange("p (c t) -> p c t", c=2) for i in (4, 5)]
        oT = [eroom[:, T * i:T * i + T].rearrange("p (h f t) -> p h f t", h=HPG, f=TB) for i in (6, 7)]
        xam = [eroom[:, T * 8 + 128 * i:T * 8 + 128 * i + 128] for i in range(2)]

        zcol = sb("zcol", [128, 1])
        exp_of_zero = sb("exp_of_zero", [128, 1])
        ident = sb("ident", [128, 128])
        ones = sb("ones", [128, 128])
        iota_i = sb("iota_i", [128, NW], i32)
        iota = sb("iota", [128, NW])
        key_i = sb("key_i", [128, KEYS], i32)
        keypos = sb("keypos", [128, KEYS])
        part_i = sb("part_i", [128, 1], i32)
        part = sb("part", [128, 6])
        part_m = sb("part_m", [128, 6], i32)
        in_tile = sb("in_tile", [128, TB])
        of_tile = sb("of_tile", [128, NT])
        in_group = sb("in_group", [128, GB])
        of_group = sb("of_group", [128, NG])
        mask_sel = sb("mask_sel", [128, TB, 128], bf16)
        halfpow = sb("halfpow", [128, H])
        inv = sb("inv", [128, HALF])

        kvlen_i = sb("kvlen_i", [128, 1], i32)
        cond_i = sb("cond_i", [128, 1], i32)
        subj_i = sb("subj_i", [128, 1], i32)
        adapt_i = sb("adapt_i", [128, 1], i32)
        table_i = sb("table_i", [128, NBLK], i32)
        tab = sb("tab", [128, NBLK])
        ci = sb("ci", [128, 8], i32)
        cf = sb("cf", [128, 8])
        slots = sb("slots", [128, NS + WP])
        blk = sb("blk", [128, NS + WP])
        pick = sb("pick", [128, NBLK])
        diag = sb("diag", [128, NS, 128])
        wrow = sb("wrow", [128, NW])
        valid = sb("valid", [128, NS, BLOCK + 1])
        vlow = sb("vlow", [128, NS, BLOCK])
        vtmp = sb("vtmp", [128, NS, BLOCK])
        dest = sb("dest", [128, NS * BLOCK])
        dest2 = sb("dest2", [128, NS * BLOCK])
        number = sb("number", [128, NS])
        owner = sb("owner", [128, NS])
        own = sb("own", [128, NS])
        crow = sb("crow", [128, NW])
        rowid = sb("rowid", [128, NS * BLOCK])
        off_bits = sb("off_bits", [128, 4])
        moved = sb("moved", [128, 2, NS * BLOCK])
        step_up = sb("step_up", [128, NS * BLOCK])
        tok = sb("tok", [128, 4, C])
        base_idx = sb("base_idx", [128, 2], i32)
        hits = sb("hits", [128, WP])
        hjunk = sb("hjunk", [128, NW])
        rd = sb("rd", [128, 2, W])
        rtmp = sb("rtmp", [128, 2, W])
        g_idx = sb("g_idx", [128, 4], i32)
        spread = sb("spread", [128, 3, 128])
        gspread = sb("gspread", [128, 2, GB, W])
        tok_idx = sb("tok_idx", [128, NT], i32)
        tok_pos = sb("tok_pos", [128, NT])
        tok_hi = sb("tok_hi", [128, NT])
        tok_lo = sb("tok_lo", [128, NT])
        rd_idx = sb("rd_idx", [128, 2, NG], i32)
        adiag = sb("adiag", [128, 128])
        amask = sb("amask", [128, B])
        scal_col = sb("scal_col", [128, 1])

        gain = sb("gain", [128, 2, HD])
        ngain = sb("ngain", [128, 2, HD])
        ctab = sb("ctab", [128, 2, NT, HD])
        stab = sb("stab", [128, 2, NT, HD])

        wkvT = sb("wkvT", [128, 2, 2 * KVD])
        wqT = sb("wqT", [128, 2, T])
        woT = sb("woT", [128, HPG, T])
        w3T = sb("w3T", [128, 2, T])
        abT = sb("abT", [128, 2, T])
        bd = sb("bd", [128, NT, 128])

        old = [sb(f"old{i}", [128, 2, G * BLOCK * HD]) for i in range(2)]
        new = [sb(f"new{i}", [128, BLOCK, 2, KVD]) for i in range(2)]

        xin = [sb(f"xin{i}", [128, T]) for i in range(4)]
        kv_idx = sb("kv_idx", [128, 8], i32)
        rp = sb("rp", [128, 5, T])
        rms = sb("rms", [128, 2, 3, H])
        qr = [sb(f"qr{i}", [128, T]) for i in range(2)]
        qbd = [sb(f"qbd{i}", [128, GB, HPG, 128]) for i in range(2)]
        pen_hi = sb("pen_hi", [128, KEYS])
        pen = [sb(f"pen{i}", [128, KEYS], bf16) for i in range(2)]
        nmax = sb("nmax", [128, 4, HPG])
        rsum = sb("rsum", [128, 4, HPG])
        rrec = sb("rrec", [128, 4, HPG])

        ps = [ctx.enter_context(nc.psum_tensor(f"bank{i}", [128, 512], f32)) for i in range(8)]
        ps_s, ps_p, ps_o, ps_m = ps[0:2], [ps[2], ps[4]], ps[5], [ps[6], ps[7], ps[3]]

        s_len, s_tab, s_cond, s_subj, s_adapt = (sem(n) for n in ("len_in", "table_in", "cond_in", "subj_in", "adapt_in"))
        s_gain, s_scal = sem("gain_in"), sem("scal_in")
        s_wk, s_wq, s_wo, s_w3, s_ab = (sem(n) for n in ("wkv_in", "wq_in", "wo_in", "w3_in", "ab_in"))
        s_pick = [sem("w0_picked_in"), sem("w2_picked_in")]
        s_pickw = [sem("w0_picked_out"), sem("w2_picked_out")]
        s_bd = [sem("bd0_in"), sem("bd2_in")]
        s_xin = [sem(f"x_in{i}") for i in range(4)]
        s_q = [sem(f"q_in{i}") for i in range(2)]
        s_vst = [sem(f"values_out{i}") for i in range(2)]
        s_vin = [sem(f"values_in{i}") for i in range(2)]
        s_spill = [sem(f"x1_out{i}") for i in range(4)]
        s_x1 = [sem(f"x1_in{i}") for i in range(4)]
        s_bg = [sem(f"base_in{i}") for i in range(4)]
        s_bs = [sem(f"base_out{i}") for i in range(2)]
        s_scat = [sem(f"tokens_out{i}") for i in range(8)]
        s_gold = [sem(f"old_in{i}") for i in range(2)]
        s_gnew = [sem(f"new_in{i}") for i in range(2)]
        s_out = [sem(f"out_done{i}") for i in range(2)]
        s_cchain = sem("constant_made")
        s_dset = sem("setup_op")
        s_wrow, s_later, s_places, s_relay, s_reads = (sem(n) for n in ("wrow_ps", "later_ps", "positions_ps", "relay_ps", "reads_ps"))
        s_wt, s_wtc, s_trig, s_perm, s_w3i = (sem(n) for n in ("weights_turned", "weights_copied", "trig_ready", "base_permuted", "w3_plus_i"))
        s_zero, s_zfill, s_crow = sem("old_zeroed"), sem("second_blocks_zeroed"), sem("crow_ps")
        s_order = [sem(f"old_reordered{i}") for i in range(2)]
        s_gix = [sem("old_index_staged"), sem("new_index_staged")]
        s_look, s_passed, s_sp_passed = sem("slot_looked_up"), sem("pool_passed"), sem("sync_passed")
        s_l0, s_xtc, s_tr1, s_kvp, s_kvc, s_qc, s_x1c = (
            sem(n) for n in ("l0_done", "x1T_copied", "x1_turned", "kvq_projected", "kv_copied", "q_copied", "x1_copied"))
        s_kr, s_ms, s_rstd, s_rope = (sem(n) for n in ("k_roped", "ms_ready", "rstd_ready", "rope_op"))
        s_tix = sem("token_index_staged")
        s_qk, s_max, s_exp, s_rec, s_pn, s_pt, s_ptc, s_pv = (
            sem(n) for n in ("qk_done", "max_done", "exp_done", "rec_done", "p_normal", "p_turned", "pT_copied", "pv_done"))
        s_oc, s_pen1, s_pen, s_qrd = (sem(n) for n in ("oT_copied", "pen_half", "pen_ready", "q_roped"))
        s_full = [sem("prep_full0"), sem("prep_full1"), sem("end_full")]
        s_empty = [sem("prep_empty0"), sem("prep_empty1"), sem("end_empty")]

        block = ctx.enter_context(nc.Block())
        mark = {}
        cmark_iota, cmark_ones, cmark_bd, cmark_masks = 5, 6, 7, 10
        cmark_all = cmark_masks + 4 + HALF
        cmark_qbd = cmark_all + 2

        PREP = {0: [("k0", None)], 1: [("k1", None)], 2: [("k2", None)], 3: [("qT", 0)], 4: [("k3", None)], 7: [("qT", 1)]}
        FIRST_PREP = {0: [("qT", 0)], 1: [("qT", 1)], 2: [("k0", None)], 3: [("k1", None)], 4: [("k2", None)],
                      5: [("k3", None)]}
        ROTATE = {0: 0, 4: 1}
        FIN = {3: ("x2", 7), 0: ("x3", 8), 1: ("xa", 9), 2: ("x4", 10)}
        LAST = 4 * (NT - 1) + 10

        def fin_step(k):
            kind, lag = FIN[k % 4]
            n = (k - lag) // 4
            return [(kind, n)] if 0 <= n < NT else []

        def prep_steps(k):
            grp, table = k // 8 + 1, PREP if k >= 0 else FIRST_PREP
            if not 0 <= grp < NG:
                return []
            return [(kind, grp if u is None else 2 * grp + u) for kind, u in table.get(k % 8, [])]

        def rotated_tiles(k):
            grp = k // 8 + 1
            return [2 * grp + ROTATE[k % 8]] if 1 <= grp < NG and k % 8 in ROTATE else []

        place = {}
        served = [0, 0, 0]
        for k in range(-8, LAST + 1):
            for step in prep_steps(k):
                bank = (served[0] + served[1]) % 2
                place[step] = (bank, served[bank])
                served[bank] += 1
            for step in fin_step(k):
                place[step] = (2, served[2])
                served[2] += 1
        PER_LOOP = [6, 6, 16]
        LOOPS = B // 16 - 2

        EARLY = 3
        ROPE = 6

        def rope_of_pair(pair):
            return pair + {12: 1}.get(pair, 2) if isinstance(pair, int) and pair >= 12 else pair

        def rope_of_tile(tile):
            return 12 + 2 * tile if isinstance(tile, int) and tile < 2 else NT // 2 + tile

        def misc(step, it):
            bank, before = place[step]
            return bank, before + PER_LOOP[bank] * it

        def await_bank(eng, step, it):
            bank, before = misc(step, it)
            if not isinstance(before, int) or before > 0:
                eng.wait_ge(s_empty[bank], before)

        def await_step(eng, step, it):
            bank, before = misc(step, it)
            eng.wait_ge(s_full[bank], before + 1)

        def await_copied(eng, step, it):
            bank, before = misc(step, it)
            eng.wait_ge(s_empty[bank], before + 1)

        def await_keys(eng, grp, it):
            last = {place[(f"k{i}", grp)][0]: (f"k{i}", grp) for i in range(4)}
            for step in last.values():
                await_copied(eng, step, it)

        def reordered_piece(i, which, piece):
            at = slice(4 * piece, 4 * piece + 4)
            return (new[i][0:ROWS, at, which, :].rearrange("p o (g d) -> p g o d", g=G),
                    old[i][0:ROWS, which, :].rearrange("p (g o d) -> p g o d", g=G, o=BLOCK)[:, :, at, :])

        def pieces_in_slot(k, by_slot):
            if k in (0, 1):
                return 0, (2 * k, 2 * k + 1)
            kk = k + EARLY
            if k < 6 or kk // 8 + 2 >= NG:
                return 0, ()
            return kk // 8 % 2, by_slot.get(k % 8, ())

        def await_refill(eng, k, it):
            kk = max(k, 0) + EARLY
            i, fills = kk // 8 % 2, it + kk // 16 + 1
            eng.wait_ge(s_gold[i], 32 * fills + 32)
            await_keys(eng, kk // 8, it)
            eng.wait_ge(s_vst[i], 16 * fills)

        def run_slots(eng, slot):
            for k in range(-8, 8):
                slot(0, k)
            with eng.Fori(0, LOOPS) as it:
                for k in range(8, 24):
                    slot(it, k)
            for k in range(8 + 16 * LOOPS, LAST + 1):
                slot(0, k)

        @block.vector
        def _(dve):
            v = nc.vector
            done = [0]

            def put(ins):
                done[0] += 1
                ins.then_inc(s_dset, 1)

            def settled():
                dve.wait_ge(s_dset, done[0])

            dve.wait_ge(s_len, 16)
            dve.wait_ge(s_cchain, cmark_iota)
            put(v.tensor_copy(iota[:, :], iota_i[:, :]))
            put(v.tensor_scalar(ci[:, 0:1], kvlen_i[:, :], 4, None, ALU.arith_shift_right))
            put(v.tensor_scalar(ci[:, 1:2], kvlen_i[:, :], BLOCK - 1, None, ALU.bitwise_and))
            for i in range(4):
                put(v.tensor_scalar(ci[:, 4 + i:5 + i], kvlen_i[:, :], i, 1, ALU.arith_shift_right, ALU.bitwise_and))
            put(v.tensor_scalar(ci[:, 2:3], kvlen_i[:, :], float(1 - WINDOW), 0.0, ALU.add, ALU.max))
            put(v.tensor_copy(cf[:, 4:5], kvlen_i[:, :]))
            put(v.tensor_scalar(part_m[:, 1:2], part_i[:, :], TB - 1, None, ALU.bitwise_and))
            put(v.tensor_scalar(part_m[:, 2:3], part_i[:, :], 2, None, ALU.arith_shift_right))
            put(v.tensor_scalar(part_m[:, 3:4], part_i[:, :], GB - 1, None, ALU.bitwise_and))
            put(v.tensor_scalar(part_m[:, 4:5], part_i[:, :], 3, None, ALU.arith_shift_right))
            put(v.tensor_scalar(part_m[:, 5:6], part_i[:, :], 4, None, ALU.arith_shift_right))
            settled()
            put(v.tensor_scalar(ci[:, 3:4], ci[:, 2:3], 4, None, ALU.arith_shift_right))
            put(v.tensor_copy(cf[:, 0:2], ci[:, 0:2]))
            put(v.tensor_copy(off_bits[:, :], ci[:, 4:8]))
            put(v.tensor_copy(part[:, 0:1], part_i[:, :]))
            put(v.tensor_copy(part[:, 1:6], part_m[:, 1:6]))
            settled()
            put(v.tensor_scalar(cf[:, 3:4], ci[:, 3:4], float(NBLK - W), None, ALU.min))
            put(v.tensor_scalar(in_tile[:, :], iota[:, 0:TB], part[:, 1:2], None, ALU.is_equal))
            put(v.tensor_scalar(of_tile[:, :], iota[:, 0:NT], part[:, 2:3], None, ALU.is_equal))
            put(v.tensor_scalar(in_group[:, :], iota[:, 0:GB], part[:, 3:4], None, ALU.is_equal))
            put(v.tensor_scalar(of_group[:, :], iota[:, 0:NG], part[:, 4:5], None, ALU.is_equal))
            settled()
            put(v.scalar_tensor_tensor(cf[:, 5:6], cf[:, 3:4], -float(BLOCK), cf[:, 4:5], ALU.mult, ALU.add))
            put(v.tensor_scalar(slots[:, 0:NS], iota[:, 0:NS], cf[:, 0:1], None, ALU.add))
            put(v.tensor_scalar(slots[:, NS:], iota[:, 0:WP], cf[:, 3:4], None, ALU.add))
            dve.wait_ge(s_tab, 16)
            put(v.tensor_copy(tab[:, :], table_i[:, :]))
            settled()
            for j, unused in enumerate((pick[:, :], hjunk[:, 0:NBLK], crow[:, 0:NBLK])):
                put(v.scalar_tensor_tensor(unused, iota[:, 0:NBLK], slots[:, j:j + 1], tab[:, :], ALU.is_equal, ALU.mult,
                                           accum_out=blk[:, j:j + 1]))
            settled()
            put(v.tensor_scalar(cf[:, 6:7], cf[:, 1:2], 0.0, None, ALU.is_gt))
            settled()
            put(v.scalar_tensor_tensor(cf[:, 7:8], blk[:, NS - 1:NS], 1.0, cf[:, 6:7], ALU.add, ALU.mult))
            settled()
            put(v.tensor_scalar(blk[:, NS - 1:NS], cf[:, 7:8], -1.0, None, ALU.add))
            settled()
            for s in range(NS):
                put(v.tensor_scalar(diag[:, s, :], ident[:, :], blk[:, s:s + 1], None, ALU.mult))
            mark["diag"] = done[0]
            for i, s in enumerate((0, NS - 1)):
                put(v.tensor_scalar(base_idx[:, i:i + 1], blk[:, s:s + 1], 0.0, None, ALU.max))
            mark["base"] = done[0]
            put(v.tensor_scalar(tok[:, 2, :], iota[:, 0:C], cf[:, 4:5], None, ALU.add))
            put(v.tensor_scalar(tok[:, 3, :], iota[:, 0:C], cf[:, 5:6], None, ALU.add))
            settled()
            for i in (1, 2):
                for f in range(TB):
                    put(v.tensor_scalar(spread[:, i, C * f:C * f + C], tok[:, i + 1, :], in_tile[:, f:f + 1], None, ALU.mult))
            mark["positions"] = done[0]
            dve.wait_ge(s_pick[0], 16)
            put(v.tensor_scalar(wpick[0][:, ::C + 1], wpick[0][:, ::C + 1], 1.0, None, ALU.add))
            mark["w0"] = done[0]
            for s in range(NS):
                put(v.tensor_scalar(vtmp[:, s, :], iota[:, BLOCK * s:BLOCK * s + BLOCK], cf[:, 1:2], None, ALU.subtract))
                put(v.tensor_scalar(number[:, s:s + 1], part[:, 0:1], float(B * s + 1), None, ALU.add))
            settled()
            for s in range(NS):
                put(v.tensor_scalar(valid[:, s, 0:BLOCK], vtmp[:, s, :], 0.0, None, ALU.is_ge))
                put(v.tensor_scalar(valid[:, s, BLOCK:BLOCK + 1], blk[:, s:s + 1], 0.0, None, ALU.is_ge))
            put(v.tensor_scalar(vlow[:, :, :], vtmp[:, :, :], float(C), None, ALU.is_lt))
            settled()
            for s in range(NS):
                put(v.tensor_tensor(valid[:, s, 0:BLOCK], valid[:, s, 0:BLOCK], vlow[:, s, :], ALU.mult))
            dve.wait_ge(s_wrow, 1)
            put(v.tensor_copy(wrow[:, :], ps[6][:, 0:NW]))
            dve.wait_ge(s_cchain, cmark_masks)
            settled()
            for s in range(NS):
                masks = later_or_same[:, NS - 1 - s:2 * NS - 1 - s, :].rearrange("p s b -> p (s b)")
                put(v.scalar_tensor_tensor(same[:, s, :], wrow[:, :], blk[:, s:s + 1], masks, ALU.is_equal, ALU.mult))
            mark["same"] = done[0]
            dve.wait_ge(s_pick[1], 16)
            put(v.tensor_scalar(wpick[1][:, ::C + 1], wpick[1][:, ::C + 1], 1.0, None, ALU.add))
            mark["w1"] = done[0]
            BIG = 12582912.0
            TWO_PI = 2.0 * math.pi
            C1 = 6.28125
            C2 = math.floor((TWO_PI - C1) * 2 ** 21) / 2 ** 21
            C3 = TWO_PI - C1 - C2
            PI = 3.1415925
            dve.wait_ge(s_places, 1)
            put(v.tensor_copy(tok_pos[:, :], ps[5][:, 0:NT]))
            put(v.tensor_copy(tok_hi[:, :], ps[5][:, NT:2 * NT]))
            put(v.tensor_scalar(tok_lo[:, :], ps[5][:, NT:2 * NT], -float(WINDOW), None, ALU.add))
            mark["placed"] = done[0]
            dve.wait_ge(s_cchain, cmark_all)
            settled()
            put(v.tensor_tensor(ang[:, :, :], tok_pos[:, :].unsqueeze(2).broadcast_to([128, NT, HALF]),
                                inv[:, :].unsqueeze(1).broadcast_to([128, NT, HALF]), ALU.mult))
            settled()
            put(v.tensor_scalar(turns[:, :, :], ang[:, :, :], 1.0 / TWO_PI, None, ALU.mult))
            settled()
            put(v.tensor_scalar(turns[:, :, :], turns[:, :, :], BIG, None, ALU.add))
            settled()
            put(v.tensor_scalar(turns[:, :, :], turns[:, :, :], -BIG, None, ALU.add))
            for part_of_turn in (C1, C2, C3):
                settled()
                put(v.scalar_tensor_tensor(trig[:, 0, :, :], turns[:, :, :], -part_of_turn,
                                           ang[:, :, :] if part_of_turn == C1 else trig[:, 0, :, :], ALU.mult, ALU.add))
            settled()
            put(v.tensor_scalar(trig[:, 0, :, :], trig[:, 0, :, :], PI, -PI, ALU.min, ALU.max))
            mark["angles"] = done[0]
            dve.wait_ge(s_later, 1)
            later = ps[7][:, 0:NS * (BLOCK + 1)].rearrange("p (s c) -> p s c", s=NS)
            for s in range(NS):
                put(v.tensor_scalar(owner[:, s:s + 1], later[:, s, BLOCK:BLOCK + 1], 0.0, number[:, s:s + 1], ALU.is_equal, ALU.mult))
            settled()
            for s in range(NS):
                put(v.tensor_scalar(owner[:, s:s + 1], owner[:, s:s + 1], valid[:, s, BLOCK:BLOCK + 1], None, ALU.mult))
            settled()
            for s in range(NS):
                put(v.tensor_scalar(diag[:, s, :], ident[:, :], owner[:, s:s + 1], None, ALU.mult))
            mark["owner"] = done[0]
            for s in range(NS):
                put(v.tensor_scalar(dest[:, BLOCK * s:BLOCK * s + BLOCK], later[:, s, 0:BLOCK], 0.0, DROP, ALU.is_gt, ALU.mult))
            dve.wait_ge(s_crow, 1)
            put(v.tensor_copy(crow[:, :], ps[6][:, 0:NW]))
            settled()
            for s, unused in enumerate((hjunk[:, :], ctab[:, 0, 0:NW // HD, :].rearrange("p n d -> p (n d)"),
                                        stab[:, 0, 0:NW // HD, :].rearrange("p n d -> p (n d)"))):
                put(v.scalar_tensor_tensor(unused, wrow[:, :], blk[:, s:s + 1], crow[:, :], ALU.is_equal, ALU.mult,
                                           accum_out=own[:, s:s + 1]))
            settled()
            put(v.tensor_scalar(own[:, :], own[:, :], -1.0, float(BLOCK), ALU.add, ALU.mult))
            settled()
            for s in range(NS):
                put(v.tensor_scalar(rowid[:, BLOCK * s:BLOCK * s + BLOCK], iota[:, 0:BLOCK], own[:, s:s + 1], None, ALU.add))
            settled()
            put(v.tensor_tensor(dest2[:, :], dest[:, :], rowid[:, :], ALU.add))
            settled()
            src, width = dest2[:, :], NS * BLOCK
            for i, bit in enumerate((3, 2, 1, 0)):
                width -= 2 ** bit
                at = tok[:, 0, 0:C] if bit == 0 else moved[:, i % 2, 0:width]
                width = C if bit == 0 else width
                put(v.tensor_tensor(step_up[:, 0:width], src[:, 2 ** bit:2 ** bit + width], src[:, 0:width], ALU.subtract))
                settled()
                put(v.scalar_tensor_tensor(at, step_up[:, 0:width], off_bits[:, bit:bit + 1], src[:, 0:width], ALU.mult, ALU.add))
                settled()
                src = at
            for f in range(TB):
                put(v.tensor_scalar(spread[:, 0, C * f:C * f + C], tok[:, 0, :], in_tile[:, f:f + 1], None, ALU.mult))
            mark["spread"] = done[0]

            def tables(which):
                for dst, of, by, lo in ((ctab[:, which, :, 0:HALF], 0, gain, 0), (ctab[:, which, :, HALF:], 0, gain, HALF),
                                        (stab[:, which, :, 0:HALF], 1, ngain, HALF), (stab[:, which, :, HALF:], 1, gain, 0)):
                    put(v.tensor_tensor(dst, trig[:, of, :, :], by[:, which, lo:lo + HALF].unsqueeze(1).broadcast_to([128, NT, HALF]),
                                        ALU.mult))

            dve.wait_ge(s_gain, 32)
            put(v.tensor_scalar(gain[:, :, :], gain[:, :, :], 1.0, None, ALU.add))
            settled()
            put(v.tensor_scalar(ngain[:, :, :], gain[:, :, :], -1.0, None, ALU.mult))
            dve.wait_ge(s_relay, 1)
            put(v.tensor_copy(tok_idx[:, :], ps[6][:, 0:NT]))
            mark["tokens"] = done[0]
            dve.wait_ge(s_trig, 4)
            settled()
            tables(1)
            settled()

            def rotate(src, cos_t, sin_t, index, i, parts=(0, 1), look=None):
                outer, inner = src.shape[1:3]

                def shaped(ap):
                    return ap.rearrange("p (a h d) -> p a h d", a=outer, d=HD)

                def cut(ap, lo, hi):
                    return ap[:, :, :, lo:hi]

                def over_heads(ap, lo, hi):
                    one = ap[:, :, lo:hi].unsqueeze(2) if ap.shape[1] == outer else ap[:, :, lo:hi].unsqueeze(1)
                    return one.broadcast_to([128, outer, inner, hi - lo])

                first = ROPE * index
                if 0 in parts:
                    v.tensor_tensor(shaped(rp[:, 0, :]), src, src, ALU.mult).then_inc(s_rope, 1)
                    if look is not None:
                        look_up_half(look[0], look[1])
                    dve.wait_ge(s_rope, first + 1)
                    v.tensor_reduce(rms[:, i, 0, :], rp[:, 0, :].rearrange("p (h d) -> p h d", d=HD), AX.X, ALU.add).then_inc(s_rope, 1)
                    if look is not None:
                        look_up_half(look[0], look[1] + 1)
                    dve.wait_ge(s_rope, first + 2)
                    v.tensor_scalar(rms[:, i, 1, :], rms[:, i, 0, :], 1.0 / HD, EPS, ALU.mult, ALU.add).then_inc(s_ms, 1)
                    v.tensor_tensor(shaped(rp[:, 1, :]), src, over_heads(cos_t, 0, HD), ALU.mult).then_inc(s_rope, 1)
                if 1 in parts:
                    v.tensor_tensor(cut(shaped(rp[:, 2, :]), 0, HALF), cut(src, HALF, HD), over_heads(sin_t, 0, HALF), ALU.mult).then_inc(s_rope, 1)
                    v.tensor_tensor(cut(shaped(rp[:, 2, :]), HALF, HD), cut(src, 0, HALF), over_heads(sin_t, HALF, HD), ALU.mult).then_inc(s_rope, 1)
                    if look is not None:
                        look_up_half(look[0], look[1] + 2)
                    dve.wait_ge(s_rope, first + 5)
                    v.tensor_tensor(rp[:, 3 + i, :], rp[:, 1, :], rp[:, 2, :], ALU.add).then_inc(s_rope, 1)

            def scale_by_rstd(dst, dst_sem, index, i):
                outer, inner = dst.shape[1:3]
                dve.wait_ge(s_rope, ROPE * index + ROPE)
                dve.wait_ge(s_rstd, index + 1)
                per_head = rms[:, i, 2, :].rearrange("p (a h) -> p a h", a=outer).unsqueeze(3).broadcast_to([128, outer, inner, HD])
                v.tensor_tensor(dst, rp[:, 3 + i, :].rearrange("p (a h d) -> p a h d", a=outer, d=HD), per_head, ALU.mult).then_inc(dst_sem, 1)

            def look_up_half(it, h):
                at = bass.ds(6 * it + h // 2, 1)
                at_blk = bass.ds(NS + 6 * it + h // 2, 1)
                if h > 0:
                    dve.wait_ge(s_look, 12 * it + h)
                if h % 2 == 0:
                    v.scalar_tensor_tensor(pick[:, :], iota[:, 0:NBLK], slots[:, at_blk], tab[:, :], ALU.is_equal, ALU.mult,
                                           accum_out=blk[:, at_blk]).then_inc(s_look, 1)
                else:
                    v.scalar_tensor_tensor(hjunk[:, :], wrow[:, :], blk[:, at_blk], crow[:, :], ALU.is_equal, ALU.mult,
                                           accum_out=hits[:, at]).then_inc(s_look, 1)

            def parity_of_pair(it, p):
                return rope_of_pair(4 * it + p) % 2 if isinstance(it, int) else p % 2

            def keys_of(p):
                return kv[:, 2 * (p % 4):2 * (p % 4) + 2, 0:KVD].rearrange("p a (h d) -> p a h d", d=HD)

            def rotate_keys(it, p, look=None):
                tile0 = 8 * it + 2 * p
                dve.wait_ge(s_kvc, tile0 + 2)
                rotate(keys_of(p), ctab[:, 1, bass.ds(tile0, 2), :], stab[:, 1, bass.ds(tile0, 2), :], rope_of_pair(4 * it + p),
                       parity_of_pair(it, p), look=look)

            def scale_keys(it, p):
                scale_by_rstd(keys_of(p), s_kr, rope_of_pair(4 * it + p), parity_of_pair(it, p))

            def rotate_queries(it, n, parts):
                at = 4 * it + n
                rotate(qs[n % 2][:, :].rearrange("p (g h d) -> p g h d", g=G, d=HD),
                       ctab[:, 0, bass.ds(at, 1), :], stab[:, 0, bass.ds(at, 1), :], rope_of_tile(at),
                       n % 2 if n >= 2 else rope_of_tile(n) % 2, parts)

            def scale_queries(it, n):
                scale_by_rstd(qr[n % 2][:, :].rearrange("p (h g d) -> p g h d", g=G, d=HD), s_qrd, rope_of_tile(4 * it + n),
                              n % 2 if n >= 2 else rope_of_tile(n) % 2)

            rotate_keys(0, 0)
            with dve.Fori(0, 2) as it:
                for p in range(4):
                    rotate_keys(it, p + 1, look=(it, 3 * p))
                    scale_keys(it, p)
            rotate_keys(2, 1)
            scale_keys(2, 0)

            dve.wait_ge(s_look, 2 * WP)
            put(v.tensor_scalar(rtmp[:, 0, :], hits[:, 0:W], 0.0, SKIP, ALU.is_gt, ALU.mult))
            put(v.tensor_scalar(rtmp[:, 1, :], hits[:, 0:W], 0.0, SKIP, ALU.is_equal, ALU.mult))
            settled()
            put(v.tensor_tensor(rd[:, 0, :], rtmp[:, 0, :], blk[:, NS:NS + W], ALU.add))
            put(v.scalar_tensor_tensor(rd[:, 1, :], hits[:, 0:W], -1.0, rtmp[:, 1, :], ALU.add, ALU.add))
            settled()
            for j in range(2):
                for f in range(GB):
                    put(v.tensor_scalar(gspread[:, j, f, :], rd[:, j, :], in_group[:, f:f + 1], None, ALU.mult))
            dve.wait_ge(s_adapt, 16)
            put(v.tensor_copy(cf[:, 2:3], adapt_i[:, :]))
            settled()
            put(v.tensor_scalar(adiag[:, :], ident[:, :], cf[:, 2:3], None, ALU.mult))
            mark["reads"] = done[0]
            rotate_keys(2, 2)
            scale_keys(2, 1)
            tables(0)
            rotate_keys(2, 3)
            scale_keys(2, 2)
            put(v.tensor_copy(keypos[:, :], key_i[:, :]))
            settled()
            dve.wait_ge(s_q[0], 16)
            rotate_queries(0, 0, (0, 1))
            scale_keys(2, 3)
            dve.wait_ge(s_reads, 1)
            put(v.tensor_copy(rd_idx[0:ROWS, :, :].rearrange("p j n -> p (j n)"), ps[7][0:ROWS, 0:2 * NG]))
            mark["second"] = done[0]
            rotate_keys(3, 0)
            scale_queries(0, 0)
            dve.wait_ge(s_q[1], 16)
            rotate_queries(0, 1, (0, 1))
            scale_keys(3, 0)
            dve.wait_ge(s_scal, 16)
            put(v.tensor_scalar(amask[:, :], ps[7][:, 128:128 + B], part[:, 5:6], scal_col[:, :], ALU.is_equal, ALU.mult))
            mark["amask"] = done[0]
            settled()
            rotate_keys(3, 1)
            scale_queries(0, 1)
            rotate_keys(3, 2)
            scale_keys(3, 1)
            rotate_keys(3, 3)
            scale_keys(3, 2)
            for i in range(2):
                dve.wait_ge(s_gold[i], 32)
                for piece in range(4):
                    v.tensor_copy(*reordered_piece(i, 0, piece)).then_inc(s_order[i], 1)
                if i == 0:
                    scale_keys(3, 3)

            def make_pen(n, n0):
                v.tensor_scalar(pen_hi[:, :], keypos[:, :], tok_hi[:, bass.ds(n, 1)], None, ALU.is_gt).then_inc(s_pen1, 1)
                dve.wait_ge(s_pen1, n + 1)
                v.scalar_tensor_tensor(pen[n0 % 2][:, :], keypos[:, :], tok_lo[:, bass.ds(n, 1)], pen_hi[:, :],
                                       ALU.is_le, ALU.add).then_inc(s_pen, 1)

            def slot(it, k):
                b = 16 * it + k
                if k == -8:
                    make_pen(0, 0)
                if 0 <= k < B:
                    dve.wait_ge(s_qk, b + 1)
                    v.tensor_reduce(nmax[:, k % 4, :], ps_s[k % 2][:, 0:HPG * KEYS].rearrange("p (h k) -> p h k", h=HPG),
                                    AX.X, ALU.max, negate=True).then_inc(s_max, 1)
                for kind, n in prep_steps(k) if k < 0 else prep_steps(k - 1) if k > 0 else []:
                    bank, _ = misc((kind, n), it)
                    if kind in ("k0", "k1", "k2", "k3"):
                        await_step(dve, (kind, n), it)
                        o = 4 * int(kind[1])
                        v.tensor_copy(kT[n % 2][:, :, :, o:o + 4].rearrange("p f w o -> p o f w"),
                                      ps_m[bank][:, 0:4 * ROWS].rearrange("p (o f w) -> p o f w", o=4, w=W)).then_inc(s_empty[bank], 1)
                for n in rotated_tiles(k - 2):
                    scale_queries(it, n)
                for n in rotated_tiles(k - 1):
                    rotate_queries(it, n, (1,))
                for n in rotated_tiles(k):
                    dve.wait_ge(s_q[n % 2], 16 * (2 * it + n // 2) + 16)
                    rotate_queries(it, n, (0,))
                if 0 <= k < B - 4 and k % 4 == 3:
                    make_pen(4 * it + k // 4 + 1, k // 4 + 1)
                i, pieces = pieces_in_slot(k, {6: (0, 1), 7: (2,), 0: (3,)})
                for piece in pieces:
                    if piece == 0:
                        await_refill(dve, k, it)
                    v.tensor_copy(*reordered_piece(i, 0, piece)).then_inc(s_order[i], 1)
                for kind, n in fin_step(k):
                    bank, _ = misc((kind, n), it)
                    if kind == "x2":
                        dve.wait_ge(s_x1[n % 4], 16 * (it + n // 4) + 16)
                        await_step(dve, (kind, n), it)
                        v.tensor_tensor(x2s[n % 2][:, :], ps_m[bank][:, 0:T], xin[n % 4][:, :], ALU.add).then_inc(s_empty[bank], 1)
                    if kind == "xa":
                        await_step(dve, (kind, n), it)
                        v.tensor_tensor(xam[n % 2][:, :].rearrange("p (f t) -> p f t", f=TB),
                                        ps_m[bank][:, 0:128].rearrange("p (f t) -> p f t", f=TB),
                                        amask[:, bass.ds(16 * it + 4 * n, TB)].unsqueeze(2).broadcast_to([128, TB, C]),
                                        ALU.mult).then_inc(s_empty[bank], 1)
                if 0 <= k < B:
                    dve.wait_ge(s_exp, b + 1)
                    v.reciprocal(rrec[:, k % 4, :], rsum[:, k % 4, :]).then_inc(s_rec, 1)
                    dve.wait_ge(s_rec, b + 1)
                    if k >= 2:
                        dve.wait_ge(s_pt, b - 1)
                    for h in range(HPG):
                        last = v.tensor_scalar(pn[k % 2][:, h, :], pex[k % 2][:, h, :], rrec[:, k % 4, h:h + 1], None, ALU.mult)
                    last.then_inc(s_pn, 1)

            run_slots(dve, slot)

        @block.gpsimd
        def _(pool):
            made = [0]

            def make(ins):
                made[0] += 1
                ins.then_inc(s_cchain, 1)

            def settled():
                pool.wait_ge(s_cchain, made[0])

            make(pool.memset(zcol[:, :], 0.0))
            make(pool.memset(ident[:, :], 0.0))
            make(pool.iota(iota_i[:, :], pattern=[[1, NW]], base=0, channel_multiplier=0))
            make(pool.iota(part_i[:, :], pattern=[[0, 1]], base=0, channel_multiplier=1))
            settled()
            make(pool.affine_select(out=ident[:, :], in_=ident[:, :], compare_op=ALU.not_equal, fill=1.0, base=0,
                                    pattern=[[-1, 128]], channel_multiplier=1))
            assert made[0] == cmark_iota
            for i, (s_idx, idx, w) in enumerate(((s_cond, cond_i, w0), (s_subj, subj_i, w2))):
                pool.wait_ge(s_idx, 16)
                pool.indirect_dma_start(out=wpick[i][:, :], out_offset=None, in_=w.rearrange("s c d -> s (c d)"),
                                        in_offset=bass.IndirectOffsetOnAxis(ap=idx[:, 0:1], axis=0),
                                        bounds_check=w.shape[0] - 1, oob_is_err=False).then_inc(s_pick[i], 16)
                if i == 0:
                    make(pool.memset(ones[:, :], 1.0))
                    assert made[0] == cmark_ones
                    make(pool.memset(bd[:, :, :], 0.0))
                    make(pool.memset(later_or_same[:, :, :], 1.0))
                    assert made[0] == cmark_bd + 1
            settled()
            make(pool.affine_select(out=later_or_same[:, 0:NS - 1, :], in_=later_or_same[:, 0:NS - 1, :], compare_op=ALU.is_ge,
                                    fill=0.0, base=0, pattern=[[0, NS - 1], [-1, 128]], channel_multiplier=1))
            make(pool.affine_select(out=later_or_same[:, NS - 1:, :], in_=later_or_same[:, NS - 1:, :], compare_op=ALU.is_gt,
                                    fill=0.0, base=0, pattern=[[0, NS], [-1, 128]], channel_multiplier=1))
            assert made[0] == cmark_masks
            make(pool.memset(mask_sel[:, :, :], 0.0))
            make(pool.memset(halfpow[:, :], -0.5))
            for i in range(HALF):
                make(pool.memset(inv[:, i:i + 1], 1.0 / 10000.0 ** (i / HALF)))
            make(pool.iota(key_i[:, :], pattern=[[1, KEYS]], base=0, channel_multiplier=0))
            settled()
            sel_v = mask_sel[:, :, :].rearrange("p f (g t) -> p f g t", g=G)
            make(pool.affine_select(out=sel_v, in_=sel_v, compare_op=ALU.not_equal, fill=NEG, base=0,
                                    pattern=[[-C, TB], [0, G], [-1, C]], channel_multiplier=1))
            assert made[0] == cmark_all

            pool.wait_ge(s_dset, mark["base"])
            pool.wait_ge(s_zero, 2)
            pool.wait_ge(s_zfill, 16)
            pool.wait_ge(s_pickw[0], 16)
            for i in range(2):
                for j, src in enumerate((k_old, v_old)):
                    pool.indirect_dma_start(out=old[i][:, j, :], out_offset=None, in_=src,
                                            in_offset=bass.IndirectOffsetOnAxis(ap=base_idx[:, i:i + 1], axis=0),
                                            bounds_check=POOL_BLOCKS - 1, oob_is_err=False).then_inc(s_bg[2 * i + j], 16)
            pool.wait_ge(s_w3, 32)
            for r in range(2):
                at = wnat[:, 12 + 3 * r, :]
                pool.tensor_tensor(out=at, in0=at, in1=ident[:, :], op=ALU.add).then_inc(s_w3i, 1)
            for i in range(2):
                make(pool.memset(qbd[i][:, :, :, :], 0.0))
            assert made[0] == cmark_qbd
            def past_waits():
                pool.sem_inc(s_passed, 1)

            def rstd(index, i):
                pool.wait_ge(s_ms, index + 1)
                pool.tensor_tensor(out=rms[:, i, 2, :], in0=rms[:, i, 1, :], in1=halfpow[:, :], op=ALU.pow).then_inc(s_rstd, 1)

            def pair(it, p, following):
                tile0, u0, index = 8 * it + 2 * p, 2 * p, 4 * it + p
                for u in (u0, u0 + 1):
                    if not isinstance(it, int) or it > 0:
                        pool.wait_ge(s_scat[u], 16 * it)
                    past_waits()
                    pool.tensor_copy(kv_idx[:, u:u + 1], tok_idx[:, bass.ds(tile0 + (u - u0), 1)]).then_inc(s_tix, 1)
                if following is not None:
                    rstd(following, following % 2 if isinstance(following, int) else (p + 1) % 2)
                pool.wait_ge(s_kr, index + 1)
                if isinstance(it, int) and index == 0:
                    for i in range(2):
                        pool.wait_ge(s_bs[i], 16)
                pool.wait_ge(s_tix, tile0 + 2)
                past_waits()
                for u in (u0, u0 + 1):
                    pool.indirect_dma_start(out=new_d, out_offset=bass.IndirectOffsetOnAxis(ap=kv_idx[:, u:u + 1], axis=0),
                                            in_=kv[:, u, :], in_offset=None,
                                            bounds_check=NW * BLOCK - 1, oob_is_err=False).then_inc(s_scat[u], 16)

            def stage_index(i, j, g2):
                past_waits()
                pool.tensor_copy(g_idx[0:ROWS, 2 * i + j:2 * i + j + 1], rd_idx[0:ROWS, j, bass.ds(g2, 1)]).then_inc(s_gix[j], 1)

            def gather_old(i, g2):
                stage_index(i, 0, g2)
                pool.wait_ge(s_gix[0], g2 + 1)
                past_waits()
                for j, src in enumerate((k_old, v_old)):
                    pool.indirect_dma_start(out=old[i][0:ROWS, j, :], out_offset=None, in_=src,
                                            in_offset=bass.IndirectOffsetOnAxis(ap=g_idx[0:ROWS, 2 * i:2 * i + 1], axis=0),
                                            bounds_check=POOL_BLOCKS - 1, oob_is_err=False).then_inc(s_gold[i], 16)

            def gather_new(i, g2, reordered):
                stage_index(i, 1, g2)
                pool.wait_ge(s_gix[1], g2 + 1)
                pool.wait_ge(s_order[i], reordered)
                past_waits()
                pool.indirect_dma_start(out=new[i][0:ROWS, :, :, :].rearrange("p o k c -> p (o k c)"), out_offset=None, in_=new_blocks,
                                        in_offset=bass.IndirectOffsetOnAxis(ap=g_idx[0:ROWS, 2 * i + 1:2 * i + 2], axis=0),
                                        bounds_check=NW - 1, oob_is_err=False).then_inc(s_gnew[i], 16)

            pool.wait_ge(s_dset, mark["tokens"])
            rstd(0, 0)
            for p in range(4):
                pair(0, p, p + 1)
            with pool.Fori(1, NT // 8 - 1) as it:
                for p in range(4):
                    pair(it, p, 4 * it + p + 1)
            rstd(rope_of_pair(12), rope_of_pair(12) % 2)
            pool.wait_ge(s_dset, mark["second"])
            for i in range(2):
                gather_old(i, i)
            pair(NT // 8 - 1, 0, rope_of_tile(1))
            rstd(rope_of_pair(13), rope_of_pair(13) % 2)
            for p in range(1, 4):
                pair(NT // 8 - 1, p, rope_of_pair(12 + p + 1) if p < 3 else None)
            pool.wait_ge(s_order[0], 8)
            gather_old(0, 2)
            for u in range(8):
                pool.wait_ge(s_scat[u], 16 * (NT // 8))
            for i in range(2):
                gather_new(i, i, 8)


            def slot(it, k):
                b = 16 * it + k
                for n in rotated_tiles(k):
                    rstd(rope_of_tile(4 * it + n), n % 2)
                kk = k + EARLY
                i, j, grp = (kk // 8) % 2, kk % 8, kk // 8 + 2
                if j == 3 and k >= 0 and grp + 1 < NG:
                    gather_old(1 - i, 2 * it + grp + 1)
                if j == 4 and k > 0 and grp < NG:
                    fills = it + kk // 16 + 1
                    pool.wait_ge(s_gnew[i], 16 * fills)
                    gather_new(i, 2 * it + grp, 8 * fills + 8)

            run_slots(pool, slot)

        @block.sync
        def _(sp):
            column = "(b u) -> b u"
            sp.dma_start(kvlen_i[:, :], kvlen.rearrange(column, u=1)).then_inc(s_len, 16)
            sp.dma_start(cond_i[:, :], cond.rearrange(column, u=1)).then_inc(s_cond, 16)
            sp.dma_start(table_i[:, :], table).then_inc(s_tab, 16)
            sp.dma_start(subj_i[:, :], subj.rearrange(column, u=1)).then_inc(s_subj, 16)
            for u in range(4):
                sp.dma_start(xin[u][:, :], x_t[u, :, :]).then_inc(s_xin[u], 16)
            sp.wait_ge(s_zero, 1)
            sp.dma_start(new_rows[1], old[0][:, :, :].rearrange("p k c -> p (k c)")).then_inc(s_zfill, 16)
            sp.wait_ge(s_cchain, cmark_bd)
            for i, wd in enumerate((w0_d, w2_d)):
                sp.wait_ge(s_dset, mark[f"w{i}"])
                sp.dma_start(wd, wpick[i][:, :]).then_inc(s_pickw[i], 16)
                if i == 0:
                    sp.wait_ge(s_pickw[0], 16)
                    for f in range(TB):
                        sp.dma_start(bd[C * f:C * f + C, :, C * f:C * f + C],
                                     w0_d.rearrange("(n f) (c d) -> f c n d", f=TB, d=C)[f]).then_inc(s_bd[0], 16)

            def past_waits():
                sp.sem_inc(s_sp_passed, 1)

            def load_and_spill(n, u, load):
                if load:
                    sp.wait_ge(s_l0, n + 1)
                    sp.dma_start(xin[u][:, :], x_t[n + 4, :, :]).then_inc(s_xin[u], 16)
                sp.wait_ge(s_x1c, n + 1)
                sp.dma_start(x1_d[n, :, :], x1s[u][:, :]).then_inc(s_spill[u], 16)
                sp.wait_ge(s_qc, n + 1)
                past_waits()
                sp.dma_start(q_d[n, :, :], q1s[u][:, :]).then_inc(s_spill[u], 16)

            with sp.Fori(0, 3) as it:
                for u in range(4):
                    load_and_spill(4 * it + u, u, True)
            for i in range(2):
                sp.wait_ge(s_spill[i], 64)
                sp.dma_start(qs[i][:, :], q_d[i, :, :]).then_inc(s_q[i], 16)
            with sp.Fori(3, NT // 4 - 1) as it:
                for u in range(4):
                    load_and_spill(4 * it + u, u, True)
            for u in range(4):
                load_and_spill(NT - 4 + u, u, False)
            for u in range(2):
                sp.sem_inc(s_out[u], 16)
            sp.wait_ge(s_pickw[1], 16)
            for u in range(4):
                sp.wait_ge(s_spill[u], 32 * (NT // 4))
            for i in range(2):
                sp.wait_ge(s_rope, ROPE * rope_of_tile(i) + ROPE)
                sp.dma_start(qs[i][:, :], q_d[i + 2, :, :]).then_inc(s_q[i], 16)
            for u in range(4):
                sp.dma_start(xin[u][:, :], x1_d[u, :, :]).then_inc(s_x1[u], 16)
            for f in range(TB):
                sp.dma_start(bd[C * f:C * f + C, :, C * f:C * f + C],
                             w2_d.rearrange("(n f) (c d) -> f c n d", f=TB, d=C)[f]).then_inc(s_bd[1], 16)

            def slot(it, k):
                grp = k // 8 + 1
                for n in rotated_tiles(k - 2):
                    if n + 2 < NT:
                        sp.wait_ge(s_rope, ROPE * rope_of_tile(4 * it + n) + ROPE)
                        past_waits()
                        sp.dma_start(qs[n % 2][:, :], q_d[4 * it + n + 2, :, :]).then_inc(s_q[n % 2], 16)
                if grp < NG:
                    i, fills = grp % 2, it + grp // 2
                    if k % 8 == 0:
                        sp.wait_ge(s_gnew[i], 16 * fills + 16)
                        past_waits()
                        sp.dma_start(v_d[2 * it + grp, :, :].rearrange("(r o) c -> r o c", o=BLOCK), new[i][0:ROWS, :, 1, :]).then_inc(s_vst[i], 16)
                    if k % 8 == 3:
                        sp.wait_ge(s_vst[i], 16 * fills + 16)
                        if grp >= 2:
                            past_waits()
                            sp.wait_ge(s_pv, 16 * it + GB * (grp - 1))
                        past_waits()
                        sp.dma_start(vg[i][:, :, :, :].rearrange("p f c d -> p (f c) d"),
                                     v_d[2 * it + grp, :, :].rearrange("(a p) d -> p a d", p=HK)).then_inc(s_vin[i], 16)
                for kind, n in fin_step(k):
                    if kind == "x2" and n + 4 < NT:
                        await_copied(sp, (kind, n), it)
                        sp.dma_start(xin[n % 4][:, :], x1_d[4 * it + n + 4, :, :]).then_inc(s_x1[n % 4], 16)
                    if kind == "x4":
                        await_copied(sp, (kind, n), it)
                        sp.dma_start(out_t[4 * it + n, :, :], x4s[n % 2][:, :]).then_inc(s_out[n % 2], 16)

            run_slots(sp, slot)
            for u in range(2):
                sp.wait_ge(s_out[u], 16 * (NT // 2) + 16)

        @block.scalar
        def _(act):
            a = nc.scalar
            halves = "o (c d) -> o c d"
            act.wait_ge(s_cchain, 1)
            for i in range(2):
                a.activation(old[i][:, :, :].rearrange("p k c -> p (k c)"), zcol[:, :].broadcast_to([128, 2 * G * BLOCK * HD]), ACT.Copy).then_inc(s_zero, 1)
            act.dma_start(wnat[:, 0:2, :], wk.rearrange(halves, c=2)).then_inc(s_wk, 16)
            act.dma_start(wnat[:, 2:4, :], wv.rearrange(halves, c=2)).then_inc(s_wk, 16)
            act.dma_start(adapt_i[:, :], adapt.rearrange("(b u) -> b u", u=1)).then_inc(s_adapt, 16)
            act.dma_start(gain[:, 0, :], qscale.partition_broadcast(128)).then_inc(s_gain, 16)
            act.dma_start(gain[:, 1, :], kscale.partition_broadcast(128)).then_inc(s_gain, 16)
            act.dma_start(scal_col[:, :], s3.rearrange("(a u) -> a u", u=1).broadcast_to([NA, RANK])).then_inc(s_scal, 16)
            for at, w, s_w in ((4, wq, s_wq), (8, wo, s_wo), (12, w3, s_w3)):
                for r in range(2):
                    rows = w[128 * r:128 * r + 128, :]
                    if w is wo:
                        for h in range(HPG):
                            act.dma_start(wnat[:, at + 2 * r + h, :].rearrange("p (g d) -> p g d", g=G),
                                          rows.rearrange("o (g h d) -> o g h d", g=G, h=HPG)[:, :, h, :]).then_inc(s_w, 16)
                    else:
                        act.dma_start(wnat[:, at + 2 * r:at + 2 * r + 2, :], rows.rearrange(halves, c=2)).then_inc(s_w, 16)
            act.dma_start(wnat[:, 16:18, :], a3.rearrange("a r (c d) -> (a r) c d", c=2)).then_inc(s_ab, 16)
            for c in range(2):
                act.dma_start(wnat[:, 18 + c, :].rearrange("p (a r) -> p a r", a=NA),
                              b3[:, 128 * c:128 * c + 128, :].rearrange("a o r -> o a r")).then_inc(s_ab, 16)
            def copy_weights(i, dst, src):
                act.wait_ge(s_wt, i + 1)
                a.activation(dst[:, :, :].rearrange("p c o -> p (c o)"), src[:, :], ACT.Copy).then_inc(s_wtc, 1)

            for i, dst in enumerate((wkvT, wqT, woT)):
                copy_weights(i, dst, ps[i])
            act.wait_ge(s_dset, mark["angles"])
            a.activation(trig[:, 1, :, :], trig[:, 0, :, :], ACT.Sin).then_inc(s_trig, 1)
            act.wait_ge(s_trig, 1)
            a.activation(trig[:, 0, :, :], trig[:, 0, :, :], ACT.Sin, scale=0.5).then_inc(s_trig, 1)
            act.wait_ge(s_trig, 2)
            a.activation(trig[:, 0, :, :], trig[:, 0, :, :], ACT.Square).then_inc(s_trig, 1)
            act.wait_ge(s_trig, 3)
            a.activation(trig[:, 0, :, :], trig[:, 0, :, :], ACT.Copy, scale=-2.0, bias=1.0).then_inc(s_trig, 1)

            def permute_base(i, j):
                act.wait_ge(s_bg[2 * i + j], 16)
                a.activation(new[i][:, :, j, :].rearrange("p o (g d) -> p g o d", g=G),
                             old[i][:, j, :].rearrange("p (g o d) -> p g o d", g=G, o=BLOCK), ACT.Copy).then_inc(s_perm, 1)
                if j == 1:
                    act.wait_ge(s_perm, 2 * i + 2)
                    act.dma_start(new_rows[(0, NS - 1)[i]], new[i][:, :, :, :].rearrange("p o k c -> p (o k c)")).then_inc(s_bs[i], 16)

            def copy_x1T(n, u):
                act.wait_ge(s_l0, n + 1)
                if not isinstance(n, int) or n >= 2:
                    act.wait_ge(s_kvp, n - 1)
                a.activation(xT[u % 2][:, :, :].rearrange("p c t -> p (c t)"), ps[u % 2][:, 0:T], ACT.Copy).then_inc(s_xtc, 1)

            def copy_kv_x1(n, u, turn):
                if turn is not None:
                    act.wait_ge(s_scat[u], 16 * turn)
                act.wait_ge(s_kvp, n + 1)
                a.activation(kv[:, u, :], ps[4 + u % 2][:, 0:2 * KVD], ACT.Copy).then_inc(s_kvc, 1)
                if turn is not None or u >= 4:
                    act.wait_ge(s_spill[u % 4], 32 * (2 * (0 if turn is None else turn) + u // 4))
                a.activation(x1s[u % 4][:, :], ps[2 + u % 2][:, 0:T], ACT.Copy).then_inc(s_x1c, 1)
                a.activation(q1s[u % 4][:, :], ps[4 + u % 2][:, 2 * KVD:2 * KVD + T], ACT.Copy).then_inc(s_qc, 1)

            def eight(n0, turn, last):
                for u in range(8):
                    if not (last and u == 7):
                        copy_x1T(n0 + u + 1, u + 1)
                    copy_kv_x1(n0 + u, u, turn)
                    if turn is None and u in BASE_AFTER:
                        permute_base(*BASE_AFTER[u])
                    if turn is None and u == 6:
                        copy_weights(3, w3T, ps[6])
                        copy_weights(4, abT, ps[7])

            BASE_AFTER = {0: (0, 1), 1: (1, 0), 2: (1, 1)}
            copy_x1T(0, 0)
            permute_base(0, 0)
            eight(0, None, False)
            with act.Fori(1, NT // 8 - 1) as it:
                eight(8 * it, it, False)
            eight(NT - 8, NT // 8 - 1, True)
            a.activation(exp_of_zero[:, :], zcol[:, :], ACT.Exp)
            for i in range(2):
                act.wait_ge(s_gold[i], 32)
                for piece in range(4):
                    a.activation(*reordered_piece(i, 1, piece), ACT.Copy).then_inc(s_order[i], 1)

            def slot(it, k):
                b = 16 * it + k
                if k % 4 == 2 and 0 <= (k - 6) // 4 < NT:
                    n = (k - 6) // 4
                    act.wait_ge(s_pv, 16 * it + 4 * n + 4)
                    a.activation(oT[n % 2][:, :, :, :].rearrange("p h f t -> p f h t"),
                                 ps_o[:, 0:TB * HPG * C].rearrange("p (f h t) -> p f h t", f=TB, h=HPG), ACT.Copy).then_inc(s_oc, 1)
                for kind, n in fin_step(k):
                    bank, _ = misc((kind, n), it)
                    if kind == "x3":
                        await_step(act, (kind, n), it)
                        a.activation(x3T[n % 2][:, :, :].rearrange("p c t -> p (c t)"), ps_m[bank][:, 0:T], ACT.Copy).then_inc(s_empty[bank], 1)
                    if kind == "x4":
                        if k >= 8:
                            act.wait_ge(s_out[n % 2], 16 * (2 * it + n // 2) + 16)
                        await_step(act, (kind, n), it)
                        a.activation(x4s[n % 2][:, :], ps_m[bank][:, 0:T], ACT.Copy).then_inc(s_empty[bank], 1)
                if 0 <= k < B:
                    act.wait_ge(s_max, b + 1)
                    if k >= 2:
                        act.wait_ge(s_pn, b - 1)
                    for h in range(HPG):
                        last = a.activation(pex[k % 2][:, h, :], ps_s[k % 2][:, h * KEYS:(h + 1) * KEYS], ACT.Exp,
                                            bias=nmax[:, k % 4, h:h + 1], accum_out=rsum[:, k % 4, h:h + 1])
                    last.then_inc(s_exp, 1)
                i, pieces = pieces_in_slot(k, {6: (0,), 7: (1,), 0: (2, 3)})
                for piece in pieces:
                    if piece == 0:
                        await_refill(act, k, it)
                    a.activation(*reordered_piece(i, 1, piece), ACT.Copy).then_inc(s_order[i], 1)
                if 0 <= k - 1 < B:
                    if k >= 3:
                        act.wait_ge(s_pv, b - 2)
                    act.wait_ge(s_pt, b)
                    a.activation(pT[(k - 1) % 2][:, :, :, :].rearrange("p c h t -> p (c h t)"), ps_p[(k - 1) % 2][0:HK, :],
                                 ACT.Copy).then_inc(s_ptc, 1)
                for kind, n in prep_steps(k):
                    bank, _ = misc((kind, n), it)
                    m = ps_m[bank]
                    if kind == "qT":
                        await_step(act, (kind, n), it)
                        for g in range(G):
                            rows = slice(HD * g, HD * g + HD)
                            last = a.activation(
                                qbd[n // 2 % 2][rows, TB * (n % 2):TB * (n % 2) + TB, :, C * g:C * g + C],
                                m[rows, 0:HPG * 128].rearrange("p (h f t) -> p f h t", h=HPG, f=TB), ACT.Copy, scale=SCALE)
                        last.then_inc(s_empty[bank], 1)
            run_slots(act, slot)

        @block.tensor
        def _(pe):
            mm, turn_over = nc.tensor.matmul, nc.tensor.transpose

            def turn_weights(i, bank):
                o = bank[:, :].rearrange("p (c o) -> p c o", c=2)
                for c in range(2):
                    for r in range(2):
                        dst = o[:, c, 128 * r:128 * r + 128]
                        if i == 0:
                            src = wnat[:, 2 * r + c, :]
                        elif i == 4:
                            src = wnat[:, 16 + 2 * c + r, :]
                        else:
                            src = wnat[:, 4 * i + 2 * r + c, :]
                        last = turn_over(dst, src, ident[:, :])
                last.then_inc(s_wt, 1)

            def row_in_every_partition(s_done):
                mm(ps[6][:, 0:NW], ones[:, :], diag[:, :, :].rearrange("p s b -> p (s b)"), start=True, stop=True).then_inc(s_done, 1)

            def relay(rows, bank):
                for at, i in enumerate(rows):
                    last = mm(bank[:, NT * at:NT * at + NT], spread[:, i, :], of_tile[:, :], start=True, stop=True)
                return last

            pe.wait_ge(s_cchain, cmark_ones)
            pe.wait_ge(s_dset, mark["diag"])
            row_in_every_partition(s_wrow)
            pe.wait_ge(s_dset, mark["positions"])
            relay((1, 2), ps[5]).then_inc(s_places, 1)
            pe.wait_ge(s_wk, 32)
            turn_weights(0, ps[0])
            pe.wait_ge(s_dset, mark["same"])
            for s in range(NS):
                for t in range(NS):
                    last = mm(ps[7][:, s * (BLOCK + 1):(s + 1) * (BLOCK + 1)], same[:, t, 128 * s:128 * s + 128], valid[:, t, :],
                              start=(t == 0), stop=(t == NS - 1))
            last.then_inc(s_later, 1)
            pe.wait_ge(s_wq, 32)
            turn_weights(1, ps[1])
            pe.wait_ge(s_wo, 64)
            turn_weights(2, ps[2])
            pe.wait_ge(s_dset, mark["owner"])
            row_in_every_partition(s_crow)

            pe.wait_ge(s_bd[0], 16 * TB)
            pe.wait_ge(s_wtc, 3)
            pe.wait_ge(s_dset, mark["placed"])

            def first_stage(n, u, turn):
                pe.wait_ge(s_xin[u % 4], 16 * (2 * turn + u // 4) + 16)
                if not isinstance(n, int) or n >= 2:
                    pe.wait_ge(s_xtc, n - 1)
                for c in range(2):
                    last = mm(ps[u % 2][:, 128 * c:128 * c + 128], xin[u % 4][:, 128 * c:128 * c + 128],
                              bd[:, bass.ds(n, 1), :].rearrange("p a b -> p (a b)"), start=True, stop=True)
                last.then_inc(s_l0, 1)

            def project(n, u):
                pe.wait_ge(s_xtc, n + 1)
                if not isinstance(n, int) or n >= 2:
                    pe.wait_ge(s_kvc, n - 1)
                    pe.wait_ge(s_x1c, n - 1)
                    pe.wait_ge(s_qc, n - 1)
                for c in range(2):
                    last = turn_over(ps[2 + u % 2][:, 128 * c:128 * c + 128], xT[u % 2][:, c, :], ident[:, :])
                last.then_inc(s_tr1, 1)
                for c in range(2):
                    mm(ps[4 + u % 2][:, 0:2 * KVD], xT[u % 2][:, c, :], wkvT[:, c, :], start=(c == 0), stop=(c == 1))
                for c in range(2):
                    last = mm(ps[4 + u % 2][:, 2 * KVD:2 * KVD + T], xT[u % 2][:, c, :], wqT[:, c, :], start=(c == 0), stop=(c == 1))
                last.then_inc(s_kvp, 1)

            def eight(n0, turn, last):
                for u in range(8):
                    if not (last and u == 7):
                        first_stage(n0 + u + 1, (u + 1) % 8, turn + (u + 1) // 8)
                    project(n0 + u, u)
                    if isinstance(n0, int) and n0 == 0 and u == RELAY_AFTER:
                        pe.wait_ge(s_dset, mark["spread"])
                        relay((0,), ps[6]).then_inc(s_relay, 1)
                    if isinstance(n0, int) and n0 == 0 and u == 5:
                        pe.wait_ge(s_w3i, 2)
                        pe.wait_ge(s_dset, mark["tokens"])
                        turn_weights(3, ps[6])
                        pe.wait_ge(s_ab, 48)
                        turn_weights(4, ps[7])

            RELAY_AFTER = 1
            first_stage(0, 0, 0)
            eight(0, 0, False)
            with pe.Fori(1, NT // 8 - 1) as it:
                eight(8 * it, it, False)
            pe.wait_ge(s_wtc, 5)
            pe.wait_ge(s_dset, mark["reads"])
            for j in range(2):
                mm(ps[7][0:ROWS, NG * j:NG * j + NG], gspread[:, j, :, :].rearrange("p f w -> p (f w)"), of_group[:, :],
                   start=True, stop=True)
            mm(ps[7][:, 128:128 + B], ones[:, :], adiag[:, :], start=True, stop=True).then_inc(s_reads, 1)
            eight(NT - 8, NT // 8 - 1, True)

            pe.wait_ge(s_xtc, NT)
            pe.wait_ge(s_kvc, NT)
            pe.wait_ge(s_x1c, NT)
            pe.wait_ge(s_qc, NT)
            pe.wait_ge(s_dset, mark["amask"])
            pe.wait_ge(s_cchain, cmark_qbd)

            def misc_step(it, kind, n):
                bank, _ = misc((kind, n), it)
                m = ps_m[bank]
                if kind == "qT":
                    pe.wait_ge(s_qrd, 4 * it + n + 1)
                    await_bank(pe, (kind, n), it)
                    for h in range(HPG):
                        last = turn_over(m[:, 128 * h:128 * h + 128],
                                         qr[n % 2][:, 128 * h:128 * h + 128], ident[:, :])
                if kind[0] == "k":
                    i, o0 = n % 2, 4 * int(kind[1])
                    if kind == "k0":
                        pe.wait_ge(s_gnew[i], 16 * (it + n // 2) + 16)
                    await_bank(pe, (kind, n), it)
                    for o in range(4):
                        last = turn_over(m[:, ROWS * o:ROWS * o + ROWS], new[i][0:ROWS, o0 + o, 0, :], ident[0:ROWS, 0:ROWS])
                if kind == "x2":
                    pe.wait_ge(s_oc, 4 * it + n + 1)
                    await_bank(pe, (kind, n), it)
                    for h in range(HPG):
                        last = mm(m[:, 0:T], oT[n % 2][:, h, :, :].rearrange("p f t -> p (f t)"), woT[:, h, :],
                                  start=(h == 0), stop=(h == HPG - 1))
                if kind == "x3":
                    if n == 0:
                        pe.wait_ge(s_bd[1], 16 * TB)
                    await_copied(pe, ("x2", n), it)
                    await_bank(pe, (kind, n), it)
                    for c in range(2):
                        last = mm(m[:, 128 * c:128 * c + 128], x2s[n % 2][:, 128 * c:128 * c + 128],
                                  bd[:, bass.ds(4 * it + n, 1), :].rearrange("p a b -> p (a b)"), start=True, stop=True)
                if kind == "xa":
                    await_copied(pe, ("x3", n), it)
                    await_bank(pe, (kind, n), it)
                    for c in range(2):
                        last = mm(m[:, 0:128], abT[:, 0, 128 * c:128 * c + 128], x3T[n % 2][:, c, :], start=(c == 0), stop=(c == 1))
                if kind == "x4":
                    await_copied(pe, ("xa", n), it)
                    await_bank(pe, (kind, n), it)
                    for c in range(2):
                        mm(m[:, 0:T], x3T[n % 2][:, c, :], w3T[:, c, :], start=(c == 0), stop=False)
                    last = mm(m[:, 0:T], xam[n % 2][:, :], abT[:, 1, :], start=False, stop=True)
                last.then_inc(s_full[bank], 1)

            def slot(it, k):
                b = 16 * it + k
                if 0 <= k < B:
                    grp, f, n = k // 8, k % 8, k // 4
                    if k % 4 == 0:
                        await_copied(pe, ("qT", n), it)
                        pe.wait_ge(s_pen, 4 * it + n + 1)
                    if f == 0:
                        await_keys(pe, grp, it)
                    if k >= 2:
                        pe.wait_ge(s_exp, b - 1)
                    for h in range(HPG):
                        dst = ps_s[k % 2][:, h * KEYS:(h + 1) * KEYS]
                        mm(dst, qbd[grp % 2][:, f, h, :], kT[grp % 2][:, f, :, :].rearrange("p w o -> p (w o)"), start=True, stop=False)
                        last = mm(dst, mask_sel[:, k % 4, :], pen[n % 2][:, :], start=False, stop=True)
                    last.then_inc(s_qk, 1)
                for kind, n in fin_step(k):
                    misc_step(it, kind, n)
                if 0 <= k - 1 < B:
                    pe.wait_ge(s_pn, b)
                    if k >= 3:
                        pe.wait_ge(s_ptc, b - 2)
                    for c in range(2):
                        for h in range(HPG):
                            last = turn_over(ps_p[(k - 1) % 2][0:HK, (HPG * c + h) * 128:(HPG * c + h + 1) * 128],
                                             pn[(k - 1) % 2][:, h, HK * c:HK * c + HK], ident[:, :])
                    last.then_inc(s_pt, 1)
                for kind, n in prep_steps(k):
                    misc_step(it, kind, n)
                if 0 <= k - 2 < B:
                    kb = k - 2
                    pe.wait_ge(s_ptc, b - 1)
                    if kb % GB == 0:
                        pe.wait_ge(s_vin[kb // GB % 2], 16 * (it + kb // 16) + 16)
                    if kb % 4 == 0 and kb >= 4:
                        pe.wait_ge(s_oc, 4 * it + kb // 4)
                    col = HPG * C * (kb % 4)
                    for c in range(2):
                        for g in range(G):
                            last = mm(ps_o[HD * g:HD * g + HD, col:col + HPG * C], vg[kb // GB % 2][:, kb % GB, c, HD * g:HD * g + HD],
                                      pT[kb % 2][:, c, :, C * g:C * g + C], start=(c == 0), stop=(c == 1))
                    last.then_inc(s_pv, 1)

            run_slots(pe, slot)


_INS = ["x", "itok_B_1_198", "itok_Bx257_0_4111", "itok_B_37_3939", "itok_B_0_7", "itok_B_0_6", "L0_cond_weights", "L1_cond_Wq",
        "L1_cond_Wk", "L1_cond_Wv", "L1_cond_Wo", "L1_cond_q_norm_scale", "L1_cond_k_norm_scale", "L1_cond_k_blocks",
        "L1_cond_v_blocks", "L2_cond_weights", "L3_cond_W", "L3_cond_A", "L3_cond_Bm", "L3_cond_scalings"]
_OUTS = [((128, 32, 256), "float32")]


def kernel(**inputs):
    import numpy as _np
    import concourse.bacc as _bacc
    from concourse import mybir as _mybir
    from concourse.bass_utils import run_bass_kernel_spmd as _run

    nc = _bacc.Bacc("TRN2", target_bir_lowering=False, num_devices=1)
    arrays, args = {}, []
    for name in _INS:
        a = _np.ascontiguousarray(inputs[name])
        arrays[f"in_{name}_dram"] = a
        args.append(nc.dram_tensor(f"in_{name}_dram", a.shape, _mybir.dt.from_np(a.dtype), kind="ExternalInput").ap())
    for i, (shape, dtype) in enumerate(_OUTS):
        dt = _mybir.dt.from_np(_np.dtype(dtype))
        args.append(nc.dram_tensor(f"out_{i}_dram", shape, dt, kind="ExternalOutput").ap())
    cond_resid_kernel(nc, *args)
    r = _run(nc, [arrays], core_ids=[0])
    return r.results[0]["out_0_dram"]
```
